# Optimizing a Trainium2 kernel written in Bass

```python
import numpy as np
import jax
import jax.numpy as jnp

def _softmax(x, axis=-1):
    return jax.nn.softmax(x, axis=axis)

def _gelu(x):
    return jax.nn.gelu(x, approximate=True)

def _silu(x):
    return jax.nn.silu(x)

def _sigmoid(x):
    return jax.nn.sigmoid(x)

def _layernorm(x, axis=-1, eps=1e-05):
    m = jnp.mean(x, axis=axis, keepdims=True)
    v = jnp.var(x, axis=axis, keepdims=True)
    return (x - m) / jnp.sqrt(v + eps)

def _scatter_add(tgt, idx, src, axis=0):
    return tgt.at[idx].add(src)

def _segment_sum(src, seg, n):
    return jax.ops.segment_sum(src, seg, n)
kernel_name = 'mk_decoder_preln_d2_seqx_r8_addd6c'

def setup_inputs(seed: int=0):
    np.random.seed(seed)
    _w = jnp.asarray

    def _rec_inputs():
        import jax
        import jax.numpy as jnp
        _rk = jax.random.key(seed)
        x = -0.0002928 + 1 * jax.random.normal(jax.random.fold_in(_rk, 1), (16, 56, 128), jnp.float32)
        _lenS = 56 - jax.random.randint(jax.random.fold_in(_rk, 7), (16,), 0, max(1, 56 // 4) + 1, jnp.int32)
        _lenS2 = 1500 - jax.random.randint(jax.random.fold_in(_rk, 8), (16,), 0, max(1, 1500 // 4) + 1, jnp.int32)
        _ctx_1024P = jax.random.normal(jax.random.fold_in(_rk, 11), (16, 16, 128), jnp.float32)
        _ctx_1024c = jax.random.dirichlet(jax.random.fold_in(_rk, 511), 0.3 * jnp.ones((16,), jnp.float32), (16, 1500))
        _ctx_1024t = jnp.einsum('bsk,bkd->bsd', _ctx_1024c, _ctx_1024P)
        _ctx_1024t = _ctx_1024t * jax.lax.rsqrt(jnp.mean(jnp.square(_ctx_1024t)) + 1e-12) * 0.953939
        ctx_1024 = -1.39393e-06 + 0.999914 * (_ctx_1024t + 0.3 * jax.random.normal(jax.random.fold_in(_rk, 611), (16, 1500, 128), jnp.float32))
        fside_SxS2_0 = 0.000376506 + 0.999991 * jax.random.normal(jax.random.fold_in(_rk, 12), (56, 1500), jnp.float32)
        return (x, ctx_1024, fside_SxS2_0)
    x, ctx_1024, fside_SxS2_0 = _rec_inputs()

    def _L0_attn_setup():
        import jax, jax.numpy as jnp
        import numpy as np
        import math
        N_HEADS = 16

        def _rope_tables(seq_len, head_dim):
            pos = jnp.arange(seq_len, dtype=jnp.float32)
            freqs = jnp.exp(jnp.arange(0, head_dim, 2, dtype=jnp.float32) * (-math.log(10000.0) / head_dim))
            angles = pos[:, None] * freqs[None, :]
            cos_emb = jnp.zeros((seq_len, head_dim), jnp.float32).at[:, 0::2].set(jnp.cos(angles))
            sin_emb = jnp.zeros((seq_len, head_dim), jnp.float32).at[:, 1::2].set(jnp.sin(angles))
            return (cos_emb, sin_emb)
        key = jax.random.key(seed)
        ks = jax.random.split(key, 5)
        B, S, D = (2, 256, 128)
        scale = 1.0 / math.sqrt(D)
        return {'x': jax.random.normal(ks[0], (B, S, D), jnp.float32), 'Wq': jax.random.normal(ks[1], (D, D), jnp.float32) * scale, 'Wk': jax.random.normal(ks[2], (D, D), jnp.float32) * scale, 'Wv': jax.random.normal(ks[3], (D, D), jnp.float32) * scale, 'Wo': jax.random.normal(ks[4], (D, D), jnp.float32) * scale}
    _L0_attn_all = _L0_attn_setup()
    _L0_attn_in = {k: v for k, v in _L0_attn_all.items() if k in ('Wq', 'Wk', 'Wv', 'Wo')}
    del _L0_attn_all

    def _L0_xattn_setup():
        import jax, jax.numpy as jnp
        import numpy as np
        D_MODEL, D_HEAD, N_HEAD = (128, 64, 16)
        B, T1, T2 = (2, 256, 256)
        key = jax.random.key(seed)
        ks = jax.random.split(key, 8)
        s = 1.0 / np.sqrt(D_MODEL)
        return {'x': jax.random.normal(ks[0], (B, T1, D_MODEL), dtype=jnp.float32), 'context': jax.random.normal(ks[1], (B, T2, D_MODEL), dtype=jnp.float32), 'bias': jax.random.normal(ks[2], (T1, T2), dtype=jnp.float32), 'W_q': jax.random.normal(ks[3], (D_MODEL, N_HEAD * D_HEAD), dtype=jnp.float32) * s, 'W_k': jax.random.normal(ks[4], (D_MODEL, N_HEAD * D_HEAD), dtype=jnp.float32) * s, 'W_v': jax.random.normal(ks[5], (D_MODEL, N_HEAD * D_HEAD), dtype=jnp.float32) * s, 'W_out': jax.random.normal(ks[6], (N_HEAD * D_HEAD, D_MODEL), dtype=jnp.float32) * s, 'b_out': jnp.zeros((D_MODEL,), dtype=jnp.float32)}
    _L0_xattn_all = _L0_xattn_setup()
    _L0_xattn_in = {k: v for k, v in _L0_xattn_all.items() if k in ('W_q', 'W_k', 'W_v', 'W_out', 'b_out')}
    del _L0_xattn_all

    def _L0_ffn_setup():
        import jax, jax.numpy as jnp
        import numpy as np
        NUM_EXPERTS = 8
        EXPERT_CAPACITY = 2.0
        key = jax.random.key(seed)
        k1, k2, k3, k4 = jax.random.split(key, 4)
        B, T, C, H, E = (4, 512, 128, 512, NUM_EXPERTS)
        x = jax.random.normal(k1, (B, T, C), jnp.float32)
        gate_w = jax.random.normal(k2, (C, E), jnp.float32) * 0.02
        w1 = jax.random.normal(k3, (E, C, H), jnp.float32) * 0.02
        w2 = jax.random.normal(k4, (E, H, C), jnp.float32) * 0.02
        return {'x': x, 'gate_w': gate_w, 'w1': w1, 'w2': w2}
    _L0_ffn_all = _L0_ffn_setup()
    _L0_ffn_in = {k: v for k, v in _L0_ffn_all.items() if k in ('gate_w', 'w1', 'w2')}
    del _L0_ffn_all

    def _L1_attn_setup():
        import jax, jax.numpy as jnp
        import numpy as np
        D_MODEL = 128
        NUM_HEADS = 16
        HEAD_DIM = D_MODEL // NUM_HEADS
        BATCH = 4
        SEQ = 256

        def circulant(x, c, b):
            d = c.shape[0]
            y = jnp.fft.irfft(jnp.fft.rfft(x, axis=-1) * jnp.fft.rfft(c), n=d, axis=-1)
            return y + b
        key = jax.random.key(seed)
        ks = jax.random.split(key, 9)
        scale = 1.0 / np.sqrt(D_MODEL)
        inp = {'x': jax.random.normal(ks[0], (BATCH, SEQ, D_MODEL), dtype=jnp.float32), 'wq_c': jax.random.normal(ks[1], (D_MODEL,), dtype=jnp.float32) * scale, 'wq_b': jnp.zeros((D_MODEL,), dtype=jnp.float32), 'wk_c': jax.random.normal(ks[2], (D_MODEL,), dtype=jnp.float32) * scale, 'wk_b': jnp.zeros((D_MODEL,), dtype=jnp.float32), 'wv_c': jax.random.normal(ks[3], (D_MODEL,), dtype=jnp.float32) * scale, 'wv_b': jnp.zeros((D_MODEL,), dtype=jnp.float32), 'wo_c': jax.random.normal(ks[4], (D_MODEL,), dtype=jnp.float32) * scale, 'wo_b': jnp.zeros((D_MODEL,), dtype=jnp.float32)}
        return inp
    _L1_attn_all = _L1_attn_setup()
    _L1_attn_in = {k: v for k, v in _L1_attn_all.items() if k in ('wq_c', 'wq_b', 'wk_c', 'wk_b', 'wv_c', 'wv_b', 'wo_c', 'wo_b')}
    del _L1_attn_all

    def _L1_xattn_setup():
        import jax, jax.numpy as jnp
        import numpy as np
        D_MODEL = 128
        N_HEADS = 16
        D_K = D_MODEL // N_HEADS

        def _split_heads(x, bs):
            return x.reshape(bs, -1, N_HEADS, D_K).transpose(0, 2, 1, 3)
        key = jax.random.key(seed)
        ks = jax.random.split(key, 11)
        bs, seq = (2, 256)
        s = 1.0 / np.sqrt(D_MODEL)
        return {'q': jax.random.normal(ks[0], (bs, seq, D_MODEL), jnp.float32), 'k': jax.random.normal(ks[1], (bs, seq, D_MODEL), jnp.float32), 'v': jax.random.normal(ks[2], (bs, seq, D_MODEL), jnp.float32), 'W_q': jax.random.normal(ks[3], (D_MODEL, D_MODEL), jnp.float32) * s, 'b_q': jnp.zeros((D_MODEL,), jnp.float32), 'W_k': jax.random.normal(ks[4], (D_MODEL, D_MODEL), jnp.float32) * s, 'b_k': jnp.zeros((D_MODEL,), jnp.float32), 'W_v': jax.random.normal(ks[5], (D_MODEL, D_MODEL), jnp.float32) * s, 'b_v': jnp.zeros((D_MODEL,), jnp.float32), 'W_o': jax.random.normal(ks[6], (D_MODEL, D_MODEL), jnp.float32) * s, 'b_o': jnp.zeros((D_MODEL,), jnp.float32)}
    _L1_xattn_all = _L1_xattn_setup()
    _L1_xattn_in = {k: v for k, v in _L1_xattn_all.items() if k in ('W_q', 'b_q', 'W_k', 'b_k', 'W_v', 'b_v', 'W_o', 'b_o')}
    del _L1_xattn_all

    def _L1_ffn_setup():
        import jax, jax.numpy as jnp
        import numpy as np
        MAX_THRESHOLD = 0.125
        key = jax.random.key(seed)
        ks = jax.random.split(key, 5)
        B, S, D, FF, E = (2, 256, 128, 512, 8)
        sd = 1.0 / np.sqrt(D)
        sf = 1.0 / np.sqrt(FF)
        return {'inputs': jax.random.normal(ks[0], (B, S, D), dtype=jnp.float32), 'Wg': jax.random.normal(ks[1], (D, E), dtype=jnp.float32) * sd, 'bg': jnp.zeros((E,), dtype=jnp.float32), 'Wt': jax.random.normal(ks[2], (D, 1), dtype=jnp.float32) * sd, 'bt': jnp.zeros((1,), dtype=jnp.float32), 'W1': jax.random.normal(ks[3], (E, D, FF), dtype=jnp.float32) * sd, 'b1': jnp.zeros((E, FF), dtype=jnp.float32), 'W2': jax.random.normal(ks[4], (E, FF, D), dtype=jnp.float32) * sf, 'b2': jnp.zeros((E, D), dtype=jnp.float32)}
    _L1_ffn_all = _L1_ffn_setup()
    _L1_ffn_in = {k: v for k, v in _L1_ffn_all.items() if k in ('Wg', 'bg', 'Wt', 'bt', 'W1', 'b1', 'W2', 'b2')}
    del _L1_ffn_all
    return {'x': x, 'ctx_1024': ctx_1024, 'fside_SxS2_0': fside_SxS2_0, 'L0_attn_Wq': _L0_attn_in['Wq'], 'L0_attn_Wk': _L0_attn_in['Wk'], 'L0_attn_Wv': _L0_attn_in['Wv'], 'L0_attn_Wo': _L0_attn_in['Wo'], 'L0_xattn_W_q': _L0_xattn_in['W_q'], 'L0_xattn_W_k': _L0_xattn_in['W_k'], 'L0_xattn_W_v': _L0_xattn_in['W_v'], 'L0_xattn_W_out': _L0_xattn_in['W_out'], 'L0_xattn_b_out': _L0_xattn_in['b_out'], 'L0_ffn_gate_w': _L0_ffn_in['gate_w'], 'L0_ffn_w1': _L0_ffn_in['w1'], 'L0_ffn_w2': _L0_ffn_in['w2'], 'L1_attn_wq_c': _L1_attn_in['wq_c'], 'L1_attn_wq_b': _L1_attn_in['wq_b'], 'L1_attn_wk_c': _L1_attn_in['wk_c'], 'L1_attn_wk_b': _L1_attn_in['wk_b'], 'L1_attn_wv_c': _L1_attn_in['wv_c'], 'L1_attn_wv_b': _L1_attn_in['wv_b'], 'L1_attn_wo_c': _L1_attn_in['wo_c'], 'L1_attn_wo_b': _L1_attn_in['wo_b'], 'L1_xattn_W_q': _L1_xattn_in['W_q'], 'L1_xattn_b_q': _L1_xattn_in['b_q'], 'L1_xattn_W_k': _L1_xattn_in['W_k'], 'L1_xattn_b_k': _L1_xattn_in['b_k'], 'L1_xattn_W_v': _L1_xattn_in['W_v'], 'L1_xattn_b_v': _L1_xattn_in['b_v'], 'L1_xattn_W_o': _L1_xattn_in['W_o'], 'L1_xattn_b_o': _L1_xattn_in['b_o'], 'L1_ffn_Wg': _L1_ffn_in['Wg'], 'L1_ffn_bg': _L1_ffn_in['bg'], 'L1_ffn_Wt': _L1_ffn_in['Wt'], 'L1_ffn_bt': _L1_ffn_in['bt'], 'L1_ffn_W1': _L1_ffn_in['W1'], 'L1_ffn_b1': _L1_ffn_in['b1'], 'L1_ffn_W2': _L1_ffn_in['W2'], 'L1_ffn_b2': _L1_ffn_in['b2']}

def reference(x, ctx_1024, fside_SxS2_0, L0_attn_Wq, L0_attn_Wk, L0_attn_Wv, L0_attn_Wo, L0_xattn_W_q, L0_xattn_W_k, L0_xattn_W_v, L0_xattn_W_out, L0_xattn_b_out, L0_ffn_gate_w, L0_ffn_w1, L0_ffn_w2, L1_attn_wq_c, L1_attn_wq_b, L1_attn_wk_c, L1_attn_wk_b, L1_attn_wv_c, L1_attn_wv_b, L1_attn_wo_c, L1_attn_wo_b, L1_xattn_W_q, L1_xattn_b_q, L1_xattn_W_k, L1_xattn_b_k, L1_xattn_W_v, L1_xattn_b_v, L1_xattn_W_o, L1_xattn_b_o, L1_ffn_Wg, L1_ffn_bg, L1_ffn_Wt, L1_ffn_bt, L1_ffn_W1, L1_ffn_b1, L1_ffn_W2, L1_ffn_b2):
    import jax
    import jax.numpy as jnp

    def _L0_attn_ref(x, Wq, Wk, Wv, Wo):
        import jax, jax.numpy as jnp
        import numpy as np
        import math
        N_HEADS = 16

        def _rope_tables(seq_len, head_dim):
            pos = jnp.arange(seq_len, dtype=jnp.float32)
            freqs = jnp.exp(jnp.arange(0, head_dim, 2, dtype=jnp.float32) * (-math.log(10000.0) / head_dim))
            angles = pos[:, None] * freqs[None, :]
            cos_emb = jnp.zeros((seq_len, head_dim), jnp.float32).at[:, 0::2].set(jnp.cos(angles))
            sin_emb = jnp.zeros((seq_len, head_dim), jnp.float32).at[:, 1::2].set(jnp.sin(angles))
            return (cos_emb, sin_emb)
        B, S, D = x.shape
        H = N_HEADS
        hd = D // H
        q = (x @ Wq.T).reshape(B, S, H, hd)
        k = (x @ Wk.T).reshape(B, S, H, hd)
        v = (x @ Wv.T).reshape(B, S, H, hd)
        cos_emb, sin_emb = _rope_tables(S, hd)
        cos = cos_emb[None, :, None, :]
        sin = sin_emb[None, :, None, :]
        q = q * cos - jnp.roll(q, 1, axis=-1) * sin
        k = k * cos - jnp.roll(k, 1, axis=-1) * sin
        q = q.transpose(0, 2, 1, 3)
        k = k.transpose(0, 2, 1, 3)
        v = v.transpose(0, 2, 1, 3)
        scores = jnp.einsum('bhqd,bhkd->bhqk', q, k) / math.sqrt(hd)
        attn = jax.nn.softmax(scores, axis=-1)
        ctx = jnp.einsum('bhqk,bhkd->bhqd', attn, v)
        ctx = ctx.transpose(0, 2, 1, 3).reshape(B, S, D)
        return ctx @ Wo.T

    def _L0_xattn_ref(x, context, bias, W_q, W_k, W_v, W_out, b_out):
        import jax, jax.numpy as jnp
        import numpy as np
        D_MODEL, D_HEAD, N_HEAD = (128, 64, 16)
        B, T1, T2 = (2, 256, 256)
        Bq, T1_, _ = x.shape
        T2_ = context.shape[1]
        atten_scale = 1.0 / np.sqrt(D_HEAD)
        head_scale = jnp.exp2(-jnp.arange(1, N_HEAD + 1, dtype=jnp.float32))
        q = (x @ W_q).reshape(Bq, T1_, N_HEAD, D_HEAD).transpose(0, 2, 1, 3)
        k = (context @ W_k).reshape(Bq, T2_, N_HEAD, D_HEAD).transpose(0, 2, 1, 3)
        v = (context @ W_v).reshape(Bq, T2_, N_HEAD, D_HEAD).transpose(0, 2, 1, 3)
        scores = jnp.einsum('bhqd,bhkd->bhqk', q, k) * atten_scale
        scores = scores + bias[None, None, :, :] * head_scale[None, :, None, None]
        attn = jax.nn.softmax(scores, axis=-1)
        out = jnp.einsum('bhqk,bhkd->bqhd', attn, v).reshape(Bq, T1_, N_HEAD * D_HEAD)
        return out @ W_out + b_out

    def _L0_ffn_ref(x, gate_w, w1, w2):
        import jax, jax.numpy as jnp
        import numpy as np
        NUM_EXPERTS = 8
        EXPERT_CAPACITY = 2.0
        B, T, C = x.shape
        E = gate_w.shape[1]
        cap = int(EXPERT_CAPACITY * T / E)
        scores = jnp.einsum('BTC,CE->BTE', x, gate_w)
        probs = jax.nn.softmax(scores, axis=-1)
        probs_et = jnp.transpose(probs, (0, 2, 1))
        top_p, top_idx = jax.lax.top_k(probs_et, cap)
        xin = jnp.take_along_axis(x[:, None, :, :], top_idx[..., None], axis=2)
        h = jax.nn.gelu(jnp.einsum('BElC,ECH->BElH', xin, w1), approximate=False)
        y = jnp.einsum('BElH,EHC->BElC', h, w2)
        y = y * top_p[..., None]
        b_idx = jnp.arange(B)[:, None, None]
        out = jnp.zeros((B, T, C), x.dtype).at[b_idx, top_idx].add(y)
        return out

    def _L1_attn_ref(x, wq_c, wq_b, wk_c, wk_b, wv_c, wv_b, wo_c, wo_b):
        import jax, jax.numpy as jnp
        import numpy as np
        D_MODEL = 128
        NUM_HEADS = 16
        HEAD_DIM = D_MODEL // NUM_HEADS
        BATCH = 4
        SEQ = 256

        def circulant(x, c, b):
            d = c.shape[0]
            y = jnp.fft.irfft(jnp.fft.rfft(x, axis=-1) * jnp.fft.rfft(c), n=d, axis=-1)
            return y + b
        bs, seq_len, dm = x.shape
        Q = circulant(x, wq_c, wq_b)
        K = circulant(x, wk_c, wk_b)
        V = circulant(x, wv_c, wv_b)
        Q = Q.reshape(bs, seq_len, NUM_HEADS, HEAD_DIM)
        K = K.reshape(bs, seq_len, NUM_HEADS, HEAD_DIM)
        V = V.reshape(bs, seq_len, NUM_HEADS, HEAD_DIM)
        scale = HEAD_DIM ** (-0.5)
        attn_logits = jnp.einsum('bqhd,bkhd->bhqk', Q, K) * scale
        attn_weights = jax.nn.softmax(attn_logits, axis=-1)
        out_heads = jnp.einsum('bhqk,bkhd->bqhd', attn_weights, V)
        out_merge = out_heads.reshape(bs, seq_len, dm)
        out = circulant(out_merge, wo_c, wo_b)
        return out

    def _L1_xattn_ref(q, k, v, W_q, b_q, W_k, b_k, W_v, b_v, W_o, b_o):
        import jax, jax.numpy as jnp
        import numpy as np
        D_MODEL = 128
        N_HEADS = 16
        D_K = D_MODEL // N_HEADS

        def _split_heads(x, bs):
            return x.reshape(bs, -1, N_HEADS, D_K).transpose(0, 2, 1, 3)
        bs = q.shape[0]
        qh = _split_heads(q @ W_q.T + b_q, bs)
        kh = _split_heads(k @ W_k.T + b_k, bs)
        vh = _split_heads(v @ W_v.T + b_v, bs)
        scores = jnp.einsum('bhqd,bhkd->bhqk', qh, kh) / jnp.sqrt(jnp.float32(D_K))
        weight = jax.nn.softmax(scores, axis=-1)
        attn = jnp.einsum('bhqk,bhkd->bhqd', weight, vh)
        concat = attn.transpose(0, 2, 1, 3).reshape(bs, -1, D_MODEL)
        return concat @ W_o.T + b_o

    def _L1_ffn_ref(inputs, Wg, bg, Wt, bt, W1, b1, W2, b2):
        import jax, jax.numpy as jnp
        import numpy as np
        MAX_THRESHOLD = 0.125
        x = inputs.reshape(-1, inputs.shape[-1])
        gate = jax.nn.softmax(x @ Wg + bg, axis=-1)
        thr = jax.nn.sigmoid(x @ Wt + bt) * MAX_THRESHOLD
        adapted = gate - thr
        mask = (adapted >= 0).astype(x.dtype)
        w = adapted * mask
        s = jnp.sum(w, axis=-1, keepdims=True)
        s = jnp.where(s == 0, jnp.ones_like(s), s)
        w = w / s
        h = jax.nn.gelu(jnp.einsum('td,edf->etf', x, W1) + b1[:, None, :])
        eo = jnp.einsum('etf,efd->etd', h, W2) + b2[:, None, :]
        out = jnp.einsum('te,etd->td', w, eo)
        return out.reshape(inputs.shape)
    x = x + _L0_attn_ref(_layernorm(x, axis=-1), L0_attn_Wq, L0_attn_Wk, L0_attn_Wv, L0_attn_Wo)
    x = x + _L0_xattn_ref(_layernorm(x, axis=-1), ctx_1024, fside_SxS2_0, L0_xattn_W_q, L0_xattn_W_k, L0_xattn_W_v, L0_xattn_W_out, L0_xattn_b_out)
    x = x + _L0_ffn_ref(_layernorm(x, axis=-1), L0_ffn_gate_w, L0_ffn_w1, L0_ffn_w2)
    x = x + _L1_attn_ref(_layernorm(x, axis=-1), L1_attn_wq_c, L1_attn_wq_b, L1_attn_wk_c, L1_attn_wk_b, L1_attn_wv_c, L1_attn_wv_b, L1_attn_wo_c, L1_attn_wo_b)
    x = x + _L1_xattn_ref(_layernorm(x, axis=-1), ctx_1024, ctx_1024, L1_xattn_W_q, L1_xattn_b_q, L1_xattn_W_k, L1_xattn_b_k, L1_xattn_W_v, L1_xattn_b_v, L1_xattn_W_o, L1_xattn_b_o)
    x = x + _L1_ffn_ref(_layernorm(x, axis=-1), L1_ffn_Wg, L1_ffn_bg, L1_ffn_Wt, L1_ffn_bt, L1_ffn_W1, L1_ffn_b1, L1_ffn_W2, L1_ffn_b2)
    return x

_drawn_inputs = setup_inputs


def setup_inputs(seed=0):
    import zlib

    import numpy as np

    out = dict(_drawn_inputs(seed))
    spreads = {'L0_xattn_b_out': (0.0, 0.1),
     'L1_attn_wq_b': (0.0, 0.8),
     'L1_attn_wk_b': (0.0, 2.0),
     'L1_attn_wv_b': (0.0, 0.289),
     'L1_attn_wo_b': (0.0, 0.1),
     'L1_xattn_b_q': (0.0, 0.8),
     'L1_xattn_b_k': (0.0, 2.0),
     'L1_xattn_b_v': (0.0, 0.1),
     'L1_xattn_b_o': (0.0, 0.1),
     'L1_ffn_bg': (0.0, 0.395),
     'L1_ffn_b1': (0.0, 0.388),
     'L1_ffn_b2': (0.0, 0.391)}
    factors = {'fside_SxS2_0': 6.917,
     'L0_ffn_gate_w': 8.0,
     'L0_ffn_w1': 8.0,
     'L0_ffn_w2': 8.0,
     'L1_ffn_Wt': 2.99}
    for name, (base, spread) in spreads.items():
        noise = np.random.default_rng([zlib.crc32(name.encode()), seed]).standard_normal(out[name].shape)
        drawn = base * np.exp(spread * noise) if base else spread * noise
        out[name] = jnp.asarray(drawn.astype(out[name].dtype))
    for name, factor in factors.items():
        out[name] = (out[name] * factor).astype(out[name].dtype)
    return out
```

```python
import math

import numpy as np

import concourse.bass as bass
from concourse import mybir
from contextlib import ExitStack

B, S, D = 16, 56, 128
NTOK = B * S
HALF = NTOK // 2
HB = B // 2
NH = 16
HQ = NH * S
NT = HQ // 128
HD = D // NH
XD = 64
S2 = 1500
KC = 125
NC = S2 // KC
KB = 500
NKB = S2 // KB
E = 8
FF = 512
NF = FF // 128
CAP = 2 * S // E
EPS = 1e-5
THRESHOLD = 0.125
GA, GB = 4, 3
WCOLS = E + 1
CONST_LOADS = 6
SA_LOADS, XA_LOADS, FFN_LOADS = 12, 9, 6 + B


def decoder_kernel(nc, t, out):
    fp32, bf16 = mybir.dt.float32, mybir.dt.bfloat16
    ALU, ACT, AX = mybir.AluOpType, mybir.ActivationFunctionType, mybir.AxisListType.X

    ctx = ExitStack()
    with ctx:
        def sb(name, shape, dt=fp32):
            return ctx.enter_context(nc.sbuf_tensor(name, shape, dt))

        def sem(name):
            return ctx.enter_context(nc.semaphore(name))

        ident = sb("ident", [128, 128])
        ones = sb("ones", [128, 128])
        mean_w = sb("mean_w", [128, 128])
        eps = sb("eps", [128, 1])
        head_mask = sb("head_mask", [128, NH])
        batch_mask = sb("batch_mask", [128, B])
        expert_mask = sb("expert_mask", [128, E])
        rope = sb("rope", [128, 2, S])
        bias_sel = sb("bias_sel", [128, HQ], bf16)
        sa_w = [sb(f"sa_w{l}", [128, 4, 128]) for l in range(2)]
        sa_bias = sb("sa_bias", [128, 4])
        sa_bv = sb("sa_bv", [128, D])
        qk_fold = sb("qk_fold", [128, NH, 128])
        vo_fold = sb("vo_fold", [128, NH, 128])
        xa_w = sb("xa_w", [128, 4, 128])
        xa_bias = sb("xa_bias", [128, 5])
        xa_bv = sb("xa_bv", [128, D])
        gate_w = [sb(f"gate_w{l}", [128, WCOLS]) for l in range(2)]
        gate_b = sb("gate_b", [S, WCOLS])
        b1 = sb("b1", [128, 2, E * NF])
        b2 = sb("b2", [128, D])
        X = sb("X", [128, NTOK])
        XC = sb("XC", [128, NTOK])
        SQ = sb("SQ", [128, NTOK])
        XN = sb("XN", [128, NTOK])
        q_all = sb("q_all", [128, NTOK])
        q_diag = [sb(f"q_diag{i}", [128, HQ]) for i in range(2)]
        sm_stat = sb("sm_stat", [128, 2, 4, NT])
        QO = sb("QO", [128, B, HQ])
        kT = [sb(f"kT{i}", [128, S2]) for i in range(2)]
        ctxT = sb("ctxT", [128, S2])
        vals = [sb(f"vals{i}", [128, NC, 128]) for i in range(2)]
        prob = [sb("prob_a", [128, GA, S2]), sb("prob_b", [128, GB, S2])]
        pT = [sb(f"pT{i}", [128, 512]) for i in range(3)]
        part_max = sb("part_max", [128, 2, NKB])
        neg_max = sb("neg_max", [128, NT])
        row_sum = sb("row_sum", [128, NT])
        row_inv = sb("row_inv", [128, NT])
        inv_diag = [sb(f"inv_diag{i}", [128, 4, 128]) for i in range(2)]
        inv_cols = sb("inv_cols", [128, 512])
        bias12 = sb("bias12", [128, S2], bf16)
        bias3 = sb("bias3", [128, S2], bf16)
        w1 = [sb(f"w1_{i}", [128, FF]) for i in range(2)]
        w2 = [sb(f"w2_{i}", [128, NF, D]) for i in range(2)]
        hidden = prob[0][:, :, 0:NTOK]
        gate_stat = sb("gate_stat", [S, 4, B])
        gT = sb("gT", [128, S])
        work = sb("work", [128, 64])
        work2 = sb("work2", [128, 64])
        top8 = sb("top8", [128, 2, 8])
        w_be = sb("w_be", [128, S])
        QO_flat = QO[:, :, :].rearrange("p b q -> p (b q)")
        taken = [0]

        def carve(rows, cols):
            at = taken[0]
            taken[0] += cols
            assert taken[0] <= B * HQ
            return QO_flat[0:rows, at:at + cols]

        k_all, att = carve(128, NTOK), carve(128, NTOK)
        v_flat = carve(S, B * D)
        v_all = v_flat.rearrange("p (b d) -> p b d", b=B)
        sm_d = [carve(128, NT * S).rearrange("p (j s) -> p j s", j=NT) for i in range(2)]
        sm_p = [carve(128, NT * S + 128 - S) for i in range(2)]
        sm_pT = [carve(S, HQ + 128 - S) for i in range(2)]
        sm_o = [carve(128, D) for i in range(2)]
        w_blk = carve(128, NTOK).rearrange("p (b s) -> p b s", b=B)
        w_blk_e = carve(128, 2 * NTOK).rearrange("p (a s) -> p a s", a=2)
        w_cols = carve(128, 2 * NTOK).rearrange("p (a s) -> p a s", a=2)
        gate = carve(S, B * WCOLS).rearrange("p (b e) -> p b e", b=B)
        gate2 = carve(S, B * E).rearrange("p (b e) -> p b e", b=B)
        routed = carve(S, B * E).rearrange("p (b e) -> p b e", b=B)
        fold_in = prob[1][:, :, :].rearrange("p j n -> p (j n)")[:, 0:4 * 8 * 128]\
            .rearrange("p (w g c) -> p w g c", w=4, g=8)

        PS = ctx.enter_context(nc.psum_tensor("PS", [128, 8, 512], fp32))
        PSF = PS[:, :, :].rearrange("p a b -> p (a b)")

        def two(bank):
            return PS[:, bank:bank + 2, 0:HALF]

        def halves(x):
            return x.rearrange("p (a b) -> p a b", a=2)

        ld_x, ld_const, ld_sa, ld_fold, ld_xa, ld_ffn, ld_bias = (
            sem(n) for n in ("ld_x", "ld_const", "ld_sa", "ld_fold", "ld_xa", "ld_ffn", "ld_bias"))
        out_done = sem("out_done")
        consts_set = sem("consts_set")
        x_ready = sem("x_ready")
        ln_mean, ln_centred, ln_squared, ln_var, ln_std, xn_ready = (
            sem(n) for n in ("ln_mean", "ln_centred", "ln_squared", "ln_var", "ln_std", "xn_ready"))
        dve_step = sem("dve_step")
        names = ("q k v qkv diag scores sub exp norm tr trc pv pvc otr att out").split()
        sa = [{n: sem(f"sa{l}_{n}") for n in names} for l in range(2)]
        fold_mm, fold_ev = sem("fold_mm"), sem("fold_ev")
        bias_split = sem("bias_split")
        names = ("q diag scores mx exp tr trc pv idiag inv invc norm out "
                 "kmm kev vmm vev vo qp qpa qpd").split()
        xa = [{n: sem(f"xa{l}_{n}") for n in names} for l in range(2)]
        ld_k = [[sem(f"ld_k{l}{i}") for i in range(2)] for l in range(2)]
        ld_v = [sem(f"ld_v{i}") for i in range(2)]
        names = ("logit gexp gsub gates gtr blk wsel wmm wcols h hact y ymul b2mm").split()
        ff = [{n: sem(f"ff{l}_{n}") for n in names} for l in range(2)]
        ld_w = [[sem(f"ld_w{l}{i}") for i in range(2)] for l in range(2)]

        class Chain:
            def __init__(self):
                self.count = 0

            def link(self, eng, ins):
                ins.then_inc(dve_step, 1)
                self.count = self.count + 1
                eng.wait_ge(dve_step, self.count)

        def norm_tensor(pe, n):
            if n == 0:
                pe.wait_ge(ld_x, 16)
                pe.wait_ge(fold_ev, 8)
                pe.wait_ge(consts_set, 1)
            else:
                pe.wait_ge(x_ready, n)
            for h in range(2):
                mm = nc.tensor.matmul(PS[:, h, 0:HALF], mean_w[:, :], X[:, h * HALF:(h + 1) * HALF],
                                      start=True, stop=True)
            mm.then_inc(ln_mean, 1)
            pe.wait_ge(ln_squared, n + 1)
            for h in range(2):
                mm = nc.tensor.matmul(PS[:, 2 + h, 0:HALF], mean_w[:, :], SQ[:, h * HALF:(h + 1) * HALF],
                                      start=True, stop=True)
            mm.then_inc(ln_var, 1)

        def norm_scalar(act, n):
            act.wait_ge(ln_centred, n + 1)
            nc.scalar.activation(SQ[:, :], XC[:, :], ACT.Square).then_inc(ln_squared, 1)
            act.wait_ge(ln_var, n + 1)
            nc.scalar.activation(halves(SQ[:, :]), two(2), ACT.Sqrt, bias=eps[:, 0:1]).then_inc(ln_std, 1)

        def norm_vector(dve, n, chain):
            dve.wait_ge(ln_mean, n + 1)
            nc.vector.tensor_tensor(halves(XC[:, :]), halves(X[:, :]), two(0), ALU.subtract)\
                .then_inc(ln_centred, 1)
            dve.wait_ge(ln_std, n + 1)
            chain.link(dve, nc.vector.reciprocal(SQ[:, :], SQ[:, :]))
            nc.vector.tensor_tensor(XN[:, :], XC[:, :], SQ[:, :], ALU.mult).then_inc(xn_ready, 1)

        def wait_past(eng, signal, b, back):
            if not isinstance(b, int) or b >= back:
                eng.wait_ge(signal, b - (back - 1))

        def self_tensor(pe, l, n):
            m = sa[l]
            if l == 0:
                pe.wait_ge(ld_sa, 16 * SA_LOADS)
            pe.wait_ge(xn_ready, n + 1)
            for w in range(2):
                for h in range(2):
                    mm = nc.tensor.matmul(PS[:, 2 * w + h, 0:HALF], sa_w[l][:, w, :],
                                          XN[:, h * HALF:(h + 1) * HALF], start=True, stop=True)
                mm.then_inc(m["q"], 1)
            for b in range(B):
                mm = nc.tensor.matmul(PS[0:S, 4 + b // 4, (b % 4) * 128:(b % 4 + 1) * 128],
                                      XN[:, b * S:(b + 1) * S], sa_w[l][:, 2, :], start=True, stop=True)
            mm.then_inc(m["v"], 1)
            pe.wait_ge(m["qkv"], 3)

            def scores(b, p):
                wait_past(pe, m["sub"], b, 2)
                pe.wait_ge(m["diag"], b + 1)
                for j in range(NT):
                    mm = nc.tensor.matmul(PS[:, p, j * S:(j + 1) * S], q_diag[p][:, j * 128:(j + 1) * 128],
                                          k_all[:, bass.ds(b * S, S)], start=True, stop=True)
                mm.then_inc(m["scores"], 1)

            def values(b, p):
                pe.wait_ge(m["norm"], b + 1)
                wait_past(pe, m["trc"], b, 2)
                base = (2 + 2 * p) * 512
                for j in range(NT):
                    mm = nc.tensor.transpose(PSF[:, base + j * 128:base + (j + 1) * 128],
                                             sm_p[p][:, j * S:j * S + 128], ident[:, :])
                mm.then_inc(m["tr"], 1)
                pe.wait_ge(m["trc"], b + 1)
                wait_past(pe, m["pvc"], b, 1)
                for h in range(NH):
                    mm = nc.tensor.matmul(PS[:, 6, h * HD:(h + 1) * HD], sm_pT[p][:, h * S:h * S + 128],
                                          v_flat[:, bass.ds(b * D + h * HD, HD)], start=True, stop=True)
                mm.then_inc(m["pv"], 1)

            def turn(b, p):
                pe.wait_ge(m["pvc"], b + 1)
                wait_past(pe, m["att"], b, 1)
                nc.tensor.transpose(PS[:, 7, 0:128], sm_o[p][:, :], ident[:, :]).then_inc(m["otr"], 1)

            scores(0, 0)
            scores(1, 1)
            values(0, 0)

            def step(b, p):
                scores(b + 1, 1 - p)
                values(b, p)
                turn(b - 1, 1 - p)

            step(1, 1)
            step(2, 0)
            with pe.Fori(3, B - 2, 2) as i:
                step(i, 1)
                step(i + 1, 0)
            values(B - 1, 1)
            turn(B - 2, 0)
            turn(B - 1, 1)
            pe.wait_ge(m["att"], B)
            for h in range(2):
                mm = nc.tensor.matmul(PS[:, h, 0:HALF], sa_w[l][:, 3, :], att[:, h * HALF:(h + 1) * HALF],
                                      start=True, stop=True)
            mm.then_inc(m["out"], 1)

        def self_gpsimd(pool, l):
            m = sa[l]

            def diagonal(b, p):
                wait_past(pool, m["scores"], b, 2)
                q = q_all[:, bass.ds(b * S, S)].rearrange("p (a q) -> p a q", a=1)
                nc.gpsimd.tensor_tensor(
                    q_diag[p][:, :].rearrange("p (h q) -> p h q", h=NH), q.broadcast_to([128, NH, S]),
                    head_mask[:, :].rearrange("p (h a) -> p h a", a=1).broadcast_to([128, NH, S]),
                    ALU.mult).then_inc(m["diag"], 1)

            pool.wait_ge(m["qkv"], 1)
            diagonal(0, 0)
            diagonal(1, 1)
            with pool.Fori(2, B - 1, 2) as i:
                for k in range(2):
                    diagonal(i + k, k)

        def self_scalar(act, l):
            m = sa[l]

            def exps(b, p):
                act.wait_ge(m["sub"], b + 1)
                wait_past(act, m["norm"], b, 2)
                nc.scalar.activation(sm_d[p][:, :, :], sm_d[p][:, :, :], ACT.Exp).then_inc(m["exp"], 1)

            def copy_probs(b, p):
                act.wait_ge(m["tr"], b + 1)
                wait_past(act, m["pv"], b, 2)
                base = (2 + 2 * p) * 512
                nc.scalar.activation(sm_pT[p][:, 0:HQ], PSF[0:S, base:base + HQ], ACT.Copy).then_inc(m["trc"], 1)

            def copy_out(b):
                act.wait_ge(m["otr"], b + 1)
                nc.scalar.activation(att[:, bass.ds(b * S, S)], PS[:, 7, 0:S], ACT.Copy).then_inc(m["att"], 1)

            exps(0, 0)
            exps(1, 1)
            copy_probs(0, 0)

            def step(b, p):
                exps(b + 1, 1 - p)
                copy_probs(b, p)
                copy_out(b - 1)

            step(1, 1)
            step(2, 0)
            with act.Fori(3, B - 2, 2) as i:
                step(i, 1)
                step(i + 1, 0)
            copy_probs(B - 1, 1)
            copy_out(B - 2)
            copy_out(B - 1)

        def self_vector(dve, l, chain):
            m = sa[l]
            for p in range(2):
                nc.vector.memset(sm_p[p][:, NT * S:], 0.0)
                chain.link(dve, nc.vector.memset(sm_pT[p][:, HQ:], 0.0))
            dve.wait_ge(m["q"], 1)
            if l == 0:
                dve.wait_ge(ld_const, 16 * CONST_LOADS)
                for w, x in ((0, q_all), (1, k_all)):
                    if w == 1:
                        dve.wait_ge(m["q"], 2)
                    table = rope[:, w, :].rearrange("p (a s) -> p a s", a=1).broadcast_to([128, HB, S])
                    for h in range(2):
                        ins = nc.vector.tensor_tensor(
                            x[:, h * HALF:(h + 1) * HALF].rearrange("p (b s) -> p b s", b=HB),
                            PS[:, 2 * w + h, 0:HALF].rearrange("p (b s) -> p b s", b=HB), table, ALU.mult)
                    ins.then_inc(m["qkv"], 1)
            else:
                nc.vector.tensor_scalar(halves(q_all[:, :]), two(0), sa_bias[:, 0:1], HD ** -0.5,
                                        ALU.add, ALU.mult).then_inc(m["qkv"], 1)
                dve.wait_ge(m["q"], 2)
                nc.vector.tensor_scalar(halves(k_all[:, :]), two(2), sa_bias[:, 1:2], None, ALU.add)\
                    .then_inc(m["qkv"], 1)
            dve.wait_ge(m["v"], 1)
            v_psum = PSF[0:S, 4 * 512:8 * 512].rearrange("p (b d) -> p b d", b=B)
            if l == 0:
                nc.vector.tensor_copy(v_all[:, :, :], v_psum).then_inc(m["qkv"], 1)
            else:
                nc.vector.tensor_tensor(
                    v_all[:, :, :], v_psum,
                    sa_bv[0:S, :].rearrange("p (a d) -> p a d", a=1).broadcast_to([S, B, D]),
                    ALU.add).then_inc(m["qkv"], 1)

            def stat(p, k):
                return sm_stat[:, p, k, :]

            def spread(x):
                return x.rearrange("p (j a) -> p j a", a=1).broadcast_to([128, NT, S])

            def centre(b, p):
                dve.wait_ge(m["scores"], b + 1)
                sc = PS[:, p, 0:NT * S].rearrange("p (j k) -> p j k", j=NT)
                chain.link(dve, nc.vector.tensor_reduce(stat(p, 0), sc, AX, ALU.max))
                wait_past(dve, m["norm"], b, 2)
                nc.vector.tensor_tensor(sm_d[p][:, :, :], sc, spread(stat(p, 0)), ALU.subtract)\
                    .then_inc(m["sub"], 1)

            def normalise(b, p):
                dve.wait_ge(m["exp"], b + 1)
                chain.link(dve, nc.vector.tensor_reduce(stat(p, 1), sm_d[p][:, :, :], AX, ALU.add))
                chain.link(dve, nc.vector.reciprocal(stat(p, 2), stat(p, 1)))
                wait_past(dve, m["tr"], b, 2)
                nc.vector.tensor_tensor(sm_p[p][:, 0:NT * S].rearrange("p (j s) -> p j s", j=NT), sm_d[p][:, :, :], spread(stat(p, 2)), ALU.mult)\
                    .then_inc(m["norm"], 1)

            def copy_out(b, p):
                dve.wait_ge(m["pv"], b + 1)
                wait_past(dve, m["otr"], b, 2)
                nc.vector.tensor_copy(sm_o[p][:, :], PS[:, 6, 0:D]).then_inc(m["pvc"], 1)

            centre(0, 0)
            centre(1, 1)
            normalise(0, 0)

            def step(b, p):
                centre(b + 1, 1 - p)
                normalise(b, p)
                copy_out(b - 1, 1 - p)

            step(1, 1)
            step(2, 0)
            start = chain.count
            with dve.Fori(3, B - 2, 2) as i:
                chain.count = (i - 3) * 3 + start
                step(i, 1)
                step(i + 1, 0)
            chain.count = start + 3 * (B - 4)
            normalise(B - 1, 1)
            copy_out(B - 2, 0)
            copy_out(B - 1, 1)
            dve.wait_ge(m["out"], 1)
            if l == 0:
                nc.vector.tensor_tensor(halves(X[:, :]), halves(X[:, :]), two(0), ALU.add).then_inc(x_ready, 1)
            else:
                nc.vector.scalar_tensor_tensor(halves(X[:, :]), two(0), sa_bias[:, 3:4], halves(X[:, :]),
                                               ALU.add, ALU.add).then_inc(x_ready, 1)

        def fold_tensor(pe):
            pe.wait_ge(ld_fold, 16 * 4)
            for k in range(8):
                odd, r = k // 2 % 2, slice(XD * (k // 2 % 2), XD * (k // 2 % 2) + XD)
                for j in range(4):
                    pair = 4 * (k % 2) + j
                    mm = nc.tensor.matmul(PS[:, k, j * 128:(j + 1) * 128], fold_in[r, 2 * (k // 4), pair, :],
                                          fold_in[r, 2 * (k // 4) + 1, pair, :], start=True, stop=True)
                mm.then_inc(fold_mm, 1)

        def fold_scalar(act):
            for k in range(8):
                act.wait_ge(fold_mm, k + 1)
                dst = (qk_fold, vo_fold)[k // 4][:, :, :].rearrange("p (g a) c -> p a g c", a=2)
                nc.scalar.activation(dst[:, k // 2 % 2, 4 * (k % 2):4 * (k % 2) + 4, :],
                                     PS[:, k, :].rearrange("p (h c) -> p h c", h=4), ACT.Copy,
                                     scale=XD ** -0.5 if k < 4 else 1.0).then_inc(fold_ev, 1)

        def bias_vector(dve, chain):
            f, part = prob[0][:, 0, :], prob[0][:, 1, :]
            dve.wait_ge(ld_bias, 32)
            dve.wait_ge(consts_set, 2)
            chain.link(dve, nc.vector.tensor_copy(bias12[:, :], f))
            chain.link(dve, nc.vector.tensor_copy(part, bias12[:, :]))
            chain.link(dve, nc.vector.tensor_tensor(f, f, part, ALU.subtract))
            chain.link(dve, nc.vector.tensor_copy(bias3[:, :], f))
            chain.link(dve, nc.vector.tensor_copy(bias12[64:128, :], bias3[64:128, :]))
            chain.link(dve, nc.vector.tensor_copy(part, bias3[:, :]))
            chain.link(dve, nc.vector.tensor_tensor(f, f, part, ALU.subtract))
            chain.link(dve, nc.vector.tensor_copy(bias3[:, :], f))
            nc.vector.memset(bias3[64:128, :], 0.0).then_inc(bias_split, 1)

        def cross_tensor(pe, l, n):
            m = xa[l]
            pe.wait_ge(xn_ready, n + 1)
            if l == 0:
                pe.wait_ge(fold_ev, 8)
                for h in range(NH):
                    p = h % 2
                    if h >= 2:
                        pe.wait_ge(m["qpa" if p == 0 else "qpd"], h // 2)
                    for a in range(2):
                        mm = nc.tensor.matmul(PS[:, 2 * p + a, 0:HALF], qk_fold[:, h, :],
                                              XN[:, a * HALF:(a + 1) * HALF], start=True, stop=True)
                    mm.then_inc(m["qp"], 1)
                pe.wait_ge(m["qpa"], NH // 2)
                pe.wait_ge(m["qpd"], NH // 2)
                pe.wait_ge(bias_split, 1)
            else:
                pe.wait_ge(ld_xa, 16 * XA_LOADS)
                for a in range(2):
                    mm = nc.tensor.matmul(PS[:, a, 0:HALF], xa_w[:, 0, :], XN[:, a * HALF:(a + 1) * HALF],
                                          start=True, stop=True)
                mm.then_inc(m["qp"], 1)
                pe.wait_ge(m["qpd"], 1)

            def project(b, par, piece):
                if piece == 0:
                    pe.wait_ge(ld_k[1][0], (b + 1) * 16)
                    wait_past(pe, m["invc"], 2 * b, 4)
                    if not isinstance(b, int) or b:
                        pe.wait_ge(m["vev"], 3 * b)
                if piece == 3:
                    wait_past(pe, m["invc"], 2 * b, 3)
                if piece < 3:
                    if piece:
                        pe.wait_ge(m["kev"], 3 * b + piece)
                    nc.tensor.matmul(PS[:, 7, 0:KB], xa_w[:, 1, :], ctxT[:, piece * KB:(piece + 1) * KB],
                                     start=True, stop=True).then_inc(m["kmm"], 1)
                else:
                    if piece == 3:
                        pe.wait_ge(m["kev"], 3 * b + 3)
                    else:
                        pe.wait_ge(m["vev"], 3 * b + piece - 3)
                    for j in range(4):
                        c = 4 * (piece - 3) + j
                        mm = nc.tensor.matmul(PS[0:KC, 7, j * 128:(j + 1) * 128],
                                              ctxT[:, c * KC:(c + 1) * KC], xa_w[:, 2, :],
                                              start=True, stop=True)
                    mm.then_inc(m["vmm"], 1)

            def scores(b, par, s):
                if s == 0:
                    pe.wait_ge(m["q"], b + 1)
                    if l == 0:
                        pe.wait_ge(ld_k[0][par], (b // 2 + 1) * 16 if isinstance(b, int) else
                                   (b - par) * 8 + 16)
                    else:
                        pe.wait_ge(m["kev"], 3 * b + 3)
                wait_past(pe, m["exp"], NT * b + s, 1)
                for j in range(NKB):
                    cols = slice(j * KB, (j + 1) * KB)
                    mm = nc.tensor.matmul(PS[:, j, 0:KB], q_diag[par][:, s * 128:(s + 1) * 128],
                                          kT[par][:, cols], start=True, stop=l == 1)
                    if l == 0:
                        sel = bias_sel[:, s * 128:(s + 1) * 128]
                        nc.tensor.matmul(PS[:, j, 0:KB], sel, bias12[:, cols], start=False, stop=False)
                        mm = nc.tensor.matmul(PS[:, j, 0:KB], sel, bias3[:, cols], start=False, stop=True)
                    mm.then_inc(m["scores"], 1)

            def transposes(b, g, k):
                at = 2 * NC * b + NC * g + k
                size = (GA, GB)[g]
                if k == 0:
                    pe.wait_ge(m["exp"], NT * b + (GA if g == 0 else NT))
                wait_past(pe, m["trc"], at, 2)
                for j in range(size):
                    mm = nc.tensor.transpose(PS[0:KC, 3 + k % 2, j * 128:(j + 1) * 128],
                                             prob[g][:, j, k * KC:(k + 1) * KC], ident[:, :])
                mm.then_inc(m["tr"], 1)

            def product(b, par, g, k):
                at = 2 * NC * b + NC * g + k
                size = (GA, GB)[g]
                if k == 0:
                    wait_past(pe, m["norm"], 2 * b + g, 2)
                    if g == 0:
                        if l == 0:
                            pe.wait_ge(ld_v[par], (b // 2 + 1) * 16 if isinstance(b, int) else
                                       (b - par) * 8 + 16)
                        else:
                            pe.wait_ge(m["vev"], 3 * b + 3)
                pe.wait_ge(m["trc"], at + 1)
                nc.tensor.matmul(PS[:, 5 + g, 0:128 * size], vals[par][0:KC, k, :],
                                 pT[k % 3][0:KC, 0:128 * size], start=k == 0, stop=k == NC - 1)\
                    .then_inc(m["pv"], 1)

            def sums(b, g):
                size = (GA, GB)[g]
                pe.wait_ge(m["idiag"], 2 * b + g + 1)
                wait_past(pe, m["invc"], 2 * b + g, 1)
                if l == 1 and not (isinstance(b, int) and b + (2 if g else 1) >= B):
                    pe.wait_ge(m["kev" if g else "vev"], 3 * b + (9 if g else 6))
                nc.tensor.matmul(PS[:, 7, 0:128 * size], ones[:, :],
                                 inv_diag[g][:, 0:size, :].rearrange("p a b -> p (a b)"),
                                 start=True, stop=True).then_inc(m["inv"], 1)

            def chunk(b, par, g, k, first):
                transposes(b, g, k)
                if k:
                    product(b, par, g, k - 1)
                elif not first:
                    pb, pp, pg = (b, par, 0) if g else (b - 1, 1 - par, 1)
                    product(pb, pp, pg, NC - 1)
                    sums(pb, pg)

            def batch(b, par):
                first = isinstance(b, int) and b == 0
                last = isinstance(b, int) and b == B - 1
                for s in range(NT):
                    scores(b, par, s)
                    if s < GA and not first:
                        for k in range(3 * s, 3 * s + 3):
                            chunk(b - 1, 1 - par, 1, k, False)
                    if s >= GA:
                        for k in range(4 * (s - GA), 4 * (s - GA) + 4):
                            chunk(b, par, 0, k, first)
                    if l == 1 and not last and s != 3:
                        project(b + 1, 1 - par, s if s < 3 else s - 1)

            if l == 1:
                for piece in range(6):
                    project(0, 0, piece)
            batch(0, 0)
            with pe.Fori(1, B - 2, 2) as i:
                batch(i, 1)
                batch(i + 1, 0)
            batch(B - 1, 1)
            for k in range(NC):
                chunk(B - 1, 1, 1, k, False)
            product(B - 1, 1, 1, NC - 1)
            sums(B - 1, 1)
            pe.wait_ge(m["norm"], 2 * B)
            if l == 1:
                pe.wait_ge(m["vo"], 1)
            for h in range(NH):
                for a in range(2):
                    mm = nc.tensor.matmul(PS[:, a, 0:HALF], vo_fold[:, h, :],
                                          QO[:, a * HB:(a + 1) * HB, h * S:(h + 1) * S],
                                          start=h == 0, stop=h == NH - 1)
            mm.then_inc(m["out"], 1)

        def cross_gpsimd(pool, l):
            m = xa[l]
            if l == 1:
                pool.wait_ge(x_ready, 2)
                pool.wait_ge(ld_xa, 16 * XA_LOADS)
                nc.gpsimd.tensor_tensor(
                    vo_fold[:, :, :],
                    xa_w[:, 3, :].rearrange("p (a o) -> p a o", a=1).broadcast_to([128, NH, 128]),
                    head_mask[:, :].rearrange("p (h a) -> p h a", a=1).broadcast_to([128, NH, 128]),
                    ALU.mult).then_inc(m["vo"], 1)
                pool.wait_ge(m["qpd"], 1)
            else:
                pool.wait_ge(m["qpa"], NH // 2)
                pool.wait_ge(m["qpd"], NH // 2)

            def queries(b, par):
                wait_past(pool, m["scores"], 21 * b, 22)
                if l == 0:
                    nc.gpsimd.tensor_copy(q_diag[par][:, :], QO_flat[:, bass.ds(b * HQ, HQ)])\
                        .then_inc(m["q"], 1)
                else:
                    q = q_all[:, bass.ds(b * S, S)].rearrange("p (a q) -> p a q", a=1)
                    nc.gpsimd.tensor_tensor(
                        q_diag[par][:, :].rearrange("p (h q) -> p h q", h=NH), q.broadcast_to([128, NH, S]),
                        head_mask[:, :].rearrange("p (h a) -> p h a", a=1).broadcast_to([128, NH, S]),
                        ALU.mult).then_inc(m["q"], 1)

            queries(0, 0)
            queries(1, 1)
            with pool.Fori(2, B - 1, 2) as i:
                queries(i, 0)
                queries(i + 1, 1)

        def cross_sync(sp, l):
            m = xa[l]

            def load_k(b, par):
                if l == 0:
                    wait_past(sp, m["scores"], 21 * b, 22)
                    sp.dma_start(kT[par][:, :], t["ctx_T"][bass.ds(b, 1), :, :].rearrange("a p n -> (a p) n"))\
                        .then_inc(ld_k[0][par], 16)
                else:
                    wait_past(sp, m["vmm"], 3 * b, 1)
                    sp.dma_start(ctxT[:, :], t["ctx_T"][bass.ds(b, 1), :, :].rearrange("a p n -> (a p) n"))\
                        .then_inc(ld_k[1][0], 16)

            def load_v(b, par):
                wait_past(sp, m["pv"], 2 * NC * b, 2 * NC + 1)
                sp.dma_start(vals[par][0:KC, :, :],
                             t["ctx_1024"][bass.ds(b, 1), :, :].rearrange("a (c p) d -> (a p) c d", p=KC))\
                    .then_inc(ld_v[par], 16)

            if l == 1:
                sp.wait_ge(x_ready, 3)
            for b in range(2):
                load_k(b, b)
                if l == 0:
                    load_v(b, b)
            with sp.Fori(2, B - 1, 2) as i:
                for p in range(2):
                    load_k(i + p, p)
                    if l == 0:
                        load_v(i + p, p)

        def cross_scalar(act, l):
            m = xa[l]
            if l == 0:
                for h in range(0, NH, 2):
                    act.wait_ge(m["qp"], h + 1)
                    for a in range(2):
                        ins = nc.scalar.activation(
                            QO[:, a * HB:(a + 1) * HB, h * S:(h + 1) * S],
                            PS[:, a, 0:HALF].rearrange("p (b s) -> p b s", b=HB), ACT.Copy)
                    ins.then_inc(m["qpa"], 1)

            def keys(b, par, piece):
                act.wait_ge(m["kmm"], 3 * b + piece + 1)
                if piece == 0:
                    wait_past(act, m["scores"], 21 * b, 22)
                nc.scalar.activation(kT[par][:, piece * KB:(piece + 1) * KB], PS[:, 7, 0:KB], ACT.Identity,
                                     bias=xa_bias[:, 1:2]).then_inc(m["kev"], 1)

            def exps(b, par, s):
                g = 0 if s < GA else 1
                act.wait_ge(m["mx"], NT * b + s + 1)
                if s == 0:
                    wait_past(act, m["tr"], 2 * NC * b, 1 + NC)
                if s == GA:
                    wait_past(act, m["tr"], 2 * NC * b, 1)
                if s == 0 or s == GA:
                    wait_past(act, m["idiag"], 2 * b + g, 2)
                nc.scalar.activation(prob[g][:, s - GA * g, :].rearrange("p (j k) -> p j k", j=NKB),
                                     PS[:, 0:NKB, 0:KB], ACT.Exp, bias=neg_max[:, s:s + 1],
                                     accum_out=row_sum[:, s:s + 1]).then_inc(m["exp"], 1)

            def copy_inv(b, g):
                act.wait_ge(m["inv"], 2 * b + g + 1)
                wait_past(act, m["norm"], 2 * b + g, 1)
                nc.scalar.activation(inv_cols[:, 0:128 * (GA, GB)[g]], PS[:, 7, 0:128 * (GA, GB)[g]],
                                     ACT.Copy).then_inc(m["invc"], 1)

            def batch(b, par):
                first = isinstance(b, int) and b == 0
                last = isinstance(b, int) and b == B - 1
                for s in range(NT):
                    exps(b, par, s)
                    if s == 0 and not first:
                        copy_inv(b - 1, 0)
                    if s == GA and not first:
                        copy_inv(b - 1, 1)
                    if l == 1 and not last and s < 3:
                        keys(b + 1, 1 - par, s)

            if l == 1:
                for piece in range(3):
                    keys(0, 0, piece)
            batch(0, 0)
            with act.Fori(1, B - 2, 2) as i:
                batch(i, 1)
                batch(i + 1, 0)
            batch(B - 1, 1)
            copy_inv(B - 1, 0)
            copy_inv(B - 1, 1)

        def cross_vector(dve, l, chain):
            m = xa[l]
            if l == 0:
                for h in range(1, NH, 2):
                    dve.wait_ge(m["qp"], h + 1)
                    for a in range(2):
                        ins = nc.vector.tensor_copy(
                            QO[:, a * HB:(a + 1) * HB, h * S:(h + 1) * S],
                            PS[:, 2 + a, 0:HALF].rearrange("p (b s) -> p b s", b=HB))
                    ins.then_inc(m["qpd"], 1)
            else:
                dve.wait_ge(m["qp"], 1)
                nc.vector.tensor_scalar(halves(q_all[:, :]), two(0), xa_bias[:, 0:1], HD ** -0.5,
                                        ALU.add, ALU.mult).then_inc(m["qpd"], 1)

            def values(b, par, piece):
                dve.wait_ge(m["vmm"], 3 * b + piece + 1)
                if piece == 0:
                    wait_past(dve, m["pv"], 2 * NC * b, 2 * NC + 1)
                nc.vector.tensor_tensor(
                    vals[par][0:KC, 4 * piece:4 * piece + 4, :],
                    PS[0:KC, 7, :].rearrange("p (c d) -> p c d", c=4),
                    xa_bv[0:KC, :].rearrange("p (a d) -> p a d", a=1).broadcast_to([KC, 4, D]),
                    ALU.add).then_inc(m["vev"], 1)

            def maxima(b, s):
                for j in range(NKB):
                    dve.wait_ge(m["scores"], 21 * b + NKB * s + j + 1)
                    ins = nc.vector.tensor_reduce(part_max[:, s % 2, j:j + 1], PS[:, j, 0:KB], AX, ALU.max)
                    if j < NKB - 1:
                        ins.then_inc(dve_step, 1)
                        chain.count = chain.count + 1
                chain.link(dve, ins)
                wait_past(dve, m["exp"], NT * b + s, NT)
                nc.vector.tensor_reduce(neg_max[:, s:s + 1], part_max[:, s % 2, :], AX, ALU.max, negate=True)\
                    .then_inc(m["mx"], 1)

            def copy_chunk(b, g, k):
                at = 2 * NC * b + NC * g + k
                dve.wait_ge(m["tr"], at + 1)
                wait_past(dve, m["pv"], at, 3)
                n = 128 * (GA, GB)[g]
                nc.vector.tensor_copy(pT[k % 3][0:KC, 0:n], PS[0:KC, 3 + k % 2, 0:n]).then_inc(m["trc"], 1)

            def reciprocals(b, g):
                lo, size = (0, GA) if g == 0 else (GA, GB)
                dve.wait_ge(m["exp"], NT * b + lo + size)
                chain.link(dve, nc.vector.reciprocal(row_inv[:, lo:lo + size], row_sum[:, lo:lo + size]))
                wait_past(dve, m["inv"], 2 * b + g, 2)
                nc.vector.tensor_tensor(
                    inv_diag[g][:, 0:size, :],
                    ident[:, :].rearrange("p (a c) -> p a c", a=1).broadcast_to([128, size, 128]),
                    row_inv[:, lo:lo + size].rearrange("p (j a) -> p j a", a=1).broadcast_to([128, size, 128]),
                    ALU.mult).then_inc(m["idiag"], 1)

            def scale_out(b, g):
                lo, size = (0, GA) if g == 0 else (GA, GB)
                dve.wait_ge(m["invc"], 2 * b + g + 1)
                dve.wait_ge(m["pv"], 2 * NC * b + NC * g + NC)
                nc.vector.tensor_tensor(
                    QO_flat[:, bass.ds(b * HQ + lo * 128, 128 * size)], PS[:, 5 + g, 0:128 * size],
                    inv_cols[:, 0:128 * size], ALU.mult).then_inc(m["norm"], 1)

            def chunk(b, g, k, first):
                copy_chunk(b, g, k)
                if k == 1 and not first:
                    scale_out(*((b, 0) if g else (b - 1, 1)))
                if k == NC - 1:
                    reciprocals(b, g)

            def batch(b, par):
                first = isinstance(b, int) and b == 0
                last = isinstance(b, int) and b == B - 1
                for s in range(NT):
                    maxima(b, s)
                    if s < GA and not first:
                        for k in range(3 * s, 3 * s + 3):
                            chunk(b - 1, 1, k, False)
                    if s >= GA:
                        for k in range(4 * (s - GA), 4 * (s - GA) + 4):
                            chunk(b, 0, k, first)
                    if l == 1 and not last and s > 3:
                        values(b + 1, 1 - par, s - 4)

            if l == 1:
                for piece in range(3):
                    values(0, 0, piece)
            batch(0, 0)
            per_batch = 3 * NT + 2
            start = chain.count
            with dve.Fori(1, B - 2, 2) as i:
                chain.count = (i - 1) * per_batch + start
                batch(i, 1)
                batch(i + 1, 0)
            chain.count = start + per_batch * (B - 2)
            batch(B - 1, 1)
            for k in range(NC):
                chunk(B - 1, 1, k, False)
            scale_out(B - 1, 1)
            dve.wait_ge(m["out"], 1)
            bias = xa_bias[:, 4:5] if l == 0 else xa_bias[:, 3:4]
            nc.vector.scalar_tensor_tensor(halves(X[:, :]), two(0), bias, halves(X[:, :]), ALU.add, ALU.add)\
                .then_inc(x_ready, 1)

        def experts_tensor(pe, l, n):
            m = ff[l]
            ng = E if l == 0 else WCOLS
            pe.wait_ge(xn_ready, n + 1)
            if l == 0:
                pe.wait_ge(ld_ffn, 16 * FFN_LOADS)
            for b in range(B):
                mm = nc.tensor.matmul(PS[0:S, 6, b * ng:(b + 1) * ng], XN[:, b * S:(b + 1) * S],
                                      gate_w[l][:, 0:ng], start=True, stop=True)
            mm.then_inc(m["logit"], 1)
            pe.wait_ge(m["gates"], 1)
            nc.tensor.transpose(PS[:, 7, 0:S], routed[:, :, :].rearrange("p b e -> p (b e)"),
                                ident[0:S, 0:S]).then_inc(m["gtr"], 1)
            pe.wait_ge(m["blk"], 1)
            if l == 1:
                for a in range(2):
                    mm = nc.tensor.matmul(PS[:, 4 + a, 0:HALF], b2[:, :],
                                          w_blk[:, a * HB:(a + 1) * HB, :], start=True, stop=True)
                mm.then_inc(m["b2mm"], 1)

            def expert(e, par):
                pe.wait_ge(ld_w[l][par], (e // 2 + 1) * 32 if isinstance(e, int) else (e - par) * 16 + 32)
                for f in range(NF):
                    p = f % 2
                    wait_past(pe, m["hact"], NF * e + f, 2)
                    for a in range(2):
                        mm = nc.tensor.matmul(PS[:, 2 * p + a, 0:HALF], w1[par][:, f * 128:(f + 1) * 128],
                                              XN[:, a * HALF:(a + 1) * HALF], start=True, stop=True)
                    mm.then_inc(m["h"], 1)
                pe.wait_ge(m["wsel"], e + 1)
                wait_past(pe, m["wcols"], e, 1)
                for a in range(2):
                    mm = nc.tensor.matmul(PS[:, 6 + a, 0:HALF], ones[:, :],
                                          w_blk_e[:, par, a * HALF:(a + 1) * HALF], start=True, stop=True)
                mm.then_inc(m["wmm"], 1)
                if isinstance(e, int) and e == 0:
                    if l == 1:
                        pe.wait_ge(m["ymul"], 1)
                else:
                    pe.wait_ge(m["ymul"], e + l)
                for f in range(NF):
                    pe.wait_ge(m["hact"], NF * e + f + 1)
                    for a in range(2):
                        mm = nc.tensor.matmul(PS[:, 4 + a, 0:HALF], w2[par][:, f, :],
                                              hidden[:, f, a * HALF:(a + 1) * HALF],
                                              start=f == 0, stop=f == NF - 1)
                mm.then_inc(m["y"], 1)

            expert(0, 0)
            expert(1, 1)
            with pe.Fori(2, E - 1, 2) as i:
                expert(i, 0)
                expert(i + 1, 1)

        def experts_sync(sp, l):
            m = ff[l]

            def load(e, par):
                wait_past(sp, m["y"], e, 2)
                w1s = t["L0_ffn_w1" if l == 0 else "L1_ffn_W1"]
                w2s = t["L0_ffn_w2" if l == 0 else "L1_ffn_W2"]
                sp.dma_start(w1[par][:, :], w1s[bass.ds(e, 1), :, :].rearrange("a c f -> (a c) f"))\
                    .then_inc(ld_w[l][par], 16)
                sp.dma_start(w2[par][:, :, :], w2s[bass.ds(e, 1), :, :].rearrange("a (g p) d -> (a p) g d", p=128))\
                    .then_inc(ld_w[l][par], 16)

            if l == 1:
                sp.wait_ge(ff[0]["y"], E)
            load(0, 0)
            load(1, 1)
            with sp.Fori(2, E - 1, 2) as i:
                load(i, 0)
                load(i + 1, 1)

        def experts_scalar(act, l):
            m = ff[l]
            func = ACT.Gelu if l == 0 else ACT.Gelu_apprx_tanh
            act.wait_ge(m["gsub"], 1)
            ins = nc.scalar.activation(gate[:, :, 0:E], gate[:, :, 0:E], ACT.Exp)
            if l == 1:
                ins = nc.scalar.activation(gate[:, :, E:WCOLS], gate[:, :, E:WCOLS], ACT.Exp, scale=-1.0)
            ins.then_inc(m["gexp"], 1)

            def expert(e, par):
                for f in range(NF):
                    act.wait_ge(m["h"], NF * e + f + 1)
                    if f == 0:
                        wait_past(act, m["y"], e, 1)
                    bias = b1[:, l, bass.ds(e * NF + f, 1)]
                    nc.scalar.activation(halves(hidden[:, f, :]), two(2 * (f % 2)), func, bias=bias)\
                        .then_inc(m["hact"], 1)
                act.wait_ge(m["wmm"], e + 1)
                wait_past(act, m["ymul"], e + l, 2 + l)
                nc.scalar.activation(halves(w_cols[:, par, :]), two(6), ACT.Copy).then_inc(m["wcols"], 1)

            expert(0, 0)
            expert(1, 1)
            with act.Fori(2, E - 1, 2) as i:
                expert(i, 0)
                expert(i + 1, 1)

        def experts_vector(dve, l, chain):
            m = ff[l]
            ng = E if l == 0 else WCOLS
            G = gate[:, :, 0:E]

            def per_batch(x):
                return x.rearrange("p (b a) -> p b a", a=1).broadcast_to([S, B, E])

            st = [gate_stat[:, k, :] for k in range(4)]
            dve.wait_ge(m["logit"], 1)
            logits = PS[0:S, 6, 0:B * ng].rearrange("p (b e) -> p b e", b=B)
            if l == 0:
                chain.link(dve, nc.vector.tensor_copy(G, logits))
            else:
                chain.link(dve, nc.vector.tensor_tensor(
                    gate[:, :, :], logits,
                    gate_b[:, :].rearrange("p (a e) -> p a e", a=1).broadcast_to([S, B, WCOLS]), ALU.add))
            chain.link(dve, nc.vector.tensor_reduce(st[0], G, AX, ALU.max))
            nc.vector.tensor_tensor(G, G, per_batch(st[0]), ALU.subtract).then_inc(m["gsub"], 1)
            dve.wait_ge(m["gexp"], 1)
            chain.link(dve, nc.vector.tensor_reduce(st[1], G, AX, ALU.add))
            chain.link(dve, nc.vector.reciprocal(st[2], st[1]))
            if l == 0:
                nc.vector.tensor_tensor(routed[:, :, :], G, per_batch(st[2]), ALU.mult).then_inc(m["gates"], 1)
            else:
                chain.link(dve, nc.vector.tensor_tensor(gate2[:, :, :], G, per_batch(st[2]), ALU.mult))
                z = gate[:, :, E]
                chain.link(dve, nc.vector.tensor_scalar(st[0], z, 1.0, None, ALU.add))
                chain.link(dve, nc.vector.reciprocal(st[1], st[0]))
                chain.link(dve, nc.vector.tensor_scalar(st[0], st[1], THRESHOLD, None, ALU.mult))
                chain.link(dve, nc.vector.tensor_tensor(gate2[:, :, :], gate2[:, :, :], per_batch(st[0]),
                                                        ALU.subtract))
                chain.link(dve, nc.vector.tensor_scalar(gate2[:, :, :], gate2[:, :, :], 0.0, None, ALU.max))
                chain.link(dve, nc.vector.tensor_reduce(st[1], gate2[:, :, :], AX, ALU.add))
                chain.link(dve, nc.vector.tensor_scalar(st[2], st[1], 0.0, None, ALU.is_equal))
                chain.link(dve, nc.vector.tensor_tensor(st[3], st[1], st[2], ALU.add))
                chain.link(dve, nc.vector.reciprocal(st[0], st[3]))
                nc.vector.tensor_tensor(routed[:, :, :], gate2[:, :, :], per_batch(st[0]), ALU.mult)\
                    .then_inc(m["gates"], 1)
            dve.wait_ge(m["gtr"], 1)
            if l == 0:
                rest = CAP - 8
                chain.link(dve, nc.vector.memset(work[:, :], 2.0))
                chain.link(dve, nc.vector.tensor_copy(gT[:, :], PS[:, 7, 0:S]))
                chain.link(dve, nc.vector.tensor_copy(work[:, 0:S], gT[:, :]))
                chain.link(dve, nc.vector.max(top8[:, 0, :], work[:, 0:S]))
                chain.link(dve, nc.vector.match_replace(work2[:, 0:S], top8[:, 0, :], work[:, 0:S], -1.0))
                chain.link(dve, nc.vector.tensor_copy(work2[:, S:64], work[:, S:64]))
                chain.link(dve, nc.vector.max(top8[:, 1, :], work2[:, 0:S]))
                chain.link(dve, nc.vector.memset(top8[:, 1, rest:8], 2.0))
                chain.link(dve, nc.vector.match_replace(work[:, :], top8[:, 1, :], work2[:, :], -1.0))
                chain.link(dve, nc.vector.tensor_scalar(work[:, 0:S], work[:, 0:S], -1.0, None, ALU.is_equal))
                chain.link(dve, nc.vector.tensor_tensor(w_be[:, :], gT[:, :], work[:, 0:S], ALU.mult))
            else:
                chain.link(dve, nc.vector.tensor_copy(w_be[:, :], PS[:, 7, 0:S]))
            ins = nc.vector.tensor_tensor(
                w_blk[:, :, :], w_be[:, :].rearrange("p (a s) -> p a s", a=1).broadcast_to([128, B, S]),
                batch_mask[:, :].rearrange("p (b a) -> p b a", a=1).broadcast_to([128, B, S]), ALU.mult)
            ins.then_inc(m["blk"], 1)
            dve.wait_ge(m["blk"], 1)

            def select(e, par):
                wait_past(dve, m["wmm"], e, 2)
                nc.vector.tensor_scalar(w_blk_e[:, par, :], w_blk[:, :, :].rearrange("p b s -> p (b s)"),
                                        expert_mask[:, bass.ds(e, 1)], None, ALU.mult).then_inc(m["wsel"], 1)

            if l == 1:
                dve.wait_ge(m["b2mm"], 1)
                nc.vector.tensor_tensor(halves(X[:, :]), halves(X[:, :]), two(4), ALU.add).then_inc(m["ymul"], 1)
            select(0, 0)
            start = chain.count

            def expert(e, par, final=False):
                if not final:
                    select(e + 1, 1 - par)
                dve.wait_ge(m["y"], e + 1)
                dve.wait_ge(m["wcols"], e + 1)
                ins = nc.vector.tensor_tensor(halves(XC[:, :]), two(4), halves(w_cols[:, par, :]), ALU.mult)
                ins.then_inc(m["ymul"], 1)
                dve.wait_ge(m["ymul"], e + 1 + l)
                ins = nc.vector.tensor_tensor(X[:, :], X[:, :], XC[:, :], ALU.add)
                if final:
                    ins.then_inc(x_ready, 1)
                else:
                    chain.link(dve, ins)

            expert(0, 0)
            with dve.Fori(1, E - 2, 2) as i:
                chain.count = i + start
                expert(i, 1)
                expert(i + 1, 0)
            chain.count = start + E - 1
            expert(E - 1, 1, final=True)

        block = ctx.enter_context(nc.Block())

        @block.sync
        def _(sp):
            sp.dma_start(X[:, :], t["x_T"]).then_inc(ld_x, 16)
            for w, name in enumerate(("xa0_qT", "xa0_kT", "xa0_vT", "L0_xattn_W_out")):
                sp.dma_start(fold_in[:, w, :, :], t[name].rearrange("(g p) c -> p g c", p=128))\
                    .then_inc(ld_fold, 16)
            for w, name in enumerate(("sa0_q", "sa0_k", "sa0_v", "sa0_o")):
                sp.dma_start(sa_w[0][:, w, :], t[name]).then_inc(ld_sa, 16)
            for w, name in enumerate(("sa1_q", "sa1_k", "sa1_v", "sa1_o")):
                sp.dma_start(sa_w[1][:, w, :], t[name]).then_inc(ld_sa, 16)
            sp.wait_ge(consts_set, 2)
            sp.dma_start(prob[0][0:S, 0, :], t["fside_SxS2_0"]).then_inc(ld_bias, 16)
            sp.dma_start(prob[0][64:64 + S, 0, :], t["fside_SxS2_0"]).then_inc(ld_bias, 16)
            cross_sync(sp, 0)
            experts_sync(sp, 0)
            cross_sync(sp, 1)
            experts_sync(sp, 1)
            sp.wait_ge(x_ready, 6)
            sp.dma_start(out, X[:, :]).then_inc(out_done, 16)
            sp.wait_ge(out_done, 16)

        @block.gpsimd
        def _(pool):
            pool.wait_ge(ld_const, 16 * CONST_LOADS)
            self_gpsimd(pool, 0)
            cross_gpsimd(pool, 0)
            self_gpsimd(pool, 1)
            cross_gpsimd(pool, 1)

        @block.scalar
        def _(act):
            act.dma_start(ident[:, :], t["ident"]).then_inc(ld_const, 16)
            act.dma_start(head_mask[:, :], t["head_mask"]).then_inc(ld_const, 16)
            act.dma_start(rope[:, :, :], t["rope"]).then_inc(ld_const, 16)
            act.dma_start(bias_sel[:, :], t["bias_sel"]).then_inc(ld_const, 16)
            act.dma_start(batch_mask[:, :], t["batch_mask"]).then_inc(ld_const, 16)
            act.dma_start(expert_mask[:, :], t["expert_mask"]).then_inc(ld_const, 16)
            act.dma_start(gate_w[0][:, 0:E], t["L0_ffn_gate_w"]).then_inc(ld_ffn, 16)
            act.dma_start(gate_w[1][:, 0:E], t["L1_ffn_Wg"]).then_inc(ld_ffn, 16)
            act.dma_start(gate_w[1][:, E:WCOLS], t["L1_ffn_Wt"]).then_inc(ld_ffn, 16)
            act.dma_start(gate_b[:, 0:E], t["L1_ffn_bg"].broadcast_to([S, E])).then_inc(ld_ffn, 16)
            act.dma_start(gate_b[:, E:WCOLS], t["L1_ffn_bt"].broadcast_to([S, 1])).then_inc(ld_ffn, 16)
            act.dma_start(b1[:, 1, :], t["b1_cols"]).then_inc(ld_ffn, 16)
            for b in range(B):
                act.dma_start(b2[b * E:(b + 1) * E, :], t["L1_ffn_b2"]).then_inc(ld_ffn, 16)
            for w, name in enumerate(("L1_attn_wq_b", "L1_attn_wk_b")):
                act.dma_start(sa_bias[:, w:w + 1], t[name]).then_inc(ld_sa, 16)
            act.dma_start(sa_bias[:, 3:4], t["L1_attn_wo_b"]).then_inc(ld_sa, 16)
            act.dma_start(sa_bv[:, :], t["sa_bv"].broadcast_to([128, D])).then_inc(ld_sa, 16)
            for w, name in enumerate(("xa1_q", "xa1_k", "xa1_v", "xa1_o")):
                act.dma_start(xa_w[:, w, :], t[name]).then_inc(ld_xa, 16)
            for w, name in ((0, "L1_xattn_b_q"), (1, "L1_xattn_b_k"), (3, "L1_xattn_b_o"),
                            (4, "L0_xattn_b_out")):
                act.dma_start(xa_bias[:, w:w + 1], t[name]).then_inc(ld_xa, 16)
            act.dma_start(xa_bv[:, :], t["xa_bv"].broadcast_to([128, D])).then_inc(ld_xa, 16)
            act.wait_ge(consts_set, 1)
            fold_scalar(act)
            norm_scalar(act, 0)
            self_scalar(act, 0)
            norm_scalar(act, 1)
            cross_scalar(act, 0)
            norm_scalar(act, 2)
            act.wait_ge(ld_ffn, 16 * FFN_LOADS)
            experts_scalar(act, 0)
            norm_scalar(act, 3)
            self_scalar(act, 1)
            norm_scalar(act, 4)
            act.wait_ge(ld_xa, 16 * XA_LOADS)
            cross_scalar(act, 1)
            norm_scalar(act, 5)
            experts_scalar(act, 1)

        @block.tensor
        def _(pe):
            pe.wait_ge(ld_const, 16 * CONST_LOADS)
            fold_tensor(pe)
            norm_tensor(pe, 0)
            self_tensor(pe, 0, 0)
            norm_tensor(pe, 1)
            cross_tensor(pe, 0, 1)
            norm_tensor(pe, 2)
            experts_tensor(pe, 0, 2)
            norm_tensor(pe, 3)
            self_tensor(pe, 1, 3)
            norm_tensor(pe, 4)
            cross_tensor(pe, 1, 4)
            norm_tensor(pe, 5)
            experts_tensor(pe, 1, 5)

        @block.vector
        def _(dve):
            chain = Chain()
            nc.vector.memset(b1[:, 0, :], 0.0)
            nc.vector.memset(ones[:, :], 1.0)
            nc.vector.memset(mean_w[:, :], 1.0 / D)
            nc.vector.memset(eps[:, :], EPS).then_inc(consts_set, 1)
            nc.vector.memset(prob[0][:, 0, :], 0.0).then_inc(consts_set, 1)
            dve.wait_ge(ld_x, 16)
            norm_vector(dve, 0, chain)
            dve.wait_ge(ld_sa, 16 * SA_LOADS)
            self_vector(dve, 0, chain)
            bias_vector(dve, chain)
            norm_vector(dve, 1, chain)
            dve.wait_ge(ld_xa, 16 * XA_LOADS)
            cross_vector(dve, 0, chain)
            norm_vector(dve, 2, chain)
            dve.wait_ge(ld_ffn, 16 * FFN_LOADS)
            experts_vector(dve, 0, chain)
            norm_vector(dve, 3, chain)
            self_vector(dve, 1, chain)
            norm_vector(dve, 4, chain)
            cross_vector(dve, 1, chain)
            norm_vector(dve, 5, chain)
            experts_vector(dve, 1, chain)


def kernel(**inputs):
    import concourse.bacc as bacc
    from concourse.bass_utils import run_bass_kernel_spmd
    import ml_dtypes

    x = {k: np.asarray(v) for k, v in inputs.items()}
    ch = np.arange(D)
    circ = (ch[None, :] - ch[:, None]) % D
    even = ch - ch % 2
    arrays = {
        "x_T": x["x"].transpose(2, 0, 1).reshape(D, NTOK),
        "ctx_1024": x["ctx_1024"],
        "ctx_T": x["ctx_1024"].transpose(0, 2, 1),
        "fside_SxS2_0": x["fside_SxS2_0"],
        "sa0_q": x["L0_attn_Wq"].T[:, even], "sa0_k": x["L0_attn_Wk"].T[:, even],
        "sa0_v": x["L0_attn_Wv"].T, "sa0_o": x["L0_attn_Wo"].T,
        "sa1_q": x["L1_attn_wq_c"][circ], "sa1_k": x["L1_attn_wk_c"][circ],
        "sa1_v": x["L1_attn_wv_c"][circ], "sa1_o": x["L1_attn_wo_c"][circ],
        "xa0_qT": x["L0_xattn_W_q"].T, "xa0_kT": x["L0_xattn_W_k"].T, "xa0_vT": x["L0_xattn_W_v"].T,
        "xa1_q": x["L1_xattn_W_q"].T, "xa1_k": x["L1_xattn_W_k"].T,
        "xa1_v": x["L1_xattn_W_v"].T, "xa1_o": x["L1_xattn_W_o"].T,
        "sa_bv": x["L1_attn_wv_b"][None, :], "xa_bv": x["L1_xattn_b_v"][None, :],
        "L1_ffn_bg": x["L1_ffn_bg"][None, :], "L1_ffn_bt": x["L1_ffn_bt"][None, :],
        "b1_cols": x["L1_ffn_b1"].reshape(E * NF, 128).T,
    }
    for name in ("L0_xattn_W_out", "L0_ffn_gate_w", "L0_ffn_w1", "L0_ffn_w2", "L1_ffn_Wg", "L1_ffn_Wt",
                 "L1_ffn_W1", "L1_ffn_W2", "L1_ffn_b2"):
        arrays[name] = x[name]
    for name in ("L1_attn_wq_b", "L1_attn_wk_b", "L1_attn_wo_b", "L1_xattn_b_q", "L1_xattn_b_k",
                 "L1_xattn_b_o", "L0_xattn_b_out"):
        arrays[name] = x[name][:, None]

    pos = np.arange(S, dtype=np.float32)
    freqs = np.exp(np.arange(0, HD, 2, dtype=np.float32) * np.float32(-math.log(10000.0) / HD))
    angle = (pos[None, :] * freqs[(ch % HD) // 2][:, None]).astype(np.float32)
    table = np.where((ch % 2 == 0)[:, None], np.cos(angle), -np.sin(angle)).astype(np.float32)
    arrays["rope"] = np.stack([table * np.float32(HD ** -0.5), table], 1)
    arrays["ident"] = np.eye(128, dtype=np.float32)
    arrays["head_mask"] = (ch[:, None] // HD == np.arange(NH)[None, :]).astype(np.float32)
    arrays["batch_mask"] = (ch[:, None] // E == np.arange(B)[None, :]).astype(np.float32)
    arrays["expert_mask"] = (ch[:, None] % E == np.arange(E)[None, :]).astype(np.float32)
    row, col = np.arange(128)[:, None] % 64, np.arange(HQ)[None, :]
    arrays["bias_sel"] = np.where(row == col % S, 2.0 ** -(col // S + 1.0), 0.0).astype(ml_dtypes.bfloat16)
    arrays = {f"in_{k}": np.ascontiguousarray(v) for k, v in arrays.items()}

    nc = bacc.Bacc("TRN2", target_bir_lowering=False, num_devices=1)
    t = {k[3:]: nc.dram_tensor(k, a.shape, mybir.dt.from_np(a.dtype), kind="ExternalInput").ap()
         for k, a in arrays.items()}
    out = nc.dram_tensor("out_0", (D, NTOK), mybir.dt.float32, kind="ExternalOutput").ap()
    decoder_kernel(nc, t, out)
    r = run_bass_kernel_spmd(nc, [arrays], core_ids=[0])
    y = r.results[0]["out_0"]
    return y.reshape(D, B, S).transpose(1, 2, 0)
```

```python
import math

import numpy as np

import concourse.bass as bass
from concourse import mybir
from contextlib import ExitStack

B, S, D = 16, 56, 128
NTOK = B * S
HALF = NTOK // 2
HB = B // 2
NH = 16
HQ = NH * S
NT = HQ // 128
HD = D // NH
XD = 64
S2 = 1500
KC = 125
NC = S2 // KC
KB = 500
NKB = S2 // KB
E = 8
FF = 512
NF = FF // 128
CAP = 2 * S // E
EPS = 1e-5
THRESHOLD = 0.125
GA, GB = 4, 3
QCOLS = (128, 96)
WCOLS = E + 1
HL_COLS = 4 * S2 + 4 * HQ + 2 * NC * 128 + 6 * 512 + S2 + HQ
CONST_LOADS = 6
SA_LOADS, XA_LOADS, FFN_LOADS = 12, 9, 6 + B


def decoder_kernel(nc, t, out):
    fp32, fp32r = mybir.dt.float32, mybir.dt.float32r
    ALU, ACT, AX = mybir.AluOpType, mybir.ActivationFunctionType, mybir.AxisListType.X

    ctx = ExitStack()
    with ctx:
        def sb(name, shape, dt=fp32):
            return ctx.enter_context(nc.sbuf_tensor(name, shape, dt))

        def sem(name):
            return ctx.enter_context(nc.semaphore(name))

        ident = sb("ident", [128, 128])
        ones = sb("ones", [128, 128])
        mean_w = sb("mean_w", [128, 128])
        eps = sb("eps", [128, 1])
        head_mask = sb("head_mask", [128, NH])
        batch_mask = sb("batch_mask", [128, B])
        expert_mask = sb("expert_mask", [128, E])
        rope = sb("rope", [128, 2, S])
        quad_mask = sb("quad_mask", [128, 4])
        sa_w = [sb(f"sa_w{l}", [128, 4, 128]) for l in range(2)]
        sa_bias = sb("sa_bias", [128, 4])
        sa_bv = sb("sa_bv", [128, D])
        vo_fold = sb("vo_fold", [128, NH, 128])
        xa_w = sb("xa_w", [128, 4, 128])
        xa_bias = sb("xa_bias", [128, 5])
        xa_bv = sb("xa_bv", [128, D])
        gate_w = [sb(f"gate_w{l}", [128, WCOLS]) for l in range(2)]
        gate_b = sb("gate_b", [S, WCOLS])
        b1 = sb("b1", [128, 2, E * NF])
        b2 = sb("b2", [128, D])
        X = sb("X", [128, NTOK])
        sm_stat = sb("sm_stat", [128, 2, 4, NT])
        QO = sb("QO", [128, B, HQ])
        ctxT = sb("ctxT", [128, S2])
        ctxV = sb("ctxV", [128, NC, 128])
        prob = [sb("prob_a", [128, GA, S2]), sb("prob_b", [128, GB, S2])]
        part_max = sb("part_max", [128, 2, NKB])
        neg_max = sb("neg_max", [128, NT])
        part_sum = sb("part_sum", [128, NT, NKB])
        row_sum = sb("row_sum", [128, NT])
        row_inv = sb("row_inv", [128, NT])
        inv_diag = [sb(f"inv_diag{i}", [128, 4, 128]) for i in range(2)]
        inv_cols = sb("inv_cols", [128, 512])
        HL = sb("HL", [128, HL_COLS], fp32r)
        hl_taken = [0]

        def halved(rows, cols):
            at = hl_taken[0]
            hl_taken[0] += cols
            assert hl_taken[0] <= HL_COLS, hl_taken
            return HL[0:rows, at:at + cols]

        kH, kL, qH, qL = ([halved(128, n) for i in range(2)] for n in (S2, S2, HQ, HQ))
        vH, vL = (halved(128, NC * 128).rearrange("p (c d) -> p c d", c=NC) for i in range(2))
        pH, pL = ([halved(128, 512) for i in range(3)] for i in range(2))
        bias_rows = halved(128, S2)
        bias_sel = halved(128, HQ)
        w1 = [ctxT[:, i * FF:(i + 1) * FF] for i in range(2)]
        w2 = [ctxV[:, i * NF:(i + 1) * NF, :] for i in range(2)]
        k_now = ctxV[:, :, :].rearrange("p c d -> p (c d)")[:, 0:S2]
        hidden = prob[0][:, :, 0:NTOK]
        QO_flat = QO[:, :, :].rearrange("p b q -> p (b q)")
        taken = [0]

        def carve(rows, cols):
            at = taken[0]
            taken[0] += cols
            assert taken[0] <= B * HQ
            return QO_flat[0:rows, at:at + cols]

        q_all = carve(128, NTOK)
        out_q = carve(128, B * 4 * S)
        q_diag1 = carve(128, HQ)
        vals = [carve(128, NC * 128).rearrange("p (c d) -> p c d", c=NC) for i in range(2)]
        pT = [carve(128, 512) for i in range(3)]
        taken = [NTOK]
        q_diag = [carve(128, HQ) for i in range(2)]
        k_all = carve(128, NTOK)
        att = carve(128, B * 4 * S)
        wo_quad = carve(128, 4 * 128).rearrange("p (r o) -> p r o", r=4)
        v_flat = carve(S, B * D)
        v_all = v_flat.rearrange("p (b d) -> p b d", b=B)
        v_now = [carve(S, D) for i in range(2)]
        sm_d = [carve(128, NT * S).rearrange("p (j s) -> p j s", j=NT) for i in range(2)]
        sm_p = [carve(128, NT * S + 128 - S) for i in range(2)]
        sm_pT = [carve(S, HQ) for i in range(2)]
        taken = [0]
        w_blk = carve(128, NTOK).rearrange("p (b s) -> p b s", b=B)
        w_blk_e = carve(128, 2 * NTOK).rearrange("p (a s) -> p a s", a=2)
        w_cols = carve(128, 2 * NTOK).rearrange("p (a s) -> p a s", a=2)
        gate = carve(S, B * WCOLS).rearrange("p (b e) -> p b e", b=B)
        gate2 = carve(S, B * E).rearrange("p (b e) -> p b e", b=B)
        routed = carve(S, B * E).rearrange("p (b e) -> p b e", b=B)
        gate_stat = carve(S, 4 * B).rearrange("p (k b) -> p k b", k=4)
        gT = carve(128, S)
        work, work2 = carve(128, 64), carve(128, 64)
        top8 = carve(128, 16).rearrange("p (r t) -> p r t", r=2)
        w_be = carve(128, S)
        prob0, prob1 = (prob[g][:, :, :].rearrange("p j n -> p (j n)") for g in range(2))
        XC, SQ, XN = (prob1[:, i * NTOK:(i + 1) * NTOK] for i in range(3))
        qk_fold = prob0[:, 2 * S2:2 * S2 + NH * 128].rearrange("p (h c) -> p h c", h=NH)
        fold_in = prob[1][:, :, :].rearrange("p j n -> p (j n)")[:, 0:4 * 8 * 128]\
            .rearrange("p (w g c) -> p w g c", w=4, g=8)

        PS = ctx.enter_context(nc.psum_tensor("PS", [128, 8, 512], fp32))
        PSF = PS[:, :, :].rearrange("p a b -> p (a b)")

        def two(bank):
            return PS[:, bank:bank + 2, 0:HALF]

        def halves(x):
            return x.rearrange("p (a b) -> p a b", a=2)

        ld_x, ld_const, ld_sa, ld_fold, ld_xa, ld_ffn, ld_bias = (
            sem(n) for n in ("ld_x", "ld_const", "ld_sa", "ld_fold", "ld_xa", "ld_ffn", "ld_bias"))
        out_done = sem("out_done")
        consts_set = sem("consts_set")
        x_ready = sem("x_ready")
        ln_mean, ln_centred, ln_squared, ln_var, ln_std, xn_ready = (
            sem(n) for n in ("ln_mean", "ln_centred", "ln_squared", "ln_var", "ln_std", "xn_ready"))
        dve_step = sem("dve_step")
        pool_step = sem("pool_step")
        pool_count = [0]
        names = ("q k v qkv diag wo scores sub exp norm tr vnow trc pv att out").split()
        sa = [{n: sem(f"sa{l}_{n}") for n in names} for l in range(2)]
        fold_mm, fold_ev = sem("fold_mm"), sem("fold_ev")
        bias_split = sem("bias_split")
        names = ("q diag scores mx exp tr trc pv idiag inv invc norm out "
                 "qh trh tra kspl vspl kmm kev vmm vev vo qp qpa qpd").split()
        xa = [{n: sem(f"xa{l}_{n}") for n in names} for l in range(2)]
        ld_k = [sem(f"ld_k{l}") for l in range(2)]
        ld_v = sem("ld_v")
        names = ("logit gexp gsub gates gtr blk wsel wmm wcols h hact y ymul b2mm").split()
        ff = [{n: sem(f"ff{l}_{n}") for n in names} for l in range(2)]
        ld_w = [[sem(f"ld_w{l}{i}") for i in range(2)] for l in range(2)]

        class Chain:
            def __init__(self):
                self.count = 0

            def link(self, eng, ins):
                ins.then_inc(dve_step, 1)
                self.count = self.count + 1
                eng.wait_ge(dve_step, self.count)

        def norm_tensor(pe, n):
            if n == 0:
                pe.wait_ge(ld_x, 16)
                pe.wait_ge(fold_ev, 8)
                pe.wait_ge(consts_set, 1)
            else:
                pe.wait_ge(x_ready, n)
            for h in range(2):
                mm = nc.tensor.matmul(PS[:, h, 0:HALF], mean_w[:, :], X[:, h * HALF:(h + 1) * HALF],
                                      start=True, stop=True)
            mm.then_inc(ln_mean, 1)
            pe.wait_ge(ln_squared, n + 1)
            for h in range(2):
                mm = nc.tensor.matmul(PS[:, 2 + h, 0:HALF], mean_w[:, :], SQ[:, h * HALF:(h + 1) * HALF],
                                      start=True, stop=True)
            mm.then_inc(ln_var, 1)

        def norm_scalar(act, n):
            act.wait_ge(ln_centred, n + 1)
            nc.scalar.activation(SQ[:, :], XC[:, :], ACT.Square).then_inc(ln_squared, 1)
            act.wait_ge(ln_var, n + 1)
            nc.scalar.activation(halves(SQ[:, :]), two(2), ACT.Sqrt, bias=eps[:, 0:1]).then_inc(ln_std, 1)

        def norm_vector(dve, n, chain):
            dve.wait_ge(ln_mean, n + 1)
            nc.vector.tensor_tensor(halves(XC[:, :]), halves(X[:, :]), two(0), ALU.subtract)\
                .then_inc(ln_centred, 1)
            dve.wait_ge(ln_std, n + 1)
            chain.link(dve, nc.vector.reciprocal(SQ[:, :], SQ[:, :]))
            nc.vector.tensor_tensor(XN[:, :], XC[:, :], SQ[:, :], ALU.mult).then_inc(xn_ready, 1)

        def wait_past(eng, signal, b, back):
            if not isinstance(b, int) or b >= back:
                eng.wait_ge(signal, b - (back - 1))

        def live(b):
            return not isinstance(b, int) or 0 <= b < B

        def rounds(eng, step):
            for i in range(4):
                step(i, i % 2)
            with eng.Fori(4, B - 3, 2) as i:
                step(i, 0)
                step(i + 1, 1)
            for i in range(B - 2, B + 2):
                step(i, i % 2)

        def self_tensor(pe, l, n):
            m = sa[l]
            if l == 0:
                pe.wait_ge(ld_sa, 16 * SA_LOADS)
            pe.wait_ge(xn_ready, n + 1)
            for w in range(2):
                for h in range(2):
                    mm = nc.tensor.matmul(PS[:, 2 * w + h, 0:HALF], sa_w[l][:, w, :],
                                          XN[:, h * HALF:(h + 1) * HALF], start=True, stop=True)
                mm.then_inc(m["q"], 1)
            for b in range(B):
                mm = nc.tensor.matmul(PS[0:S, 4 + b // 4, (b % 4) * 128:(b % 4 + 1) * 128],
                                      XN[:, b * S:(b + 1) * S], sa_w[l][:, 2, :], start=True, stop=True)
            mm.then_inc(m["v"], 1)
            pe.wait_ge(m["qkv"], 3)

            def scores(b, p):
                wait_past(pe, m["sub"], b, 2)
                pe.wait_ge(m["diag"], b + 1)
                for j in range(NT):
                    mm = nc.tensor.matmul(PS[:, p, j * S:(j + 1) * S], q_diag[p][:, j * 128:(j + 1) * 128],
                                          k_all[:, bass.ds(b * S, S)], start=True, stop=True)
                mm.then_inc(m["scores"], 1)

            def turn(b, p):
                pe.wait_ge(m["norm"], b + 1)
                base = (2 + 2 * p) * 512
                for j in range(NT):
                    mm = nc.tensor.transpose(PSF[:, base + j * 128:base + (j + 1) * 128],
                                             sm_p[p][:, j * S:j * S + 128], ident[:, :])
                mm.then_inc(m["tr"], 1)

            def await_values(b):
                pe.wait_ge(m["vnow"], b + 1)
                pe.wait_ge(m["trc"], b + 1)
                wait_past(pe, m["att"], b, 2)

            def values(b, p):
                for j in range(4):
                    r = slice(32 * j, 32 * j + 32)
                    mm = nc.tensor.matmul(PS[r, 6 + p, 0:4 * S], v_now[p][:, r],
                                          sm_pT[p][:, j * 4 * S:(j + 1) * 4 * S], start=True, stop=True)
                mm.then_inc(m["pv"], 1)

            scores(0, 0)
            scores(1, 1)

            def step(i, p):
                if live(i + 2):
                    scores(i + 2, p)
                if live(i - 2):
                    await_values(i - 2)
                if live(i - 1):
                    turn(i - 1, 1 - p)
                if live(i - 2):
                    values(i - 2, p)

            rounds(pe, step)
            pe.wait_ge(m["att"], B)
            pe.wait_ge(m["wo"], 1)
            for r in range(4):
                for a in range(2):
                    x = att.rearrange("p (b q) -> p b q", b=B)[:, a * HB:(a + 1) * HB, r * S:(r + 1) * S]
                    mm = nc.tensor.matmul(PS[:, a, 0:HALF], wo_quad[:, r, :], x, start=r == 0, stop=r == 3)
            mm.then_inc(m["out"], 1)

        def self_gpsimd(pool, l):
            m = sa[l]

            def diagonal(b, p):
                wait_past(pool, m["scores"], b, 2)
                q = q_all[:, bass.ds(b * S, S)].rearrange("p (a q) -> p a q", a=1)
                nc.gpsimd.tensor_tensor(
                    q_diag[p][:, :].rearrange("p (h q) -> p h q", h=NH), q.broadcast_to([128, NH, S]),
                    head_mask[:, :].rearrange("p (h a) -> p h a", a=1).broadcast_to([128, NH, S]),
                    ALU.mult).then_inc(m["diag"], 1)

            pool.wait_ge(m["qkv"], 1)
            diagonal(0, 0)
            diagonal(1, 1)
            pool.wait_ge(ld_sa, 16 * SA_LOADS)
            pool.wait_ge(m["qkv"], 3)
            nc.gpsimd.tensor_tensor(
                wo_quad,
                sa_w[l][:, 3, :].rearrange("p (a o) -> p a o", a=1).broadcast_to([128, 4, 128]),
                quad_mask[:, :].rearrange("p (h a) -> p h a", a=1).broadcast_to([128, 4, 128]),
                ALU.mult).then_inc(m["wo"], 1)
            with pool.Fori(2, B - 1, 2) as i:
                for k in range(2):
                    diagonal(i + k, k)

        def self_scalar(act, l):
            m = sa[l]

            def exps(b, p):
                act.wait_ge(m["sub"], b + 1)
                wait_past(act, m["norm"], b, 2)
                nc.scalar.activation(sm_d[p][:, :, :], sm_d[p][:, :, :], ACT.Exp).then_inc(m["exp"], 1)

            def copy_probs(b, p):
                act.wait_ge(m["tr"], b + 1)
                wait_past(act, m["pv"], b, 2)
                base = (2 + 2 * p) * 512
                nc.scalar.activation(sm_pT[p][:, 0:HQ], PSF[0:S, base:base + HQ], ACT.Copy).then_inc(m["trc"], 1)

            def take_values(b, p):
                wait_past(act, m["pv"], b, 2)
                nc.scalar.activation(v_now[p][:, :], v_flat[:, bass.ds(b * D, D)], ACT.Copy).then_inc(m["vnow"], 1)

            def copy_out(b, p):
                act.wait_ge(m["pv"], b + 1)
                nc.scalar.activation(att[:, bass.ds(b * 4 * S, 4 * S)], PS[:, 6 + p, 0:4 * S], ACT.Copy)\
                    .then_inc(m["att"], 1)

            act.wait_ge(m["qkv"], 3)
            exps(0, 0)

            def step(i, p):
                if live(i + 1):
                    exps(i + 1, 1 - p)
                if live(i - 2):
                    copy_out(i - 2, p)
                if live(i - 1):
                    take_values(i - 1, 1 - p)
                    copy_probs(i - 1, 1 - p)

            rounds(act, step)

        def self_vector(dve, l, chain):
            m = sa[l]
            for p in range(2):
                chain.link(dve, nc.vector.memset(sm_p[p][:, NT * S:], 0.0))
            dve.wait_ge(m["q"], 1)
            if l == 0:
                dve.wait_ge(ld_const, 16 * CONST_LOADS)
                for w, x in ((0, q_all), (1, k_all)):
                    if w == 1:
                        dve.wait_ge(m["q"], 2)
                    table = rope[:, w, :].rearrange("p (a s) -> p a s", a=1).broadcast_to([128, HB, S])
                    for h in range(2):
                        ins = nc.vector.tensor_tensor(
                            x[:, h * HALF:(h + 1) * HALF].rearrange("p (b s) -> p b s", b=HB),
                            PS[:, 2 * w + h, 0:HALF].rearrange("p (b s) -> p b s", b=HB), table, ALU.mult)
                    ins.then_inc(m["qkv"], 1)
            else:
                nc.vector.tensor_scalar(halves(q_all[:, :]), two(0), sa_bias[:, 0:1], HD ** -0.5,
                                        ALU.add, ALU.mult).then_inc(m["qkv"], 1)
                dve.wait_ge(m["q"], 2)
                nc.vector.tensor_scalar(halves(k_all[:, :]), two(2), sa_bias[:, 1:2], None, ALU.add)\
                    .then_inc(m["qkv"], 1)
            dve.wait_ge(m["v"], 1)
            v_psum = PSF[0:S, 4 * 512:8 * 512].rearrange("p (b d) -> p b d", b=B)
            if l == 0:
                nc.vector.tensor_copy(v_all[:, :, :], v_psum).then_inc(m["qkv"], 1)
            else:
                nc.vector.tensor_tensor(
                    v_all[:, :, :], v_psum,
                    sa_bv[0:S, :].rearrange("p (a d) -> p a d", a=1).broadcast_to([S, B, D]),
                    ALU.add).then_inc(m["qkv"], 1)

            def stat(p, k):
                return sm_stat[:, p, k, :]

            def spread(x):
                return x.rearrange("p (j a) -> p j a", a=1).broadcast_to([128, NT, S])

            def centre(b, p):
                dve.wait_ge(m["scores"], b + 1)
                sc = PS[:, p, 0:NT * S].rearrange("p (j k) -> p j k", j=NT)
                chain.link(dve, nc.vector.tensor_reduce(stat(p, 0), sc, AX, ALU.max))
                wait_past(dve, m["norm"], b, 2)
                nc.vector.tensor_tensor(sm_d[p][:, :, :], sc, spread(stat(p, 0)), ALU.subtract)\
                    .then_inc(m["sub"], 1)

            def normalise(b, p):
                dve.wait_ge(m["exp"], b + 1)
                chain.link(dve, nc.vector.tensor_reduce(stat(p, 1), sm_d[p][:, :, :], AX, ALU.add))
                chain.link(dve, nc.vector.reciprocal(stat(p, 2), stat(p, 1)))
                wait_past(dve, m["tr"], b, 2)
                nc.vector.tensor_tensor(sm_p[p][:, 0:NT * S].rearrange("p (j s) -> p j s", j=NT), sm_d[p][:, :, :], spread(stat(p, 2)), ALU.mult)\
                    .then_inc(m["norm"], 1)

            centre(0, 0)
            start = chain.count

            def step(i, p):
                if live(i):
                    chain.count = i * 3 + start
                if live(i + 1):
                    centre(i + 1, 1 - p)
                if live(i):
                    normalise(i, p)

            rounds(dve, step)
            dve.wait_ge(m["out"], 1)
            if l == 0:
                nc.vector.tensor_tensor(halves(X[:, :]), halves(X[:, :]), two(0), ALU.add).then_inc(x_ready, 1)
            else:
                nc.vector.scalar_tensor_tensor(halves(X[:, :]), two(0), sa_bias[:, 3:4], halves(X[:, :]),
                                               ALU.add, ALU.add).then_inc(x_ready, 1)

        def fold_tensor(pe):
            pe.wait_ge(ld_fold, 16 * 4)
            for k in range(8):
                odd, r = k // 2 % 2, slice(XD * (k // 2 % 2), XD * (k // 2 % 2) + XD)
                for j in range(4):
                    pair = 4 * (k % 2) + j
                    mm = nc.tensor.matmul(PS[:, k, j * 128:(j + 1) * 128], fold_in[r, 2 * (k // 4), pair, :],
                                          fold_in[r, 2 * (k // 4) + 1, pair, :], start=True, stop=True)
                mm.then_inc(fold_mm, 1)

        def fold_scalar(act):
            for k in range(8):
                act.wait_ge(fold_mm, k + 1)
                dst = (qk_fold, vo_fold)[k // 4][:, :, :].rearrange("p (g a) c -> p a g c", a=2)
                nc.scalar.activation(dst[:, k // 2 % 2, 4 * (k % 2):4 * (k % 2) + 4, :],
                                     PS[:, k, :].rearrange("p (h c) -> p h c", h=4), ACT.Copy,
                                     scale=XD ** -0.5 if k < 4 else 1.0).then_inc(fold_ev, 1)

        def bias_vector(dve, chain):
            f, s = prob0[:, 0:S2], prob0[:, S2:S2 + HQ]
            dve.wait_ge(ld_bias, 48)
            nc.vector.tensor_copy(bias_sel, s)
            chain.link(dve, nc.vector.tensor_copy(bias_rows, f))
            nc.vector.tensor_tensor(bias_rows[64:128, :], f[64:128, :], bias_rows[64:128, :].bitcast(fp32),
                                    ALU.subtract).then_inc(bias_split, 1)

        def by_scalar(g, k):
            return k % 4 in (0, 3) if g == 0 else k % 3 in (0, 2)

        def copied(m, b, g, k):
            mine = [(h, c) for h in range(2) for c in range(NC) if by_scalar(h, c) == by_scalar(g, k)]
            return m["tra" if by_scalar(g, k) else "trc"], len(mine) * b + mine.index((g, k)) + 1

        def cross_tensor(pe, l, n):
            m = xa[l]
            pe.wait_ge(xn_ready, n + 1)
            if l == 0:
                pe.wait_ge(fold_ev, 8)
                for h in range(NH):
                    p = h % 2
                    if h >= 2:
                        pe.wait_ge(m["qpa" if p == 0 else "qpd"], h // 2)
                    for a in range(2):
                        mm = nc.tensor.matmul(PS[:, 2 * p + a, 0:HALF], qk_fold[:, h, :],
                                              XN[:, a * HALF:(a + 1) * HALF], start=True, stop=True)
                    mm.then_inc(m["qp"], 1)
                pe.wait_ge(m["qpa"], NH // 2)
                pe.wait_ge(m["qpd"], NH // 2)
                pe.wait_ge(bias_split, 1)
            else:
                pe.wait_ge(ld_xa, 16 * XA_LOADS)
                for a in range(2):
                    mm = nc.tensor.matmul(PS[:, a, 0:HALF], xa_w[:, 0, :], XN[:, a * HALF:(a + 1) * HALF],
                                          start=True, stop=True)
                mm.then_inc(m["qp"], 1)
                pe.wait_ge(m["qpd"], 1)

            def project(b, par, piece):
                if piece == 0:
                    pe.wait_ge(ld_k[1], (b + 1) * 16)
                    wait_past(pe, m["invc"], 2 * b, 4)
                    if not isinstance(b, int) or b:
                        pe.wait_ge(m["vev"], 3 * b)
                if piece == 3:
                    wait_past(pe, m["invc"], 2 * b, 3)
                if piece < 3:
                    if piece:
                        pe.wait_ge(m["kev"], 3 * b + piece)
                    nc.tensor.matmul(PS[:, 7, 0:KB], xa_w[:, 1, :], ctxT[:, piece * KB:(piece + 1) * KB],
                                     start=True, stop=True).then_inc(m["kmm"], 1)
                else:
                    if piece == 3:
                        pe.wait_ge(m["kev"], 3 * b + 3)
                    else:
                        pe.wait_ge(m["vev"], 3 * b + piece - 3)
                    for j in range(4):
                        c = 4 * (piece - 3) + j
                        mm = nc.tensor.matmul(PS[0:KC, 7, j * 128:(j + 1) * 128],
                                              ctxT[:, c * KC:(c + 1) * KC], xa_w[:, 2, :],
                                              start=True, stop=True)
                    mm.then_inc(m["vmm"], 1)

            def scores(b, par, s):
                if s == 0:
                    pe.wait_ge(m["q"], b + 1)
                    pe.wait_ge(m["kspl"], b + 1)
                rows = slice(s * 128, (s + 1) * 128)
                for j in range(NKB):
                    cols = slice(j * KB, (j + 1) * KB)
                    dst = PS[:, j, 0:KB]
                    wait_past(pe, m["exp"], NKB * (NT * b + s) + j, NKB)
                    nc.tensor.matmul(dst, qH[par][:, rows], kH[par][:, cols], start=True, stop=False)
                    nc.tensor.matmul(dst, qH[par][:, rows], kL[par][:, cols], start=False, stop=False)
                    mm = nc.tensor.matmul(dst, qL[par][:, rows], kH[par][:, cols], start=False, stop=l == 1)
                    if l == 0:
                        mm = nc.tensor.matmul(dst, bias_sel[:, rows], bias_rows[:, cols], start=False, stop=True)
                    mm.then_inc(m["scores"], 1)

            def transposes(b, g, k):
                at = 2 * NC * b + NC * g + k
                size = (GA, GB)[g]
                if k == 0:
                    pe.wait_ge(m["exp"], NKB * (NT * b + (GA if g == 0 else NT)))
                if l == 0:
                    wait_past(pe, m["trc"], at, 2)
                elif k >= 2:
                    pe.wait_ge(*copied(m, b, g, k - 2))
                elif g == 1:
                    pe.wait_ge(*copied(m, b, 0, k - 2 + NC))
                elif not isinstance(b, int) or b:
                    pe.wait_ge(*copied(m, b - 1, 1, k - 2 + NC))
                for j in range(size):
                    mm = nc.tensor.transpose(PS[0:KC, 3 + k % 2, j * 128:(j + 1) * 128],
                                             prob[g][:, j, k * KC:(k + 1) * KC], ident[:, :])
                mm.then_inc(m["tr"], 1)

            def product(b, par, g, k):
                at = 2 * NC * b + NC * g + k
                size = (GA, GB)[g]
                if k == 0:
                    wait_past(pe, m["norm"], 2 * b + g, 2)
                if l == 0:
                    if g == 0 and k % 4 == 0:
                        pe.wait_ge(m["vspl"], 3 * b + k // 4 + 1)
                    pe.wait_ge(m["trc"], at + 1)
                    dst, n, p = PS[:, 5 + g, 0:128 * size], 128 * size, k % 3
                    v_hi, v_lo = vH[0:KC, k, :], vL[0:KC, k, :]
                    p_hi, p_lo = pH[p][0:KC, 0:n], pL[p][0:KC, 0:n]
                    nc.tensor.matmul(dst, v_hi, p_hi, start=k == 0, stop=False)
                    nc.tensor.matmul(dst, v_lo, p_hi, start=False, stop=False)
                    mm = nc.tensor.matmul(dst, v_hi, p_lo, start=False, stop=k == NC - 1)
                else:
                    if g == 0 and k == 0:
                        pe.wait_ge(m["vev"], 3 * b + 3)
                    pe.wait_ge(*copied(m, b, g, k))
                    n = QCOLS[g]
                    for j in range(4):
                        r = slice(32 * j, 32 * j + 32)
                        mm = nc.tensor.matmul(PS[r, 5 + g, 0:n], vals[par][0:KC, k, r],
                                              pT[k % 3][0:KC, j * n:(j + 1) * n], start=k == 0, stop=k == NC - 1)
                mm.then_inc(m["pv"], 1)

            def sums(b, g):
                size = (GA, GB)[g]
                pe.wait_ge(m["idiag"], 2 * b + g + 1)
                wait_past(pe, m["invc"], 2 * b + g, 1)
                if l == 1 and not (isinstance(b, int) and b + (2 if g else 1) >= B):
                    pe.wait_ge(m["kev" if g else "vev"], 3 * b + (9 if g else 6))
                if l == 0:
                    mm = nc.tensor.matmul(PS[:, 7, 0:128 * size], ones[:, :],
                                          inv_diag[g][:, 0:size, :].rearrange("p a b -> p (a b)"),
                                          start=True, stop=True)
                else:
                    n, cols = QCOLS[g], inv_diag[g][:, 0:size, :].rearrange("p a b -> p (a b)")
                    for j in range(4):
                        lo = j * n
                        while lo < (j + 1) * n:
                            hi = min((j + 1) * n, (lo // 128 + 1) * 128)
                            mm = nc.tensor.matmul(PS[32 * j:32 * j + 32, 7, lo - j * n:hi - j * n],
                                                  ones[:, 0:32], cols[:, lo:hi], start=True, stop=True)
                            lo = hi
                mm.then_inc(m["inv"], 1)

            def chunk(b, par, g, k, first):
                transposes(b, g, k)
                if k >= 2:
                    product(b, par, g, k - 2)
                elif not first:
                    pb, pp, pg = (b, par, 0) if g else (b - 1, 1 - par, 1)
                    product(pb, pp, pg, NC - 2 + k)
                    if k == 1:
                        sums(pb, pg)

            def batch(b, par):
                first = isinstance(b, int) and b == 0
                last = isinstance(b, int) and b == B - 1
                for s in range(NT):
                    scores(b, par, s)
                    if s < GA and not first:
                        for k in range(3 * s, 3 * s + 3):
                            chunk(b - 1, 1 - par, 1, k, False)
                    if s >= GA:
                        for k in range(4 * (s - GA), 4 * (s - GA) + 4):
                            chunk(b, par, 0, k, first)
                    if l == 1 and not last and s != 3:
                        project(b + 1, 1 - par, s if s < 3 else s - 1)

            if l == 1:
                for piece in range(6):
                    project(0, 0, piece)
            batch(0, 0)
            batch(1, 1)
            batch(2, 0)
            with pe.Fori(3, B - 2, 2) as i:
                batch(i, 1)
                batch(i + 1, 0)
            batch(B - 1, 1)
            for k in range(NC):
                chunk(B - 1, 1, 1, k, False)
            product(B - 1, 1, 1, NC - 2)
            product(B - 1, 1, 1, NC - 1)
            sums(B - 1, 1)
            pe.wait_ge(m["norm"], 2 * B)
            if l == 1:
                pe.wait_ge(m["vo"], 1)
            parts = NH if l == 0 else 4
            for h in range(parts):
                for a in range(2):
                    if l == 0:
                        x = QO[:, a * HB:(a + 1) * HB, h * S:(h + 1) * S]
                    else:
                        x = out_q.rearrange("p (b q) -> p b q", b=B)[:, a * HB:(a + 1) * HB, h * S:(h + 1) * S]
                    mm = nc.tensor.matmul(PS[:, a, 0:HALF], vo_fold[:, h, :], x,
                                          start=h == 0, stop=h == parts - 1)
            mm.then_inc(m["out"], 1)

        def cross_gpsimd(pool, l):
            m = xa[l]
            if l == 1:
                pool.wait_ge(x_ready, 2)
                pool.wait_ge(ld_xa, 16 * XA_LOADS)
                nc.gpsimd.tensor_tensor(
                    vo_fold[:, 0:4, :],
                    xa_w[:, 3, :].rearrange("p (a o) -> p a o", a=1).broadcast_to([128, 4, 128]),
                    quad_mask[:, :].rearrange("p (h a) -> p h a", a=1).broadcast_to([128, 4, 128]),
                    ALU.mult).then_inc(m["vo"], 1)
                pool.wait_ge(m["qpd"], 1)
            else:
                pool.wait_ge(m["qpa"], NH // 2)
                pool.wait_ge(m["qpd"], NH // 2)
            steps = [0]

            def once(x):
                o = ones[0:x.shape[0], 0:1]
                if len(x.shape) == 3:
                    o = o.rearrange("p (a b) -> p a b", a=1)
                return o.broadcast_to(list(x.shape))

            def link(ins):
                ins.then_inc(pool_step, 1)
                pool_count[0] = pool_count[0] + 1
                steps[0] += 1
                pool.wait_ge(pool_step, pool_count[0])

            def halve(hi, lo, x, last):
                link(nc.gpsimd.tensor_tensor(hi, x, once(x), ALU.mult))
                nc.gpsimd.tensor_tensor(lo, x, hi.bitcast(fp32), ALU.subtract).then_inc(last, 1)

            def queries(b, par):
                wait_past(pool, m["scores"], 21 * b, 22)
                if l == 0:
                    nc.gpsimd.tensor_copy(qH[par], QO_flat[:, bass.ds(b * HQ, HQ)]).then_inc(m["qh"], 1)
                else:
                    q = q_all[:, bass.ds(b * S, S)].rearrange("p (a q) -> p a q", a=1)
                    link(nc.gpsimd.tensor_tensor(
                        q_diag1.rearrange("p (h q) -> p h q", h=NH), q.broadcast_to([128, NH, S]),
                        head_mask[:, :].rearrange("p (h a) -> p h a", a=1).broadcast_to([128, NH, S]),
                        ALU.mult))
                    by4 = q_diag1.rearrange("p (j c) -> p j c", j=4)
                    for g, (lo, n) in enumerate(((0, 128), (128, 96))):
                        dst = slice(0, 512) if g == 0 else slice(512, HQ)
                        link(nc.gpsimd.tensor_tensor(qH[par][:, dst].rearrange("p (j c) -> p j c", j=4),
                                                     by4[:, :, lo:lo + n], once(by4[:, :, lo:lo + n]), ALU.mult))
                        ins = nc.gpsimd.tensor_tensor(
                            qL[par][:, dst].rearrange("p (j c) -> p j c", j=4), by4[:, :, lo:lo + n],
                            qH[par][:, dst].bitcast(fp32).rearrange("p (j c) -> p j c", j=4), ALU.subtract)
                    ins.then_inc(m["q"], 1)
                    pool.wait_ge(m["q"], b + 1)

            def keys(b, par):
                if l == 0:
                    pool.wait_ge(ld_k[0], (b + 1) * 16)
                    halve(kH[par], kL[par], ctxT[:, :], m["kspl"])
                else:
                    pool.wait_ge(m["kev"], NKB * b + NKB)
                    halve(kH[par], kL[par], k_now, m["kspl"])

            def context(b):
                pool.wait_ge(ld_v, (b + 1) * 16)
                for i in range(3):
                    wait_past(pool, m["pv"], 2 * NC * b + 4 * i, 9)
                    c = slice(4 * i, 4 * i + 4)
                    halve(vH[0:KC, c, :], vL[0:KC, c, :], ctxV[0:KC, c, :], m["vspl"])

            def batch(b, par):
                if not (isinstance(b, int) and b == B - 1):
                    queries(b + 1, 1 - par)
                    keys(b + 1, 1 - par)
                if l == 0:
                    context(b)

            queries(0, 0)
            keys(0, 0)
            batch(0, 0)
            batch(1, 1)
            batch(2, 0)
            steps[0] = 0
            start = pool_count[0]
            per_batch = 4
            with pool.Fori(3, B - 2, 2) as i:
                pool_count[0] = (i - 3) * per_batch + start
                batch(i, 1)
                batch(i + 1, 0)
            assert steps[0] == 2 * per_batch
            pool_count[0] = start + per_batch * (B - 4)
            batch(B - 1, 1)

        def cross_sync(sp, l):
            m = xa[l]

            def load(b):
                if l == 0:
                    wait_past(sp, m["kspl"], b, 1)
                else:
                    wait_past(sp, m["vmm"], 3 * b, 1)
                sp.dma_start(ctxT[:, :], t["ctx_T"][bass.ds(b, 1), :, :].rearrange("a p n -> (a p) n"))\
                    .then_inc(ld_k[l], 16)
                if l == 0:
                    wait_past(sp, m["vspl"], 3 * b, 1)
                    sp.dma_start(ctxV[0:KC, :, :],
                                 t["ctx_1024"][bass.ds(b, 1), :, :].rearrange("a (c p) d -> (a p) c d", p=KC))\
                        .then_inc(ld_v, 16)

            if l == 1:
                sp.wait_ge(x_ready, 3)
            load(0)
            with sp.Fori(1, B) as i:
                load(i)

        def cross_scalar(act, l):
            m = xa[l]
            if l == 0:
                for h in range(0, NH, 2):
                    act.wait_ge(m["qp"], h + 1)
                    for a in range(2):
                        ins = nc.scalar.activation(
                            QO[:, a * HB:(a + 1) * HB, h * S:(h + 1) * S],
                            PS[:, a, 0:HALF].rearrange("p (b s) -> p b s", b=HB), ACT.Copy)
                    ins.then_inc(m["qpa"], 1)

            def keys(b, piece):
                act.wait_ge(m["kmm"], NKB * b + piece + 1)
                if piece == 0:
                    wait_past(act, m["kspl"], b, 1)
                nc.scalar.activation(k_now[:, piece * KB:(piece + 1) * KB], PS[:, 7, 0:KB], ACT.Identity,
                                     bias=xa_bias[:, 1:2]).then_inc(m["kev"], 1)

            def copy_chunk(b, g, k):
                if l == 1 and not by_scalar(g, k):
                    return
                at = 2 * NC * b + NC * g + k
                n = 128 * (GA, GB)[g]
                act.wait_ge(m["tr"], at + 1)
                wait_past(act, m["pv"], at, 3)
                if l == 0:
                    nc.scalar.activation(pH[k % 3][0:KC, 0:n], PS[0:KC, 3 + k % 2, 0:n], ACT.Copy)\
                        .then_inc(m["trh"], 1)
                else:
                    nc.scalar.activation(pT[k % 3][0:KC, 0:n], PS[0:KC, 3 + k % 2, 0:n], ACT.Copy)\
                        .then_inc(m["tra"], 1)

            def exps(b, s, j):
                g = 0 if s < GA else 1
                if j == 0:
                    act.wait_ge(m["mx"], NT * b + s + 1)
                    if s == 0:
                        wait_past(act, m["tr"], 2 * NC * b, 1 + NC)
                    if s == GA:
                        wait_past(act, m["tr"], 2 * NC * b, 1)
                    if s == 0 or s == GA:
                        wait_past(act, m["idiag"], 2 * b + g, 2)
                nc.scalar.activation(prob[g][:, s - GA * g, j * KB:(j + 1) * KB], PS[:, j, 0:KB], ACT.Exp,
                                     bias=neg_max[:, s:s + 1],
                                     accum_out=part_sum[:, s, j:j + 1]).then_inc(m["exp"], 1)

            def copy_inv(b, g):
                n = 128 * (GA, GB)[g] if l == 0 else QCOLS[g]
                act.wait_ge(m["inv"], 2 * b + g + 1)
                wait_past(act, m["norm"], 2 * b + g, 1)
                nc.scalar.activation(inv_cols[:, 0:n], PS[:, 7, 0:n], ACT.Copy).then_inc(m["invc"], 1)

            def chunk(b, g, k, first):
                copy_chunk(b, g, k)
                if k == 1 and not first:
                    copy_inv(*((b, 0) if g else (b - 1, 1)))

            def batch(b, par):
                first = isinstance(b, int) and b == 0
                last = isinstance(b, int) and b == B - 1
                for s in range(NT):
                    if s < GA:
                        todo = [] if first else [(b - 1, 1, k, False) for k in range(3 * s, 3 * s + 3)]
                    else:
                        todo = [(b, 0, k, first) for k in range(4 * (s - GA), 4 * (s - GA) + 4)]
                    between = (2, 3) if l == 0 else (2, 2)
                    for c in todo[:1]:
                        chunk(*c)
                    exps(b, s, 0)
                    for c in todo[1:between[0]]:
                        chunk(*c)
                    exps(b, s, 1)
                    for c in todo[between[0]:between[1]]:
                        chunk(*c)
                    exps(b, s, 2)
                    if l == 1 and not last and s < 3:
                        keys(b + 1, s)
                    for c in todo[between[1]:]:
                        chunk(*c)

            if l == 1:
                for piece in range(3):
                    keys(0, piece)
            batch(0, 0)
            batch(1, 1)
            batch(2, 0)
            with act.Fori(3, B - 2, 2) as i:
                batch(i, 1)
                batch(i + 1, 0)
            batch(B - 1, 1)
            for k in range(NC):
                chunk(B - 1, 1, k, False)
            copy_inv(B - 1, 1)

        def cross_vector(dve, l, chain):
            m = xa[l]
            if l == 0:
                for h in range(1, NH, 2):
                    dve.wait_ge(m["qp"], h + 1)
                    for a in range(2):
                        ins = nc.vector.tensor_copy(
                            QO[:, a * HB:(a + 1) * HB, h * S:(h + 1) * S],
                            PS[:, 2 + a, 0:HALF].rearrange("p (b s) -> p b s", b=HB))
                    ins.then_inc(m["qpd"], 1)
            else:
                dve.wait_ge(m["qp"], 1)
                nc.vector.tensor_scalar(halves(q_all[:, :]), two(0), xa_bias[:, 0:1], HD ** -0.5,
                                        ALU.add, ALU.mult).then_inc(m["qpd"], 1)

            def values(b, par, piece):
                dve.wait_ge(m["vmm"], 3 * b + piece + 1)
                if piece == 0:
                    wait_past(dve, m["pv"], 2 * NC * b, 2 * NC + 1)
                nc.vector.tensor_tensor(
                    vals[par][0:KC, 4 * piece:4 * piece + 4, :],
                    PS[0:KC, 7, :].rearrange("p (c d) -> p c d", c=4),
                    xa_bv[0:KC, :].rearrange("p (a d) -> p a d", a=1).broadcast_to([KC, 4, D]),
                    ALU.add).then_inc(m["vev"], 1)

            def maxima(b, s):
                for j in range(NKB):
                    dve.wait_ge(m["scores"], 21 * b + NKB * s + j + 1)
                    ins = nc.vector.tensor_reduce(part_max[:, s % 2, j:j + 1], PS[:, j, 0:KB], AX, ALU.max)
                    if j < NKB - 1:
                        ins.then_inc(dve_step, 1)
                        chain.count = chain.count + 1
                chain.link(dve, ins)
                wait_past(dve, m["exp"], NKB * (NT * b + s) + NKB - 1, NKB * NT)
                nc.vector.tensor_reduce(neg_max[:, s:s + 1], part_max[:, s % 2, :], AX, ALU.max, negate=True)\
                    .then_inc(m["mx"], 1)

            def copy_chunk(b, g, k):
                at = 2 * NC * b + NC * g + k
                n = 128 * (GA, GB)[g]
                if l == 0:
                    dve.wait_ge(m["trh"], at + 1)
                    wait_past(dve, m["pv"], at, 3)
                    nc.vector.tensor_tensor(pL[k % 3][0:KC, 0:n], PS[0:KC, 3 + k % 2, 0:n],
                                            pH[k % 3][0:KC, 0:n].bitcast(fp32), ALU.subtract)\
                        .then_inc(m["trc"], 1)
                elif not by_scalar(g, k):
                    dve.wait_ge(m["tr"], at + 1)
                    wait_past(dve, m["pv"], at, 3)
                    nc.vector.tensor_copy(pT[k % 3][0:KC, 0:n], PS[0:KC, 3 + k % 2, 0:n]).then_inc(m["trc"], 1)

            def reciprocals(b, g):
                lo, size = (0, GA) if g == 0 else (GA, GB)
                dve.wait_ge(m["exp"], NKB * (NT * b + lo + size))
                chain.link(dve, nc.vector.tensor_reduce(row_sum[:, lo:lo + size], part_sum[:, lo:lo + size, :],
                                                        AX, ALU.add))
                chain.link(dve, nc.vector.reciprocal(row_inv[:, lo:lo + size], row_sum[:, lo:lo + size]))
                wait_past(dve, m["inv"], 2 * b + g, 2)
                nc.vector.tensor_tensor(
                    inv_diag[g][:, 0:size, :],
                    ident[:, :].rearrange("p (a c) -> p a c", a=1).broadcast_to([128, size, 128]),
                    row_inv[:, lo:lo + size].rearrange("p (j a) -> p j a", a=1).broadcast_to([128, size, 128]),
                    ALU.mult).then_inc(m["idiag"], 1)

            def scale_out(b, g):
                lo, size = (0, GA) if g == 0 else (GA, GB)
                dve.wait_ge(m["invc"], 2 * b + g + 1)
                dve.wait_ge(m["pv"], 2 * NC * b + NC * g + NC)
                n = 128 * size if l == 0 else QCOLS[g]
                dst = QO_flat[:, bass.ds(b * HQ + lo * 128, n)] if l == 0 else \
                    out_q[:, bass.ds(b * 4 * S + (QCOLS[0] if g else 0), n)]
                nc.vector.tensor_tensor(dst, PS[:, 5 + g, 0:n], inv_cols[:, 0:n], ALU.mult).then_inc(m["norm"], 1)

            def chunk(b, g, k, first):
                copy_chunk(b, g, k)
                if k == 2 and not first:
                    scale_out(*((b, 0) if g else (b - 1, 1)))
                if k == NC - 1:
                    reciprocals(b, g)

            def queries(b, par):
                dve.wait_ge(m["qh"], b + 1)
                nc.vector.tensor_tensor(qL[par], QO_flat[:, bass.ds(b * HQ, HQ)], qH[par].bitcast(fp32),
                                        ALU.subtract).then_inc(m["q"], 1)

            def batch(b, par):
                first = isinstance(b, int) and b == 0
                last = isinstance(b, int) and b == B - 1
                for s in range(NT):
                    maxima(b, s)
                    if l == 0 and s == 3 and not last:
                        queries(b + 1, 1 - par)
                    if s < GA and not first:
                        for k in range(3 * s, 3 * s + 3):
                            chunk(b - 1, 1, k, False)
                    if s >= GA:
                        for k in range(4 * (s - GA), 4 * (s - GA) + 4):
                            chunk(b, 0, k, first)
                    if l == 1 and not last and s > 3:
                        values(b + 1, 1 - par, s - 4)

            if l == 1:
                for piece in range(3):
                    values(0, 0, piece)
            else:
                queries(0, 0)
            batch(0, 0)
            batch(1, 1)
            batch(2, 0)
            per_batch = 3 * NT + 4
            start = chain.count
            with dve.Fori(3, B - 2, 2) as i:
                chain.count = (i - 3) * per_batch + start
                batch(i, 1)
                batch(i + 1, 0)
            chain.count = start + per_batch * (B - 4)
            batch(B - 1, 1)
            for k in range(NC):
                chunk(B - 1, 1, k, False)
            scale_out(B - 1, 1)
            dve.wait_ge(m["out"], 1)
            bias = xa_bias[:, 4:5] if l == 0 else xa_bias[:, 3:4]
            nc.vector.scalar_tensor_tensor(halves(X[:, :]), two(0), bias, halves(X[:, :]), ALU.add, ALU.add)\
                .then_inc(x_ready, 1)

        def experts_tensor(pe, l, n):
            m = ff[l]
            ng = E if l == 0 else WCOLS
            pe.wait_ge(xn_ready, n + 1)
            if l == 0:
                pe.wait_ge(ld_ffn, 16 * FFN_LOADS)
            for b in range(B):
                mm = nc.tensor.matmul(PS[0:S, 6, b * ng:(b + 1) * ng], XN[:, b * S:(b + 1) * S],
                                      gate_w[l][:, 0:ng], start=True, stop=True)
            mm.then_inc(m["logit"], 1)
            pe.wait_ge(m["gates"], 1)
            nc.tensor.transpose(PS[:, 7, 0:S], routed[:, :, :].rearrange("p b e -> p (b e)"),
                                ident[0:S, 0:S]).then_inc(m["gtr"], 1)
            pe.wait_ge(m["blk"], 1)
            if l == 1:
                for a in range(2):
                    mm = nc.tensor.matmul(PS[:, 4 + a, 0:HALF], b2[:, :],
                                          w_blk[:, a * HB:(a + 1) * HB, :], start=True, stop=True)
                mm.then_inc(m["b2mm"], 1)

            def expert(e, par):
                pe.wait_ge(ld_w[l][par], (e // 2 + 1) * 32 if isinstance(e, int) else (e - par) * 16 + 32)
                for f in range(NF):
                    p = f % 2
                    wait_past(pe, m["hact"], NF * e + f, 2)
                    for a in range(2):
                        mm = nc.tensor.matmul(PS[:, 2 * p + a, 0:HALF], w1[par][:, f * 128:(f + 1) * 128],
                                              XN[:, a * HALF:(a + 1) * HALF], start=True, stop=True)
                    mm.then_inc(m["h"], 1)
                pe.wait_ge(m["wsel"], e + 1)
                wait_past(pe, m["wcols"], e, 1)
                for a in range(2):
                    mm = nc.tensor.matmul(PS[:, 6 + a, 0:HALF], ones[:, :],
                                          w_blk_e[:, par, a * HALF:(a + 1) * HALF], start=True, stop=True)
                mm.then_inc(m["wmm"], 1)
                if isinstance(e, int) and e == 0:
                    if l == 1:
                        pe.wait_ge(m["ymul"], 1)
                else:
                    pe.wait_ge(m["ymul"], e + l)
                for f in range(NF):
                    pe.wait_ge(m["hact"], NF * e + f + 1)
                    for a in range(2):
                        mm = nc.tensor.matmul(PS[:, 4 + a, 0:HALF], w2[par][:, f, :],
                                              hidden[:, f, a * HALF:(a + 1) * HALF],
                                              start=f == 0, stop=f == NF - 1)
                mm.then_inc(m["y"], 1)

            expert(0, 0)
            expert(1, 1)
            with pe.Fori(2, E - 1, 2) as i:
                expert(i, 0)
                expert(i + 1, 1)

        def experts_sync(sp, l):
            m = ff[l]

            def load(e, par):
                wait_past(sp, m["y"], e, 2)
                w1s = t["L0_ffn_w1" if l == 0 else "L1_ffn_W1"]
                w2s = t["L0_ffn_w2" if l == 0 else "L1_ffn_W2"]
                sp.dma_start(w1[par], w1s[bass.ds(e, 1), :, :].rearrange("a c f -> (a c) f"))\
                    .then_inc(ld_w[l][par], 16)
                sp.dma_start(w2[par], w2s[bass.ds(e, 1), :, :].rearrange("a (g p) d -> (a p) g d", p=128))\
                    .then_inc(ld_w[l][par], 16)

            if l == 0:
                sp.wait_ge(xa[0]["kspl"], B)
                sp.wait_ge(xa[0]["vspl"], 3 * B)
            else:
                sp.wait_ge(xa[1]["vmm"], 3 * B)
                sp.wait_ge(xa[1]["kspl"], B)
            load(0, 0)
            load(1, 1)
            with sp.Fori(2, E - 1, 2) as i:
                load(i, 0)
                load(i + 1, 1)

        def experts_scalar(act, l):
            m = ff[l]
            func = ACT.Gelu if l == 0 else ACT.Gelu_apprx_tanh
            act.wait_ge(m["gsub"], 1)
            ins = nc.scalar.activation(gate[:, :, 0:E], gate[:, :, 0:E], ACT.Exp)
            if l == 1:
                ins = nc.scalar.activation(gate[:, :, E:WCOLS], gate[:, :, E:WCOLS], ACT.Exp, scale=-1.0)
            ins.then_inc(m["gexp"], 1)

            def expert(e, par):
                for f in range(NF):
                    act.wait_ge(m["h"], NF * e + f + 1)
                    if f == 0:
                        wait_past(act, m["y"], e, 1)
                    bias = b1[:, l, bass.ds(e * NF + f, 1)]
                    nc.scalar.activation(halves(hidden[:, f, :]), two(2 * (f % 2)), func, bias=bias)\
                        .then_inc(m["hact"], 1)
                act.wait_ge(m["wmm"], e + 1)
                wait_past(act, m["ymul"], e + l, 2 + l)
                nc.scalar.activation(halves(w_cols[:, par, :]), two(6), ACT.Copy).then_inc(m["wcols"], 1)

            expert(0, 0)
            expert(1, 1)
            with act.Fori(2, E - 1, 2) as i:
                expert(i, 0)
                expert(i + 1, 1)

        def experts_vector(dve, l, chain):
            m = ff[l]
            ng = E if l == 0 else WCOLS
            G = gate[:, :, 0:E]

            def per_batch(x):
                return x.rearrange("p (b a) -> p b a", a=1).broadcast_to([S, B, E])

            st = [gate_stat[:, k, :] for k in range(4)]
            dve.wait_ge(m["logit"], 1)
            logits = PS[0:S, 6, 0:B * ng].rearrange("p (b e) -> p b e", b=B)
            if l == 0:
                chain.link(dve, nc.vector.tensor_copy(G, logits))
            else:
                chain.link(dve, nc.vector.tensor_tensor(
                    gate[:, :, :], logits,
                    gate_b[:, :].rearrange("p (a e) -> p a e", a=1).broadcast_to([S, B, WCOLS]), ALU.add))
            chain.link(dve, nc.vector.tensor_reduce(st[0], G, AX, ALU.max))
            nc.vector.tensor_tensor(G, G, per_batch(st[0]), ALU.subtract).then_inc(m["gsub"], 1)
            dve.wait_ge(m["gexp"], 1)
            chain.link(dve, nc.vector.tensor_reduce(st[1], G, AX, ALU.add))
            chain.link(dve, nc.vector.reciprocal(st[2], st[1]))
            if l == 0:
                nc.vector.tensor_tensor(routed[:, :, :], G, per_batch(st[2]), ALU.mult).then_inc(m["gates"], 1)
            else:
                chain.link(dve, nc.vector.tensor_tensor(gate2[:, :, :], G, per_batch(st[2]), ALU.mult))
                z = gate[:, :, E]
                chain.link(dve, nc.vector.tensor_scalar(st[0], z, 1.0, None, ALU.add))
                chain.link(dve, nc.vector.reciprocal(st[1], st[0]))
                chain.link(dve, nc.vector.tensor_scalar(st[0], st[1], THRESHOLD, None, ALU.mult))
                chain.link(dve, nc.vector.tensor_tensor(gate2[:, :, :], gate2[:, :, :], per_batch(st[0]),
                                                        ALU.subtract))
                chain.link(dve, nc.vector.tensor_scalar(gate2[:, :, :], gate2[:, :, :], 0.0, None, ALU.max))
                chain.link(dve, nc.vector.tensor_reduce(st[1], gate2[:, :, :], AX, ALU.add))
                chain.link(dve, nc.vector.tensor_scalar(st[2], st[1], 0.0, None, ALU.is_equal))
                chain.link(dve, nc.vector.tensor_tensor(st[3], st[1], st[2], ALU.add))
                chain.link(dve, nc.vector.reciprocal(st[0], st[3]))
                nc.vector.tensor_tensor(routed[:, :, :], gate2[:, :, :], per_batch(st[0]), ALU.mult)\
                    .then_inc(m["gates"], 1)
            dve.wait_ge(m["gtr"], 1)
            if l == 0:
                rest = CAP - 8
                chain.link(dve, nc.vector.memset(work[:, :], 2.0))
                chain.link(dve, nc.vector.tensor_copy(gT[:, :], PS[:, 7, 0:S]))
                chain.link(dve, nc.vector.tensor_copy(work[:, 0:S], gT[:, :]))
                chain.link(dve, nc.vector.max(top8[:, 0, :], work[:, 0:S]))
                chain.link(dve, nc.vector.match_replace(work2[:, 0:S], top8[:, 0, :], work[:, 0:S], -1.0))
                chain.link(dve, nc.vector.tensor_copy(work2[:, S:64], work[:, S:64]))
                chain.link(dve, nc.vector.max(top8[:, 1, :], work2[:, 0:S]))
                chain.link(dve, nc.vector.memset(top8[:, 1, rest:8], 2.0))
                chain.link(dve, nc.vector.match_replace(work[:, :], top8[:, 1, :], work2[:, :], -1.0))
                chain.link(dve, nc.vector.tensor_scalar(work[:, 0:S], work[:, 0:S], -1.0, None, ALU.is_equal))
                chain.link(dve, nc.vector.tensor_tensor(w_be[:, :], gT[:, :], work[:, 0:S], ALU.mult))
            else:
                chain.link(dve, nc.vector.tensor_copy(w_be[:, :], PS[:, 7, 0:S]))
            ins = nc.vector.tensor_tensor(
                w_blk[:, :, :], w_be[:, :].rearrange("p (a s) -> p a s", a=1).broadcast_to([128, B, S]),
                batch_mask[:, :].rearrange("p (b a) -> p b a", a=1).broadcast_to([128, B, S]), ALU.mult)
            ins.then_inc(m["blk"], 1)
            dve.wait_ge(m["blk"], 1)

            def select(e, par):
                wait_past(dve, m["wmm"], e, 2)
                nc.vector.tensor_scalar(w_blk_e[:, par, :], w_blk[:, :, :].rearrange("p b s -> p (b s)"),
                                        expert_mask[:, bass.ds(e, 1)], None, ALU.mult).then_inc(m["wsel"], 1)

            if l == 1:
                dve.wait_ge(m["b2mm"], 1)
                nc.vector.tensor_tensor(halves(X[:, :]), halves(X[:, :]), two(4), ALU.add).then_inc(m["ymul"], 1)
            select(0, 0)
            start = chain.count

            def expert(e, par, final=False):
                if not final:
                    select(e + 1, 1 - par)
                dve.wait_ge(m["y"], e + 1)
                dve.wait_ge(m["wcols"], e + 1)
                ins = nc.vector.tensor_tensor(halves(XC[:, :]), two(4), halves(w_cols[:, par, :]), ALU.mult)
                ins.then_inc(m["ymul"], 1)
                dve.wait_ge(m["ymul"], e + 1 + l)
                ins = nc.vector.tensor_tensor(X[:, :], X[:, :], XC[:, :], ALU.add)
                if final:
                    ins.then_inc(x_ready, 1)
                else:
                    chain.link(dve, ins)

            expert(0, 0)
            with dve.Fori(1, E - 2, 2) as i:
                chain.count = i + start
                expert(i, 1)
                expert(i + 1, 0)
            chain.count = start + E - 1
            expert(E - 1, 1, final=True)

        block = ctx.enter_context(nc.Block())

        @block.sync
        def _(sp):
            sp.dma_start(X[:, :], t["x_T"]).then_inc(ld_x, 16)
            for w, name in enumerate(("xa0_qT", "xa0_kT", "xa0_vT", "L0_xattn_W_out")):
                sp.dma_start(fold_in[:, w, :, :], t[name].rearrange("(g p) c -> p g c", p=128))\
                    .then_inc(ld_fold, 16)
            for w, name in enumerate(("sa0_q", "sa0_k", "sa0_v", "sa0_o")):
                sp.dma_start(sa_w[0][:, w, :], t[name]).then_inc(ld_sa, 16)
            for w, name in enumerate(("sa1_q", "sa1_k", "sa1_v", "sa1_o")):
                sp.dma_start(sa_w[1][:, w, :], t[name]).then_inc(ld_sa, 16)
            sp.wait_ge(consts_set, 2)
            sp.dma_start(prob0[0:S, 0:S2], t["fside_SxS2_0"]).then_inc(ld_bias, 16)
            sp.dma_start(prob0[64:64 + S, 0:S2], t["fside_SxS2_0"]).then_inc(ld_bias, 16)
            sp.dma_start(prob0[:, S2:S2 + HQ], t["bias_sel"]).then_inc(ld_bias, 16)
            cross_sync(sp, 0)
            experts_sync(sp, 0)
            cross_sync(sp, 1)
            experts_sync(sp, 1)
            sp.wait_ge(x_ready, 6)
            sp.dma_start(out, X[:, :]).then_inc(out_done, 16)
            sp.wait_ge(out_done, 16)

        @block.gpsimd
        def _(pool):
            pool.wait_ge(ld_const, 16 * CONST_LOADS)
            self_gpsimd(pool, 0)
            cross_gpsimd(pool, 0)
            self_gpsimd(pool, 1)
            cross_gpsimd(pool, 1)

        @block.scalar
        def _(act):
            act.dma_start(ident[:, :], t["ident"]).then_inc(ld_const, 16)
            act.dma_start(head_mask[:, :], t["head_mask"]).then_inc(ld_const, 16)
            act.dma_start(rope[:, :, :], t["rope"]).then_inc(ld_const, 16)
            act.dma_start(quad_mask[:, :], t["quad_mask"]).then_inc(ld_const, 16)
            act.dma_start(batch_mask[:, :], t["batch_mask"]).then_inc(ld_const, 16)
            act.dma_start(expert_mask[:, :], t["expert_mask"]).then_inc(ld_const, 16)
            act.dma_start(gate_w[0][:, 0:E], t["L0_ffn_gate_w"]).then_inc(ld_ffn, 16)
            act.dma_start(gate_w[1][:, 0:E], t["L1_ffn_Wg"]).then_inc(ld_ffn, 16)
            act.dma_start(gate_w[1][:, E:WCOLS], t["L1_ffn_Wt"]).then_inc(ld_ffn, 16)
            act.dma_start(gate_b[:, 0:E], t["L1_ffn_bg"].broadcast_to([S, E])).then_inc(ld_ffn, 16)
            act.dma_start(gate_b[:, E:WCOLS], t["L1_ffn_bt"].broadcast_to([S, 1])).then_inc(ld_ffn, 16)
            act.dma_start(b1[:, 1, :], t["b1_cols"]).then_inc(ld_ffn, 16)
            for b in range(B):
                act.dma_start(b2[b * E:(b + 1) * E, :], t["L1_ffn_b2"]).then_inc(ld_ffn, 16)
            for w, name in enumerate(("L1_attn_wq_b", "L1_attn_wk_b")):
                act.dma_start(sa_bias[:, w:w + 1], t[name]).then_inc(ld_sa, 16)
            act.dma_start(sa_bias[:, 3:4], t["L1_attn_wo_b"]).then_inc(ld_sa, 16)
            act.dma_start(sa_bv[:, :], t["sa_bv"].broadcast_to([128, D])).then_inc(ld_sa, 16)
            for w, name in enumerate(("xa1_q", "xa1_k", "xa1_v", "xa1_o")):
                act.dma_start(xa_w[:, w, :], t[name]).then_inc(ld_xa, 16)
            for w, name in ((0, "L1_xattn_b_q"), (1, "L1_xattn_b_k"), (3, "L1_xattn_b_o"),
                            (4, "L0_xattn_b_out")):
                act.dma_start(xa_bias[:, w:w + 1], t[name]).then_inc(ld_xa, 16)
            act.dma_start(xa_bv[:, :], t["xa_bv"].broadcast_to([128, D])).then_inc(ld_xa, 16)
            act.wait_ge(consts_set, 1)
            fold_scalar(act)
            norm_scalar(act, 0)
            self_scalar(act, 0)
            norm_scalar(act, 1)
            cross_scalar(act, 0)
            norm_scalar(act, 2)
            act.wait_ge(ld_ffn, 16 * FFN_LOADS)
            experts_scalar(act, 0)
            norm_scalar(act, 3)
            self_scalar(act, 1)
            norm_scalar(act, 4)
            act.wait_ge(ld_xa, 16 * XA_LOADS)
            cross_scalar(act, 1)
            norm_scalar(act, 5)
            experts_scalar(act, 1)

        @block.tensor
        def _(pe):
            pe.wait_ge(ld_const, 16 * CONST_LOADS)
            fold_tensor(pe)
            norm_tensor(pe, 0)
            self_tensor(pe, 0, 0)
            norm_tensor(pe, 1)
            cross_tensor(pe, 0, 1)
            norm_tensor(pe, 2)
            experts_tensor(pe, 0, 2)
            norm_tensor(pe, 3)
            self_tensor(pe, 1, 3)
            norm_tensor(pe, 4)
            cross_tensor(pe, 1, 4)
            norm_tensor(pe, 5)
            experts_tensor(pe, 1, 5)

        @block.vector
        def _(dve):
            chain = Chain()
            nc.vector.memset(b1[:, 0, :], 0.0)
            nc.vector.memset(ones[:, :], 1.0)
            nc.vector.memset(mean_w[:, :], 1.0 / D)
            nc.vector.memset(eps[:, :], EPS).then_inc(consts_set, 1)
            nc.vector.memset(prob[0][:, 0, :], 0.0).then_inc(consts_set, 1)
            dve.wait_ge(ld_x, 16)
            norm_vector(dve, 0, chain)
            dve.wait_ge(ld_sa, 16 * SA_LOADS)
            self_vector(dve, 0, chain)
            bias_vector(dve, chain)
            norm_vector(dve, 1, chain)
            dve.wait_ge(ld_xa, 16 * XA_LOADS)
            cross_vector(dve, 0, chain)
            norm_vector(dve, 2, chain)
            dve.wait_ge(ld_ffn, 16 * FFN_LOADS)
            experts_vector(dve, 0, chain)
            norm_vector(dve, 3, chain)
            self_vector(dve, 1, chain)
            norm_vector(dve, 4, chain)
            cross_vector(dve, 1, chain)
            norm_vector(dve, 5, chain)
            experts_vector(dve, 1, chain)


def kernel(**inputs):
    import concourse.bacc as bacc
    from concourse.bass_utils import run_bass_kernel_spmd

    x = {k: np.asarray(v) for k, v in inputs.items()}
    ch = np.arange(D)
    circ = (ch[None, :] - ch[:, None]) % D
    even = ch - ch % 2
    arrays = {
        "x_T": x["x"].transpose(2, 0, 1).reshape(D, NTOK),
        "ctx_1024": x["ctx_1024"],
        "ctx_T": x["ctx_1024"].transpose(0, 2, 1),
        "fside_SxS2_0": x["fside_SxS2_0"],
        "sa0_q": x["L0_attn_Wq"].T[:, even], "sa0_k": x["L0_attn_Wk"].T[:, even],
        "sa0_v": x["L0_attn_Wv"].T, "sa0_o": x["L0_attn_Wo"].T,
        "sa1_q": x["L1_attn_wq_c"][circ], "sa1_k": x["L1_attn_wk_c"][circ],
        "sa1_v": x["L1_attn_wv_c"][circ], "sa1_o": x["L1_attn_wo_c"][circ],
        "xa0_qT": x["L0_xattn_W_q"].T, "xa0_kT": x["L0_xattn_W_k"].T, "xa0_vT": x["L0_xattn_W_v"].T,
        "xa1_q": x["L1_xattn_W_q"].T, "xa1_k": x["L1_xattn_W_k"].T,
        "xa1_v": x["L1_xattn_W_v"].T, "xa1_o": x["L1_xattn_W_o"].T,
        "sa_bv": x["L1_attn_wv_b"][None, :], "xa_bv": x["L1_xattn_b_v"][None, :],
        "L1_ffn_bg": x["L1_ffn_bg"][None, :], "L1_ffn_bt": x["L1_ffn_bt"][None, :],
        "b1_cols": x["L1_ffn_b1"].reshape(E * NF, 128).T,
    }
    for name in ("L0_xattn_W_out", "L0_ffn_gate_w", "L0_ffn_w1", "L0_ffn_w2", "L1_ffn_Wg", "L1_ffn_Wt",
                 "L1_ffn_W1", "L1_ffn_W2", "L1_ffn_b2"):
        arrays[name] = x[name]
    for name in ("L1_attn_wq_b", "L1_attn_wk_b", "L1_attn_wo_b", "L1_xattn_b_q", "L1_xattn_b_k",
                 "L1_xattn_b_o", "L0_xattn_b_out"):
        arrays[name] = x[name][:, None]

    pos = np.arange(S, dtype=np.float32)
    freqs = np.exp(np.arange(0, HD, 2, dtype=np.float32) * np.float32(-math.log(10000.0) / HD))
    angle = (pos[None, :] * freqs[(ch % HD) // 2][:, None]).astype(np.float32)
    table = np.where((ch % 2 == 0)[:, None], np.cos(angle), -np.sin(angle)).astype(np.float32)
    arrays["rope"] = np.stack([table * np.float32(HD ** -0.5), table], 1)
    arrays["ident"] = np.eye(128, dtype=np.float32)
    arrays["head_mask"] = (ch[:, None] // HD == np.arange(NH)[None, :]).astype(np.float32)
    arrays["batch_mask"] = (ch[:, None] // E == np.arange(B)[None, :]).astype(np.float32)
    arrays["expert_mask"] = (ch[:, None] % E == np.arange(E)[None, :]).astype(np.float32)
    row, col = np.arange(128)[:, None] % 64, np.arange(HQ)[None, :]
    arrays["bias_sel"] = np.where(row == col % S, 2.0 ** -(col // S + 1.0), 0.0).astype(np.float32)
    arrays["quad_mask"] = (ch[:, None] // HD % 4 == np.arange(4)[None, :]).astype(np.float32)
    arrays = {f"in_{k}": np.ascontiguousarray(v) for k, v in arrays.items()}

    nc = bacc.Bacc("TRN2", target_bir_lowering=False, num_devices=1)
    t = {k[3:]: nc.dram_tensor(k, a.shape, mybir.dt.from_np(a.dtype), kind="ExternalInput").ap()
         for k, a in arrays.items()}
    out = nc.dram_tensor("out_0", (D, NTOK), mybir.dt.float32, kind="ExternalOutput").ap()
    decoder_kernel(nc, t, out)
    r = run_bass_kernel_spmd(nc, [arrays], core_ids=[0])
    y = r.results[0]["out_0"]
    return y.reshape(D, B, S).transpose(1, 2, 0)
```

```python
import math

import numpy as np

import concourse.bass as bass
from concourse import mybir
from contextlib import ExitStack

B, S, D = 16, 56, 128
NTOK = B * S
HALF = NTOK // 2
HB = B // 2
NH = 16
HQ = NH * S
NT = HQ // 128
HD = D // NH
XD = 64
S2 = 1500
KC = 125
NC = S2 // KC
KB = 500
NKB = S2 // KB
E = 8
FF = 512
NF = FF // 128
CAP = 2 * S // E
EPS = 1e-5
THRESHOLD = 0.125
TROWS = (128, 2 * S)
GROUPS = ((4, 3), (4, 4))
GA = 4
QUAD = 4 * HD
WCOLS = E + 1
HL_COLS = 4 * S2 + 4 * HQ + 2 * NC * 128 + 6 * 512 + S2 + HQ
CONST_LOADS = 6
SA_LOADS, XA_LOADS, FFN_LOADS = 12, 9, 6 + B


def decoder_kernel(nc, t, out):
    fp32, fp32r = mybir.dt.float32, mybir.dt.float32r
    ALU, ACT, AX = mybir.AluOpType, mybir.ActivationFunctionType, mybir.AxisListType.X

    ctx = ExitStack()
    with ctx:
        def sb(name, shape, dt=fp32):
            return ctx.enter_context(nc.sbuf_tensor(name, shape, dt))

        def sem(name):
            return ctx.enter_context(nc.semaphore(name))

        ident = sb("ident", [128, 128])
        ones = sb("ones", [128, 128])
        mean_w = sb("mean_w", [128, 128])
        eps = sb("eps", [128, 1])
        head_mask = sb("head_mask", [128, NH])
        batch_mask = sb("batch_mask", [128, B])
        expert_mask = sb("expert_mask", [128, E])
        rope = sb("rope", [128, 2, S])
        quad_mask = sb("quad_mask", [128, 4])
        sa_w = [sb(f"sa_w{l}", [128, 4, 128]) for l in range(2)]
        sa_bias = sb("sa_bias", [128, 4])
        sa_bv = sb("sa_bv", [128, D])
        vo_fold = sb("vo_fold", [128, NH, 128])
        xa_bq = sb("xa_bq", [3 * QUAD, 4])
        xa_w = sb("xa_w", [128, 4, 128])
        xa_bias = sb("xa_bias", [128, 5])
        xa_bv = sb("xa_bv", [128, D])
        gate_w = [sb(f"gate_w{l}", [128, WCOLS]) for l in range(2)]
        gate_b = sb("gate_b", [S, WCOLS])
        b1 = sb("b1", [128, 2, E * NF])
        b2 = sb("b2", [128, D])
        X = sb("X", [128, NTOK])
        QO = sb("QO", [128, B, HQ])
        ctxT = sb("ctxT", [128, S2])
        ctxV = sb("ctxV", [128, NC, 128])
        prob = [sb("prob_a", [128, 4, S2]), sb("prob_b", [128, 3, S2])]
        part_max = sb("part_max", [128, 2, NKB])
        neg_max = sb("neg_max", [128, 2 * GA])
        part_sum = sb("part_sum", [128, 2 * GA, NKB])
        row_sum = sb("row_sum", [128, 2 * GA])
        row_inv = sb("row_inv", [128, 2 * GA])
        inv_diag = [sb(f"inv_diag{i}", [128, 4, 128]) for i in range(2)]
        inv_cols = sb("inv_cols", [128, 512])
        pause = sb("pause", [128, 1])
        HL = sb("HL", [128, HL_COLS], fp32r)
        hl_taken = [0]

        def halved(rows, cols):
            at = hl_taken[0]
            hl_taken[0] += cols
            assert hl_taken[0] <= HL_COLS, hl_taken
            return HL[0:rows, at:at + cols]

        kH, kL, qH, qL = ([halved(128, n) for i in range(2)] for n in (S2, S2, HQ, HQ))
        vH, vL = (halved(128, NC * 128).rearrange("p (c d) -> p c d", c=NC) for i in range(2))
        pH, pL = ([halved(128, 512) for i in range(3)] for i in range(2))
        bias_rows = halved(128, S2)
        bias_sel = halved(128, HQ)
        w1 = [ctxT[:, i * FF:(i + 1) * FF] for i in range(2)]
        w2 = [ctxV[:, i * NF:(i + 1) * NF, :] for i in range(2)]
        k_now = vo_fold[:, :, :].rearrange("p h c -> p (h c)")[:, 4 * 128:4 * 128 + S2]
        hl_taken = [0]
        kH_flat, kL_flat = halved(128, S2), halved(128, S2)
        k_quad = [[halved(3 * QUAD, S2) for j in range(4)] for i in range(2)]
        q_quad_diag = [halved(3 * QUAD, HQ) for i in range(2)]

        hl_taken = [0]
        xn_hl = [halved(128, NTOK) for i in range(2)]
        w1_hl = [[halved(128, FF) for h in range(2)] for i in range(2)]
        w2_hl = [[halved(128, FF) for h in range(2)] for i in range(2)]
        hid_hl = [halved(128, NF * NTOK) for h in range(2)]
        w_blk_hl = [halved(128, NTOK) for h in range(2)]
        mask_cols = [halved(128, 128) for i in range(2)]

        def tile_prob(l, g, j):
            if l == 1 and g == 1 and j == 3:
                return ctxV[:, :, :].rearrange("p c d -> p (c d)")[0:TROWS[l], 0:S2]
            return prob[g][0:TROWS[l], j, :]

        hidden = prob[0][:, :, 0:NTOK]
        QO_flat = QO[:, :, :].rearrange("p b q -> p (b q)")
        taken = [0]

        def carve(rows, cols):
            at = taken[0]
            taken[0] += cols
            assert taken[0] <= B * HQ
            return QO_flat[0:rows, at:at + cols]

        q_all = carve(128, NTOK)
        out_q = carve(128, B * 4 * S)
        q_quad = carve(3 * QUAD, 4 * NTOK).rearrange("p (j t) -> p j t", j=4)
        q_diag1 = carve(3 * QUAD, HQ)
        wq_quad = carve(128, 4 * 3 * QUAD).rearrange("p (j r c) -> p j r c", j=4, r=3)
        vals = [carve(128, NC * 128).rearrange("p (c d) -> p c d", c=NC) for i in range(2)]
        pT = [carve(128, 512) for i in range(3)]
        taken = [NTOK]
        q_diag = [carve(128, HQ) for i in range(2)]
        k_all = carve(128, NTOK)
        att = carve(128, B * 4 * S)
        wo_quad = carve(128, 4 * 128).rearrange("p (r o) -> p r o", r=4)
        v_flat = carve(S, B * D)
        v_all = v_flat.rearrange("p (b d) -> p b d", b=B)
        v_now = [carve(S, D) for i in range(2)]
        sm_d = [carve(128, NT * S).rearrange("p (j s) -> p j s", j=NT) for i in range(2)]
        sm_p = [carve(128, 8 * 64) for i in range(2)]
        sm_pT = [carve(S, HQ) for i in range(2)]
        sm_stat = carve(128, 2 * 4 * NT).rearrange("p (i k j) -> p i k j", i=2, k=4)
        taken = [0]
        w_blk = carve(128, NTOK).rearrange("p (b s) -> p b s", b=B)
        w_cols = carve(128, 2 * NTOK).rearrange("p (a s) -> p a s", a=2)
        gate = carve(S, B * WCOLS).rearrange("p (b e) -> p b e", b=B)
        gate2 = carve(S, B * E).rearrange("p (b e) -> p b e", b=B)
        routed = carve(S, B * E).rearrange("p (b e) -> p b e", b=B)
        gate_stat = carve(S, 4 * B).rearrange("p (k b) -> p k b", k=4)
        gT = carve(128, S)
        work, work2 = carve(128, 64), carve(128, 64)
        top8 = carve(128, 16).rearrange("p (r t) -> p r t", r=2)
        w_be = carve(128, S)
        prob0, prob1 = (prob[g][:, :, :].rearrange("p j n -> p (j n)") for g in range(2))
        XC, SQ, XN = (prob1[:, i * NTOK:(i + 1) * NTOK] for i in range(3))
        qk_fold = prob0[:, S2 + HQ:S2 + HQ + NH * 128].rearrange("p (h c) -> p h c", h=NH)
        free = (ctxT[:, 0:1024], ctxV[:, :, :].rearrange("p c d -> p (c d)")[:, 0:1024],
                prob1[:, 3 * NTOK:3 * NTOK + 1024], prob0[:, S2 + HQ + NH * 128:S2 + HQ + NH * 128 + 1024])
        fold_in = [x.rearrange("p (g c) -> p g c", g=8) for x in free]

        PS = ctx.enter_context(nc.psum_tensor("PS", [128, 8, 512], fp32))
        PSF = PS[:, :, :].rearrange("p a b -> p (a b)")

        def two(bank):
            return PS[:, bank:bank + 2, 0:HALF]

        def half_of(x, h):
            return x[:, h * HALF:(h + 1) * HALF]

        def halves(x):
            return x.rearrange("p (a b) -> p a b", a=2)

        ld_x, ld_const, ld_sa, ld_fold, ld_xa, ld_ffn, ld_bias = (
            sem(n) for n in ("ld_x", "ld_const", "ld_sa", "ld_fold", "ld_xa", "ld_ffn", "ld_bias"))
        out_done = sem("out_done")
        consts_set = sem("consts_set")
        x_ready = sem("x_ready")
        ln_mean, ln_centred, ln_squared, ln_var, ln_std, xn_ready = (
            sem(n) for n in ("ln_mean", "ln_centred", "ln_squared", "ln_var", "ln_std", "xn_ready"))
        dve_step = sem("dve_step")
        pool_step = sem("pool_step")
        pool_count = [0]
        names = ("q v qkv diag wo scores sub exp norm tr vnow trc pv att out").split()
        sa = [{n: sem(f"sa{l}_{n}") for n in names} for l in range(2)]
        fold_mm, fold_ev = sem("fold_mm"), sem("fold_ev")
        bias_split = sem("bias_split")
        names = ("q scores mx exp tr trc pv idiag inv invc norm out "
                 "qh trh tra stack kspl vspl kmm kev vmm vev vo wo qp qpa qpd").split()
        xa = [{n: sem(f"xa{l}_{n}") for n in names} for l in range(2)]
        ld_k = [sem(f"ld_k{l}") for l in range(2)]
        ld_v = sem("ld_v")
        names = ("logit gexp gsub gates gtr blk xsp bsp w1sp w2sp wsel wmm wcols h hact hhi hlo y ymul b2mm").split()
        ff = [{n: sem(f"ff{l}_{n}") for n in names} for l in range(2)]
        ld_w = [[sem(f"ld_w{l}{i}") for i in range(2)] for l in range(2)]

        class Chain:
            def __init__(self):
                self.count = 0

            def link(self, eng, ins):
                ins.then_inc(dve_step, 1)
                self.count = self.count + 1
                eng.wait_ge(dve_step, self.count)

        def norm_tensor(pe, n):
            if n == 0:
                pe.wait_ge(ld_x, 16)
                pe.wait_ge(consts_set, 1)
            else:
                pe.wait_ge(x_ready, n)
            for h in range(2):
                nc.tensor.matmul(PS[:, h, 0:HALF], mean_w[:, :], half_of(X, h), start=True, stop=True)\
                    .then_inc(ln_mean, 1)
            for h in range(2):
                pe.wait_ge(ln_squared, 2 * n + h + 1)
                nc.tensor.matmul(PS[:, 2 + h, 0:HALF], mean_w[:, :], half_of(SQ, h), start=True, stop=True)\
                    .then_inc(ln_var, 1)

        def norm_scalar(act, n):
            for h in range(2):
                act.wait_ge(ln_centred, 2 * n + h + 1)
                nc.scalar.activation(half_of(SQ, h), half_of(XC, h), ACT.Square).then_inc(ln_squared, 1)
            for h in range(2):
                act.wait_ge(ln_var, 2 * n + h + 1)
                nc.scalar.activation(half_of(SQ, h), PS[:, 2 + h, 0:HALF], ACT.Sqrt, bias=eps[:, 0:1])\
                    .then_inc(ln_std, 1)

        def norm_vector(dve, n, chain):
            for h in range(2):
                dve.wait_ge(ln_mean, 2 * n + h + 1)
                nc.vector.tensor_tensor(half_of(XC, h), half_of(X, h), PS[:, h, 0:HALF], ALU.subtract)\
                    .then_inc(ln_centred, 1)
            for h in range(2):
                dve.wait_ge(ln_std, 2 * n + h + 1)
                chain.link(dve, nc.vector.reciprocal(half_of(SQ, h), half_of(SQ, h)))
                nc.vector.tensor_tensor(half_of(XN, h), half_of(XC, h), half_of(SQ, h), ALU.mult)\
                    .then_inc(xn_ready, 1)

        def wait_past(eng, signal, b, back):
            if not isinstance(b, int) or b >= back:
                eng.wait_ge(signal, b - (back - 1))

        def live(b):
            return not isinstance(b, int) or 0 <= b < B

        def rounds(eng, step):
            for i in range(4):
                step(i, i % 2)
            with eng.Fori(4, B - 3, 2) as i:
                step(i, 0)
                step(i + 1, 1)
            for i in range(B - 2, B + 2):
                step(i, i % 2)

        def self_tensor(pe, l, n):
            m = sa[l]
            if l == 0:
                pe.wait_ge(ld_sa, 16 * SA_LOADS)
            for h in range(2):
                pe.wait_ge(xn_ready, 2 * n + h + 1)
                for w in range(2):
                    mm = nc.tensor.matmul(PS[:, 2 * w + h, 0:HALF], sa_w[l][:, w, :], half_of(XN, h),
                                          start=True, stop=True)
                    if h == 1:
                        mm.then_inc(m["q"], 1)
            for b in range(B):
                mm = nc.tensor.matmul(PS[0:S, 4 + b // 4, (b % 4) * 128:(b % 4 + 1) * 128],
                                      XN[:, b * S:(b + 1) * S], sa_w[l][:, 2, :], start=True, stop=True)
            mm.then_inc(m["v"], 1)
            pe.wait_ge(m["qkv"], 3)

            def scores(b, p):
                wait_past(pe, m["sub"], b, 2)
                pe.wait_ge(m["diag"], b + 1)
                for j in range(NT):
                    mm = nc.tensor.matmul(PS[:, p, j * S:(j + 1) * S], q_diag[p][:, j * 128:(j + 1) * 128],
                                          k_all[:, bass.ds(b * S, S)], start=True, stop=True)
                mm.then_inc(m["scores"], 1)

            def turn(b, p):
                pe.wait_ge(m["norm"], b + 1)
                base = (2 + 2 * p) * 512
                for j in range((NT + 1) // 2):
                    mm = nc.tensor.transpose(PSF[:, base + j * 128:base + (j + 1) * 128],
                                             sm_p[p][:, j * 128:(j + 1) * 128], ident[:, :])
                mm.then_inc(m["tr"], 1)

            def await_values(b):
                pe.wait_ge(m["vnow"], b + 1)
                pe.wait_ge(m["trc"], 2 * b + 2)
                wait_past(pe, m["att"], b, 2)

            def values(b, p):
                for j in range(4):
                    r = slice(32 * j, 32 * j + 32)
                    mm = nc.tensor.matmul(PS[r, 6 + p, 0:4 * S], v_now[p][:, r],
                                          sm_pT[p][:, j * 4 * S:(j + 1) * 4 * S], start=True, stop=True)
                mm.then_inc(m["pv"], 1)

            scores(0, 0)
            scores(1, 1)

            def step(i, p):
                if live(i + 2):
                    scores(i + 2, p)
                if live(i - 2):
                    await_values(i - 2)
                if live(i - 1):
                    turn(i - 1, 1 - p)
                if live(i - 2):
                    values(i - 2, p)

            rounds(pe, step)
            pe.wait_ge(m["att"], B)
            pe.wait_ge(m["wo"], 1)
            for r in range(4):
                for a in range(2):
                    x = att.rearrange("p (b q) -> p b q", b=B)[:, a * HB:(a + 1) * HB, r * S:(r + 1) * S]
                    mm = nc.tensor.matmul(PS[:, a, 0:HALF], wo_quad[:, r, :], x, start=r == 0, stop=r == 3)
            mm.then_inc(m["out"], 1)

        def self_gpsimd(pool, l):
            m = sa[l]

            def diagonal(b, p):
                wait_past(pool, m["scores"], b, 2)
                q = q_all[:, bass.ds(b * S, S)].rearrange("p (a q) -> p a q", a=1)
                nc.gpsimd.tensor_tensor(
                    q_diag[p][:, :].rearrange("p (h q) -> p h q", h=NH), q.broadcast_to([128, NH, S]),
                    head_mask[:, :].rearrange("p (h a) -> p h a", a=1).broadcast_to([128, NH, S]),
                    ALU.mult).then_inc(m["diag"], 1)

            pool.wait_ge(m["qkv"], 1)
            diagonal(0, 0)
            diagonal(1, 1)
            pool.wait_ge(ld_sa, 16 * SA_LOADS)
            pool.wait_ge(m["qkv"], 3)
            nc.gpsimd.tensor_tensor(
                wo_quad,
                sa_w[l][:, 3, :].rearrange("p (a o) -> p a o", a=1).broadcast_to([128, 4, 128]),
                quad_mask[:, :].rearrange("p (h a) -> p h a", a=1).broadcast_to([128, 4, 128]),
                ALU.mult).then_inc(m["wo"], 1)
            with pool.Fori(2, B - 1, 2) as i:
                for k in range(2):
                    diagonal(i + k, k)

        def self_scalar(act, l):
            m = sa[l]

            def exps(b, p):
                act.wait_ge(m["sub"], b + 1)
                wait_past(act, m["norm"], b, 2)
                nc.scalar.activation(sm_d[p][:, :, :], sm_d[p][:, :, :], ACT.Exp).then_inc(m["exp"], 1)

            def copy_probs(b, p):
                act.wait_ge(m["tr"], b + 1)
                wait_past(act, m["pv"], b, 2)
                base = (2 + 2 * p) * 512
                tiles = sm_pT[p].rearrange("p (j c) -> p j c", j=NT)
                for odd in range(2):
                    n = (NT + 1 - odd) // 2
                    nc.scalar.activation(tiles[:, odd:NT:2, :],
                                         PSF[64 * odd:64 * odd + S, base:base + n * 128]
                                         .rearrange("p (j c) -> p j c", j=n), ACT.Copy).then_inc(m["trc"], 1)

            def take_values(b, p):
                wait_past(act, m["pv"], b, 2)
                nc.scalar.activation(v_now[p][:, :], v_flat[:, bass.ds(b * D, D)], ACT.Copy).then_inc(m["vnow"], 1)

            def copy_out(b, p):
                act.wait_ge(m["pv"], b + 1)
                nc.scalar.activation(att[:, bass.ds(b * 4 * S, 4 * S)], PS[:, 6 + p, 0:4 * S], ACT.Copy)\
                    .then_inc(m["att"], 1)

            act.wait_ge(m["qkv"], 3)
            exps(0, 0)

            def step(i, p):
                if live(i + 1):
                    exps(i + 1, 1 - p)
                if live(i - 2):
                    copy_out(i - 2, p)
                if live(i - 1):
                    take_values(i - 1, 1 - p)
                    copy_probs(i - 1, 1 - p)

            rounds(act, step)

        def self_vector(dve, l, chain):
            m = sa[l]
            for p in range(2):
                chain.link(dve, nc.vector.memset(sm_p[p][:, :], 0.0))
            dve.wait_ge(m["q"], 1)
            if l == 0:
                dve.wait_ge(ld_const, 16 * CONST_LOADS)
                for w, x in ((0, q_all), (1, k_all)):
                    if w == 1:
                        dve.wait_ge(m["q"], 2)
                    table = rope[:, w, :].rearrange("p (a s) -> p a s", a=1).broadcast_to([128, HB, S])
                    for h in range(2):
                        ins = nc.vector.tensor_tensor(
                            x[:, h * HALF:(h + 1) * HALF].rearrange("p (b s) -> p b s", b=HB),
                            PS[:, 2 * w + h, 0:HALF].rearrange("p (b s) -> p b s", b=HB), table, ALU.mult)
                    ins.then_inc(m["qkv"], 1)
            else:
                nc.vector.tensor_scalar(halves(q_all[:, :]), two(0), sa_bias[:, 0:1], HD ** -0.5,
                                        ALU.add, ALU.mult).then_inc(m["qkv"], 1)
                dve.wait_ge(m["q"], 2)
                nc.vector.tensor_scalar(halves(k_all[:, :]), two(2), sa_bias[:, 1:2], None, ALU.add)\
                    .then_inc(m["qkv"], 1)
            dve.wait_ge(m["v"], 1)
            v_psum = PSF[0:S, 4 * 512:8 * 512].rearrange("p (b d) -> p b d", b=B)
            if l == 0:
                nc.vector.tensor_copy(v_all[:, :, :], v_psum).then_inc(m["qkv"], 1)
            else:
                nc.vector.tensor_tensor(
                    v_all[:, :, :], v_psum,
                    sa_bv[0:S, :].rearrange("p (a d) -> p a d", a=1).broadcast_to([S, B, D]),
                    ALU.add).then_inc(m["qkv"], 1)

            def stat(p, k):
                return sm_stat[:, p, k, :]

            def spread(x):
                return x.rearrange("p (j a) -> p j a", a=1).broadcast_to([128, NT, S])

            def centre(b, p):
                dve.wait_ge(m["scores"], b + 1)
                sc = PS[:, p, 0:NT * S].rearrange("p (j k) -> p j k", j=NT)
                chain.link(dve, nc.vector.tensor_reduce(stat(p, 0), sc, AX, ALU.max))
                wait_past(dve, m["norm"], b, 2)
                nc.vector.tensor_tensor(sm_d[p][:, :, :], sc, spread(stat(p, 0)), ALU.subtract)\
                    .then_inc(m["sub"], 1)

            def normalise(b, p):
                dve.wait_ge(m["exp"], b + 1)
                chain.link(dve, nc.vector.tensor_reduce(stat(p, 1), sm_d[p][:, :, :], AX, ALU.add))
                chain.link(dve, nc.vector.reciprocal(stat(p, 2), stat(p, 1)))
                wait_past(dve, m["tr"], b, 2)
                nc.vector.tensor_tensor(sm_p[p].rearrange("p (j s) -> p j s", j=8)[:, 0:NT, 0:S],
                                        sm_d[p][:, :, :], spread(stat(p, 2)), ALU.mult)\
                    .then_inc(m["norm"], 1)

            centre(0, 0)
            start = chain.count

            def step(i, p):
                if live(i):
                    chain.count = i * 3 + start
                if live(i + 1):
                    centre(i + 1, 1 - p)
                if live(i):
                    normalise(i, p)

            rounds(dve, step)
            dve.wait_ge(m["out"], 1)
            if l == 0:
                nc.vector.tensor_tensor(halves(X[:, :]), halves(X[:, :]), two(0), ALU.add).then_inc(x_ready, 1)
            else:
                nc.vector.scalar_tensor_tensor(halves(X[:, :]), two(0), sa_bias[:, 3:4], halves(X[:, :]),
                                               ALU.add, ALU.add).then_inc(x_ready, 1)

        def fold_tensor(pe):
            pe.wait_ge(ld_fold, 16 * 4)
            for k in range(8):
                odd, w = k // 2 % 2, 2 * (k // 4)
                r = slice(XD * odd, XD * odd + XD)
                wait_past(pe, fold_ev, k, 4)
                for j in range(4):
                    pair = 4 * (k % 2) + j
                    mm = nc.tensor.matmul(PS[:, 4 + k % 4, j * 128:(j + 1) * 128], fold_in[w][r, pair, :],
                                          fold_in[w + 1][r, pair, :], start=True, stop=True)
                mm.then_inc(fold_mm, 1)

        def fold_scalar(act):
            for k in range(8):
                act.wait_ge(fold_mm, k + 1)
                dst = (qk_fold, vo_fold)[k // 4][:, :, :].rearrange("p (g a) c -> p a g c", a=2)
                nc.scalar.activation(dst[:, k // 2 % 2, 4 * (k % 2):4 * (k % 2) + 4, :],
                                     PS[:, 4 + k % 4, :].rearrange("p (h c) -> p h c", h=4), ACT.Copy,
                                     scale=XD ** -0.5 if k < 4 else 1.0).then_inc(fold_ev, 1)

        def bias_vector(dve, chain):
            f, s = prob0[:, 0:S2], prob0[:, S2:S2 + HQ]
            dve.wait_ge(ld_bias, 48)
            nc.vector.tensor_copy(bias_sel, s)
            chain.link(dve, nc.vector.tensor_copy(bias_rows, f))
            nc.vector.tensor_tensor(bias_rows[64:128, :], f[64:128, :], bias_rows[64:128, :].bitcast(fp32),
                                    ALU.subtract).then_inc(bias_split, 1)

        def by_scalar(g, k):
            return k % 3 == 0 or g == 0 and k % 3 == 2

        def slot_chunks(l, s):
            if s < GA:
                return 1, range(3 * s, 3 * s + 3)
            n = NC // GROUPS[l][1]
            return 0, range(n * (s - GA), n * (s - GA) + n)

        def copied(m, b, g, k):
            mine = [(h, c) for h in range(2) for c in range(NC) if by_scalar(h, c) == by_scalar(g, k)]
            return m["tra" if by_scalar(g, k) else "trc"], len(mine) * b + mine.index((g, k)) + 1

        def cross_tensor(pe, l, n):
            m = xa[l]
            tiles = sum(GROUPS[l])
            def project(b, par, piece):
                if piece == 0:
                    pe.wait_ge(ld_k[1], (b + 1) * 16)
                    wait_past(pe, m["invc"], 2 * b, 4)
                    if not isinstance(b, int) or b:
                        pe.wait_ge(m["vev"], 3 * b)
                if piece == 3:
                    wait_past(pe, m["invc"], 2 * b, 3)
                if piece < 3:
                    if piece:
                        pe.wait_ge(m["kev"], 3 * b + piece)
                    nc.tensor.matmul(PS[:, 7, 0:KB], xa_w[:, 1, :], ctxT[:, piece * KB:(piece + 1) * KB],
                                     start=True, stop=True).then_inc(m["kmm"], 1)
                else:
                    if piece == 3:
                        pe.wait_ge(m["kev"], 3 * b + 3)
                    else:
                        pe.wait_ge(m["vev"], 3 * b + piece - 3)
                    for j in range(4):
                        c = 4 * (piece - 3) + j
                        mm = nc.tensor.matmul(PS[0:KC, 7, j * 128:(j + 1) * 128],
                                              ctxT[:, c * KC:(c + 1) * KC], xa_w[:, 2, :],
                                              start=True, stop=True)
                    mm.then_inc(m["vmm"], 1)

            def scores(b, par, s, j):
                if s == 0 and j == 0:
                    pe.wait_ge(m["q"], 2 * b + 2 if l == 0 else b + 1)
                    if l == 0:
                        pe.wait_ge(m["kspl"], b + 1)
                    else:
                        pe.wait_ge(m["stack"], 12 * 16 * b + 12 * 16)
                rows = slice(s * TROWS[l], (s + 1) * TROWS[l])
                cols = slice(j * KB, (j + 1) * KB)
                dst = PS[0:TROWS[l], j, 0:KB]
                wait_past(pe, m["exp"], NKB * (tiles * b + s) + j, NKB)
                if l == 0:
                    nc.tensor.matmul(dst, qH[par][:, rows], kH[par][:, cols], start=True, stop=False)
                    nc.tensor.matmul(dst, qH[par][:, rows], kL[par][:, cols], start=False, stop=False)
                    nc.tensor.matmul(dst, qL[par][:, rows], kH[par][:, cols], start=False, stop=False)
                    mm = nc.tensor.matmul(dst, bias_sel[:, rows], bias_rows[:, cols], start=False, stop=True)
                else:
                    mm = nc.tensor.matmul(dst, q_quad_diag[par][:, rows], k_quad[par][s % 4][:, cols],
                                          start=True, stop=True)
                mm.then_inc(m["scores"], 1)

            def transposes(b, g, k):
                at = 2 * NC * b + NC * g + k
                size, n = GROUPS[l][g], TROWS[l]
                if k == 0:
                    pe.wait_ge(m["exp"], NKB * (tiles * b + (GA if g == 0 else tiles)))
                if l == 0:
                    wait_past(pe, m["trc"], at, 2)
                elif k >= 2:
                    pe.wait_ge(*copied(m, b, g, k - 2))
                elif g == 1:
                    pe.wait_ge(*copied(m, b, 0, k - 2 + NC))
                elif not isinstance(b, int) or b:
                    pe.wait_ge(*copied(m, b - 1, 1, k - 2 + NC))
                for j in range(size):
                    mm = nc.tensor.transpose(PS[0:KC, 3 + k % 2, j * n:(j + 1) * n],
                                             tile_prob(l, g, j)[:, k * KC:(k + 1) * KC], ident[0:n, 0:n])
                mm.then_inc(m["tr"], 1)

            def product(b, par, g, k):
                at = 2 * NC * b + NC * g + k
                size = GROUPS[l][g]
                if k == 0:
                    wait_past(pe, m["norm"], 2 * b + g, 2)
                if l == 0:
                    if g == 0 and k % 4 == 0:
                        pe.wait_ge(m["vspl"], 3 * b + k // 4 + 1)
                    pe.wait_ge(m["trc"], at + 1)
                    dst, n, p = PS[:, 5 + g, 0:128 * size], 128 * size, k % 3
                    v_hi, v_lo = vH[0:KC, k, :], vL[0:KC, k, :]
                    p_hi, p_lo = pH[p][0:KC, 0:n], pL[p][0:KC, 0:n]
                    nc.tensor.matmul(dst, v_hi, p_hi, start=k == 0, stop=False)
                    nc.tensor.matmul(dst, v_lo, p_hi, start=False, stop=False)
                    mm = nc.tensor.matmul(dst, v_hi, p_lo, start=False, stop=k == NC - 1)
                else:
                    if g == 0 and k == 0:
                        pe.wait_ge(m["vev"], 3 * b + 3)
                    pe.wait_ge(*copied(m, b, g, k))
                    n = TROWS[l]
                    for j in range(4):
                        r = slice(32 * j, 32 * j + 32)
                        mm = nc.tensor.matmul(PS[r, 5 + g, 0:n], vals[par][0:KC, k, r],
                                              pT[k % 3][0:KC, j * n:(j + 1) * n], start=k == 0, stop=k == NC - 1)
                mm.then_inc(m["pv"], 1)

            def sums(b, g):
                size = GROUPS[l][g]
                pe.wait_ge(m["idiag"], 2 * b + g + 1)
                wait_past(pe, m["invc"], 2 * b + g, 1)
                if l == 1 and not (isinstance(b, int) and b + (2 if g else 1) >= B):
                    pe.wait_ge(m["kev" if g else "vev"], 3 * b + (9 if g else 6))
                if l == 0:
                    mm = nc.tensor.matmul(PS[:, 7, 0:128 * size], ones[:, :],
                                          inv_diag[g][:, 0:size, :].rearrange("p a b -> p (a b)"),
                                          start=True, stop=True)
                else:
                    n, cols = TROWS[l], inv_diag[g][:, :, :].rearrange("p a b -> p (a b)")
                    for j in range(4):
                        mm = nc.tensor.matmul(PS[32 * j:32 * j + 32, 7, 0:n], ones[0:n, 0:32],
                                              cols[0:n, j * n:(j + 1) * n], start=True, stop=True)
                mm.then_inc(m["inv"], 1)

            def products(b, par, g, k, first):
                if k >= 2:
                    product(b, par, g, k - 2)
                elif not first:
                    pb, pp, pg = (b, par, 0) if g else (b - 1, 1 - par, 1)
                    product(pb, pp, pg, NC - 2 + k)
                    if k == 1:
                        sums(pb, pg)

            def batch(b, par):
                first = isinstance(b, int) and b == 0
                last = isinstance(b, int) and b == B - 1
                for s in range(tiles):
                    g, ks = slot_chunks(l, s)
                    at = (b, par, 0) if g == 0 else (b - 1, 1 - par, 1)
                    if g == 1 and first:
                        ks = ()
                    skip = first and g == 0
                    scores(b, par, s, 0)
                    if l == 0 or not ks:
                        scores(b, par, s, 1)
                        scores(b, par, s, 2)
                        for k in ks:
                            transposes(at[0], g, k)
                            products(*at, k, skip)
                    elif ks[0] > 0:
                        for i, k in enumerate(ks):
                            transposes(at[0], g, k)
                            if i < 2:
                                scores(b, par, s, i + 1)
                            products(*at, k, skip)
                    else:
                        for k in range(2):
                            products(*at, k, skip)
                            scores(b, par, s, k + 1)
                        for k in ks:
                            transposes(at[0], g, k)
                        products(*at, 2, skip)
                    if l == 1 and not last and s not in (3, 7):
                        project(b + 1, 1 - par, s if s < 3 else s - 1)

            if l == 1:
                pe.wait_ge(ld_xa, 16 * XA_LOADS)
                for piece in range(3):
                    project(0, 0, piece)
            pe.wait_ge(xn_ready, 2 * n + 2)
            if l == 0:
                pe.wait_ge(fold_ev, 8)
                for h in range(NH):
                    p = h % 2
                    if h >= 2:
                        pe.wait_ge(m["qpa" if p == 0 else "qpd"], h // 2)
                    for a in range(2):
                        mm = nc.tensor.matmul(PS[:, 2 * p + a, 0:HALF], qk_fold[:, h, :],
                                              XN[:, a * HALF:(a + 1) * HALF], start=True, stop=True)
                    mm.then_inc(m["qp"], 1)
                pe.wait_ge(m["qpa"], NH // 2)
                pe.wait_ge(m["qpd"], NH // 2)
                pe.wait_ge(bias_split, 1)
            else:
                pe.wait_ge(m["vo"], 1)
                for j in range(4):
                    if j == 3:
                        pe.wait_ge(m["kev"], NKB)
                    for a in range(2):
                        mm = nc.tensor.matmul(PS[0:3 * QUAD, 2 * j + a, 0:HALF],
                                              wq_quad[:, j, :, :].rearrange("p r c -> p (r c)"),
                                              XN[:, a * HALF:(a + 1) * HALF], start=True, stop=True)
                    mm.then_inc(m["qp"], 1)
                pe.wait_ge(m["qpd"], 4)
                for piece in range(3, 6):
                    project(0, 0, piece)
            batch(0, 0)
            batch(1, 1)
            batch(2, 0)
            with pe.Fori(3, B - 2, 2) as i:
                batch(i, 1)
                batch(i + 1, 0)
            batch(B - 1, 1)
            for k in range(NC):
                transposes(B - 1, 1, k)
                products(B - 1, 1, 1, k, False)
            product(B - 1, 1, 1, NC - 2)
            product(B - 1, 1, 1, NC - 1)
            sums(B - 1, 1)
            if l == 1:
                pe.wait_ge(m["wo"], 1)
            parts = NH if l == 0 else 4
            for a in range(2):
                pe.wait_ge(m["norm"], 2 * HB * (a + 1))
                for h in range(parts):
                    if l == 0:
                        x = QO[:, a * HB:(a + 1) * HB, h * S:(h + 1) * S]
                    else:
                        x = out_q.rearrange("p (b q) -> p b q", b=B)[:, a * HB:(a + 1) * HB, h * S:(h + 1) * S]
                    mm = nc.tensor.matmul(PS[:, a, 0:HALF], vo_fold[:, h, :], x,
                                          start=h == 0, stop=h == parts - 1)
            mm.then_inc(m["out"], 1)

        def cross_gpsimd(pool, l):
            m = xa[l]
            tiles = sum(GROUPS[l])
            if l == 1:
                pool.wait_ge(x_ready, 2)
                pool.wait_ge(ld_xa, 16 * XA_LOADS)
                nc.gpsimd.tensor_tensor(
                    vo_fold[:, 0:4, :],
                    xa_w[:, 3, :].rearrange("p (a o) -> p a o", a=1).broadcast_to([128, 4, 128]),
                    quad_mask[:, :].rearrange("p (h a) -> p h a", a=1).broadcast_to([128, 4, 128]),
                    ALU.mult).then_inc(m["wo"], 1)
            steps = [0]

            def once(x):
                o = ones[0:x.shape[0], 0:1]
                if len(x.shape) == 3:
                    o = o.rearrange("p (a b) -> p a b", a=1)
                return o.broadcast_to(list(x.shape))

            def link(ins):
                ins.then_inc(pool_step, 1)
                pool_count[0] = pool_count[0] + 1
                steps[0] += 1
                pool.wait_ge(pool_step, pool_count[0])

            def halve(hi, lo, x, last):
                link(nc.gpsimd.tensor_tensor(hi, x, once(x), ALU.mult))
                nc.gpsimd.tensor_tensor(lo, x, hi.bitcast(fp32), ALU.subtract).then_inc(last, 1)

            def queries(b, par):
                wait_past(pool, m["scores"], NKB * tiles * b, NKB * tiles + 1)
                if l == 0:
                    nc.gpsimd.tensor_copy(qH[par], QO_flat[:, bass.ds(b * HQ, HQ)]).then_inc(m["qh"], 1)
                else:
                    q = q_quad[:, :, bass.ds(b * S, S)].rearrange("p j (a q) -> p j a q", a=1)
                    link(nc.gpsimd.tensor_tensor(
                        q_diag1.rearrange("p (j r q) -> p j r q", j=4, r=4), q.broadcast_to([3 * QUAD, 4, 4, S]),
                        quad_mask[0:3 * QUAD, :].rearrange("p (j r a) -> p j r a", j=1, a=1)
                        .broadcast_to([3 * QUAD, 4, 4, S]), ALU.mult))
                    by_tile = q_diag1.rearrange("p (j g c) -> p g j c", j=4, g=2)
                    dst = q_quad_diag[par].rearrange("p (g j c) -> p g j c", g=2, j=4)
                    for g in range(2):
                        ins = nc.gpsimd.tensor_tensor(dst[:, g, :, :], by_tile[:, g, :, :],
                                                      once(by_tile[:, g, :, :]), ALU.mult)
                    link(ins)
                    for g in range(2):
                        low = slice(QUAD, 2 * QUAD)
                        ins = nc.gpsimd.tensor_tensor(dst[low, g, :, :], by_tile[low, g, :, :],
                                                      dst[low, g, :, :].bitcast(fp32), ALU.subtract)
                    ins.then_inc(m["q"], 1)
                    pool.wait_ge(m["q"], b + 1)

            def keys(b, par):
                if l == 0:
                    pool.wait_ge(ld_k[0], (b + 1) * 16)
                    halve(kH[par], kL[par], ctxT[:, :], m["kspl"])
                else:
                    wait_past(pool, m["stack"], 12 * 16 * b, 1)
                    for piece in range(NKB):
                        pool.wait_ge(m["kev"], NKB * b + piece + 1)
                        c = slice(piece * KB, (piece + 1) * KB)
                        halve(kH_flat[:, c], kL_flat[:, c], k_now[:, c], m["kspl"])
                    pool.wait_ge(m["kspl"], NKB * b + NKB)
                    nc.gpsimd.tensor_tensor(pause[:, :], ones[:, 0:1], ones[:, 0:1], ALU.mult)
                    for j in range(4):
                        for r, half in enumerate((kH_flat, kH_flat, kL_flat)):
                            nc.gpsimd.dma_start(k_quad[par][j][r * QUAD:(r + 1) * QUAD, :],
                                                half[j * QUAD:(j + 1) * QUAD, :]).then_inc(m["stack"], 16)

            def context(b):
                pool.wait_ge(ld_v, (b + 1) * 16)
                for i in range(3):
                    wait_past(pool, m["pv"], 2 * NC * b + 4 * i, 9)
                    c = slice(4 * i, 4 * i + 4)
                    halve(vH[0:KC, c, :], vL[0:KC, c, :], ctxV[0:KC, c, :], m["vspl"])

            def batch(b, par):
                if not (isinstance(b, int) and b == B - 1):
                    queries(b + 1, 1 - par)
                    keys(b + 1, 1 - par)
                if l == 0:
                    context(b)

            keys(0, 0)
            if l == 0:
                pool.wait_ge(m["qpa"], NH // 2)
                pool.wait_ge(m["qpd"], NH // 2)
            else:
                pool.wait_ge(m["qpd"], 4)
            queries(0, 0)
            batch(0, 0)
            batch(1, 1)
            batch(2, 0)
            steps[0] = 0
            start = pool_count[0]
            per_batch = 4 if l == 0 else 5
            with pool.Fori(3, B - 2, 2) as i:
                pool_count[0] = (i - 3) * per_batch + start
                batch(i, 1)
                batch(i + 1, 0)
            assert steps[0] == 2 * per_batch
            pool_count[0] = start + per_batch * (B - 4)
            batch(B - 1, 1)

        def cross_sync(sp, l):
            m = xa[l]

            def load(b):
                if l == 0:
                    wait_past(sp, m["kspl"], b, 1)
                else:
                    wait_past(sp, m["vmm"], 3 * b, 1)
                sp.dma_start(ctxT[:, :], t["ctx_T"][bass.ds(b, 1), :, :].rearrange("a p n -> (a p) n"))\
                    .then_inc(ld_k[l], 16)
                if l == 0:
                    wait_past(sp, m["vspl"], 3 * b, 1)
                    sp.dma_start(ctxV[0:KC, :, :],
                                 t["ctx_1024"][bass.ds(b, 1), :, :].rearrange("a (c p) d -> (a p) c d", p=KC))\
                        .then_inc(ld_v, 16)

            if l == 0:
                sp.wait_ge(fold_mm, 8)
            else:
                sp.wait_ge(x_ready, 3)
            load(0)
            with sp.Fori(1, B) as i:
                load(i)

        def cross_scalar(act, l):
            m = xa[l]
            tiles = sum(GROUPS[l])
            if l == 0:
                for h in range(0, NH, 2):
                    act.wait_ge(m["qp"], h + 1)
                    for a in range(2):
                        ins = nc.scalar.activation(
                            QO[:, a * HB:(a + 1) * HB, h * S:(h + 1) * S],
                            PS[:, a, 0:HALF].rearrange("p (b s) -> p b s", b=HB), ACT.Copy)
                    ins.then_inc(m["qpa"], 1)

            def keys(b, piece):
                act.wait_ge(m["kmm"], NKB * b + piece + 1)
                if piece == 0:
                    wait_past(act, m["kspl"], NKB * b, 1)
                nc.scalar.activation(k_now[:, piece * KB:(piece + 1) * KB], PS[:, 7, 0:KB], ACT.Identity,
                                     bias=xa_bias[:, 1:2]).then_inc(m["kev"], 1)

            def copy_chunk(b, g, k):
                if l == 1 and not by_scalar(g, k):
                    return
                at = 2 * NC * b + NC * g + k
                n = TROWS[l] * GROUPS[l][g]
                act.wait_ge(m["tr"], at + 1)
                wait_past(act, m["pv"], at, 3)
                if l == 0:
                    nc.scalar.activation(pH[k % 3][0:KC, 0:n], PS[0:KC, 3 + k % 2, 0:n], ACT.Copy)\
                        .then_inc(m["trh"], 1)
                else:
                    nc.scalar.activation(pT[k % 3][0:KC, 0:n], PS[0:KC, 3 + k % 2, 0:n], ACT.Copy)\
                        .then_inc(m["tra"], 1)

            def exps(b, s, j):
                g = 0 if s < GA else 1
                if j == 0:
                    act.wait_ge(m["mx"], tiles * b + s + 1)
                    if s == 0:
                        wait_past(act, m["tr"], 2 * NC * b, 1 + NC)
                    if s == GA:
                        wait_past(act, m["tr"], 2 * NC * b, 1)
                    if s == 0 or s == GA:
                        wait_past(act, m["idiag"], 2 * b + g, 2)
                r = slice(0, TROWS[l])
                nc.scalar.activation(tile_prob(l, g, s - GA * g)[:, j * KB:(j + 1) * KB], PS[r, j, 0:KB], ACT.Exp,
                                     bias=neg_max[r, s:s + 1],
                                     accum_out=part_sum[r, s, j:j + 1]).then_inc(m["exp"], 1)

            def copy_inv(b, g):
                n = 128 * GROUPS[l][g] if l == 0 else TROWS[l]
                act.wait_ge(m["inv"], 2 * b + g + 1)
                wait_past(act, m["norm"], 2 * b + g, 1)
                nc.scalar.activation(inv_cols[:, 0:n], PS[:, 7, 0:n], ACT.Copy).then_inc(m["invc"], 1)

            def chunk(b, g, k, first):
                if l == 1 and k == 0 and not first:
                    copy_inv(*((b, 0) if g else (b - 1, 1)))
                copy_chunk(b, g, k)
                if l == 0 and k == 1 and not first:
                    copy_inv(*((b, 0) if g else (b - 1, 1)))

            def batch(b, par):
                first = isinstance(b, int) and b == 0
                last = isinstance(b, int) and b == B - 1
                for s in range(tiles):
                    g, ks = slot_chunks(l, s)
                    if g == 0:
                        todo = [(b, 0, k, first) for k in ks]
                    else:
                        todo = [] if first else [(b - 1, 1, k, False) for k in ks]
                    early = 3 if l == 1 and ks[0] > 0 else 1
                    for c in todo[:early]:
                        chunk(*c)
                    exps(b, s, 0)
                    for c in todo[early:2]:
                        chunk(*c)
                    exps(b, s, 1)
                    for c in todo[max(early, 2):3]:
                        chunk(*c)
                    exps(b, s, 2)
                    if l == 1 and not last and s < 3:
                        keys(b + 1, s)
                    for c in todo[max(early, 3):]:
                        chunk(*c)

            if l == 1:
                for piece in range(3):
                    keys(0, piece)
            batch(0, 0)
            batch(1, 1)
            batch(2, 0)
            with act.Fori(3, B - 2, 2) as i:
                batch(i, 1)
                batch(i + 1, 0)
            batch(B - 1, 1)
            for k in range(NC):
                chunk(B - 1, 1, k, False)
            copy_inv(B - 1, 1)

        def cross_vector(dve, l, chain):
            m = xa[l]
            tiles = sum(GROUPS[l])
            if l == 0:
                for h in range(1, NH, 2):
                    dve.wait_ge(m["qp"], h + 1)
                    for a in range(2):
                        ins = nc.vector.tensor_copy(
                            QO[:, a * HB:(a + 1) * HB, h * S:(h + 1) * S],
                            PS[:, 2 + a, 0:HALF].rearrange("p (b s) -> p b s", b=HB))
                    ins.then_inc(m["qpd"], 1)
            else:
                nc.vector.tensor_copy(wq_quad, xa_w[:, 0, :].rearrange("p (j a c) -> p j a c", j=4, a=1)
                                      .broadcast_to([128, 4, 3, QUAD])).then_inc(m["vo"], 1)
                for j in range(4):
                    dve.wait_ge(m["qp"], j + 1)
                    nc.vector.tensor_scalar(halves(q_quad[:, j, :]), PS[0:3 * QUAD, 2 * j:2 * j + 2, 0:HALF],
                                            xa_bq[:, j:j + 1], HD ** -0.5, ALU.add, ALU.mult)\
                        .then_inc(m["qpd"], 1)

            def values(b, par, piece):
                dve.wait_ge(m["vmm"], 3 * b + piece + 1)
                if piece == 0:
                    wait_past(dve, m["pv"], 2 * NC * b, 2 * NC + 1)
                nc.vector.tensor_tensor(
                    vals[par][0:KC, 4 * piece:4 * piece + 4, :],
                    PS[0:KC, 7, :].rearrange("p (c d) -> p c d", c=4),
                    xa_bv[0:KC, :].rearrange("p (a d) -> p a d", a=1).broadcast_to([KC, 4, D]),
                    ALU.add).then_inc(m["vev"], 1)

            def maxima(b, s):
                r = slice(0, TROWS[l])
                for j in range(NKB):
                    dve.wait_ge(m["scores"], NKB * (tiles * b + s) + j + 1)
                    ins = nc.vector.tensor_reduce(part_max[r, s % 2, j:j + 1], PS[r, j, 0:KB], AX, ALU.max)
                    if j < NKB - 1:
                        ins.then_inc(dve_step, 1)
                        chain.count = chain.count + 1
                chain.link(dve, ins)
                wait_past(dve, m["exp"], NKB * (tiles * b + s) + NKB - 1, NKB * tiles)
                nc.vector.tensor_reduce(neg_max[r, s:s + 1], part_max[r, s % 2, :], AX, ALU.max, negate=True)\
                    .then_inc(m["mx"], 1)

            def copy_chunk(b, g, k):
                at = 2 * NC * b + NC * g + k
                n = TROWS[l] * GROUPS[l][g]
                if l == 0:
                    dve.wait_ge(m["trh"], at + 1)
                    wait_past(dve, m["pv"], at, 3)
                    nc.vector.tensor_tensor(pL[k % 3][0:KC, 0:n], PS[0:KC, 3 + k % 2, 0:n],
                                            pH[k % 3][0:KC, 0:n].bitcast(fp32), ALU.subtract)\
                        .then_inc(m["trc"], 1)
                elif not by_scalar(g, k):
                    dve.wait_ge(m["tr"], at + 1)
                    wait_past(dve, m["pv"], at, 3)
                    nc.vector.tensor_copy(pT[k % 3][0:KC, 0:n], PS[0:KC, 3 + k % 2, 0:n]).then_inc(m["trc"], 1)

            def reciprocals(b, g):
                n, size = TROWS[l], GROUPS[l][g]
                c, r = slice(GA * g, GA * g + size), slice(0, n)
                dve.wait_ge(m["exp"], NKB * (tiles * b + GA * g + size))
                chain.link(dve, nc.vector.tensor_reduce(row_sum[r, c], part_sum[r, c, :], AX, ALU.add))
                chain.link(dve, nc.vector.reciprocal(row_inv[r, c], row_sum[r, c]))
                wait_past(dve, m["inv"], 2 * b + g, 2)
                nc.vector.tensor_tensor(
                    inv_diag[g][:, :, :].rearrange("p a c -> p (a c)")[r, 0:size * n]
                    .rearrange("p (a c) -> p a c", a=size),
                    ident[r, r].rearrange("p (a c) -> p a c", a=1).broadcast_to([n, size, n]),
                    row_inv[r, c].rearrange("p (j a) -> p j a", a=1).broadcast_to([n, size, n]),
                    ALU.mult).then_inc(m["idiag"], 1)

            def scale_out(b, g):
                dve.wait_ge(m["invc"], 2 * b + g + 1)
                dve.wait_ge(m["pv"], 2 * NC * b + NC * g + NC)
                n = 128 * GROUPS[l][g] if l == 0 else TROWS[l]
                dst = QO_flat[:, bass.ds(b * HQ + g * GA * 128, n)] if l == 0 else \
                    out_q[:, bass.ds(b * 4 * S + g * n, n)]
                nc.vector.tensor_tensor(dst, PS[:, 5 + g, 0:n], inv_cols[:, 0:n], ALU.mult).then_inc(m["norm"], 1)

            def chunk(b, g, k, first):
                copy_chunk(b, g, k)
                if k == 2 and not first:
                    scale_out(*((b, 0) if g else (b - 1, 1)))
                if k == (9 if l == 0 else NC - 1):
                    reciprocals(b, g)

            def queries(b, par, part):
                dve.wait_ge(m["qh"], b + 1)
                n = HQ // 2
                c = slice(part * n, part * n + n)
                nc.vector.tensor_tensor(qL[par][:, c], QO_flat[:, bass.ds(b * HQ + part * n, n)],
                                        qH[par][:, c].bitcast(fp32), ALU.subtract).then_inc(m["q"], 1)

            def batch(b, par):
                first = isinstance(b, int) and b == 0
                last = isinstance(b, int) and b == B - 1
                for s in range(tiles):
                    maxima(b, s)
                    g, ks = slot_chunks(l, s)
                    for k in ks:
                        if g == 0:
                            chunk(b, 0, k, first)
                        elif not first:
                            chunk(b - 1, 1, k, False)
                    if l == 0 and s in (1, 2) and not last:
                        queries(b + 1, 1 - par, s - 1)
                    if l == 1 and not last and 3 < s < 7:
                        values(b + 1, 1 - par, s - 4)

            if l == 1:
                for piece in range(3):
                    values(0, 0, piece)
            else:
                queries(0, 0, 0)
                queries(0, 0, 1)
            batch(0, 0)
            batch(1, 1)
            batch(2, 0)
            per_batch = 3 * tiles + 4
            start = chain.count
            with dve.Fori(3, B - 2, 2) as i:
                chain.count = (i - 3) * per_batch + start
                batch(i, 1)
                batch(i + 1, 0)
            chain.count = start + per_batch * (B - 4)
            batch(B - 1, 1)
            for k in range(NC):
                chunk(B - 1, 1, k, False)
            scale_out(B - 1, 1)
            dve.wait_ge(m["out"], 1)
            bias = xa_bias[:, 4:5] if l == 0 else xa_bias[:, 3:4]
            nc.vector.scalar_tensor_tensor(halves(X[:, :]), two(0), bias, halves(X[:, :]), ALU.add, ALU.add)\
                .then_inc(x_ready, 1)

        def experts_tensor(pe, l, n):
            m = ff[l]
            ng = E if l == 0 else WCOLS
            pe.wait_ge(xn_ready, 2 * n + 2)
            if l == 0:
                pe.wait_ge(ld_ffn, 16 * FFN_LOADS)
            for b in range(B):
                mm = nc.tensor.matmul(PS[0:S, 6, b * ng:(b + 1) * ng], XN[:, b * S:(b + 1) * S],
                                      gate_w[l][:, 0:ng], start=True, stop=True)
            mm.then_inc(m["logit"], 1)
            def three_passes(dst, a_hl, b_hl, first, last):
                nc.tensor.matmul(dst, a_hl[0], b_hl[0], start=first, stop=False)
                nc.tensor.matmul(dst, a_hl[0], b_hl[1], start=False, stop=False)
                return nc.tensor.matmul(dst, a_hl[1], b_hl[0], start=False, stop=last)

            def hidden_product(e, par, f):
                if f == 0:
                    pe.wait_ge(m["w1sp"], e + 1)
                wait_past(pe, m["hact"], NF * e + f, 2)
                for a in range(2):
                    mm = three_passes(PS[:, 2 * (f % 2) + a, 0:HALF],
                                      [w[:, f * 128:(f + 1) * 128] for w in w1_hl[par]],
                                      [x[:, a * HALF:(a + 1) * HALF] for x in xn_hl], True, True)
                mm.then_inc(m["h"], 1)

            def gates_product(e, par):
                pe.wait_ge(m["wsel"], e + 1)
                wait_past(pe, m["wcols"], e, 1)
                for a in range(2):
                    for h in range(2):
                        mm = nc.tensor.matmul(PS[:, 6 + a, 0:HALF], mask_cols[par],
                                              w_blk_hl[h][:, a * HALF:(a + 1) * HALF], start=h == 0, stop=h == 1)
                mm.then_inc(m["wmm"], 1)

            def output_product(e, par, f):
                if f == 0:
                    pe.wait_ge(m["w2sp"], e + 1)
                    if isinstance(e, int) and e == 0:
                        if l == 1:
                            pe.wait_ge(m["ymul"], 1)
                    else:
                        pe.wait_ge(m["ymul"], e + l)
                pe.wait_ge(m["hlo"], NF * e + f + 1)
                for a in range(2):
                    at = f * NTOK + a * HALF
                    mm = three_passes(PS[:, 4 + a, 0:HALF],
                                      [w[:, f * 128:(f + 1) * 128] for w in w2_hl[par]],
                                      [x[:, at:at + HALF] for x in hid_hl], f == 0, f == NF - 1)
                mm.then_inc(m["y"], 1)

            def step(e, par, final=False):
                gates_product(e, par)
                for f in range(NF):
                    if not final:
                        hidden_product(e + 1, 1 - par, f)
                    output_product(e, par, f)

            pe.wait_ge(m["xsp"], 1)
            for f in range(NF):
                hidden_product(0, 0, f)
            pe.wait_ge(m["gates"], 1)
            nc.tensor.transpose(PS[:, 7, 0:S], routed[:, :, :].rearrange("p b e -> p (b e)"),
                                ident[0:S, 0:S]).then_inc(m["gtr"], 1)
            pe.wait_ge(m["blk"], 1)
            if l == 1:
                for a in range(2):
                    mm = nc.tensor.matmul(PS[:, 4 + a, 0:HALF], b2[:, :],
                                          w_blk[:, a * HB:(a + 1) * HB, :], start=True, stop=True)
                mm.then_inc(m["b2mm"], 1)

            pe.wait_ge(m["bsp"], 1)
            step(0, 0)
            step(1, 1)
            with pe.Fori(2, E - 3, 2) as i:
                step(i, 0)
                step(i + 1, 1)
            step(E - 2, 0)
            step(E - 1, 1, final=True)

        def experts_gpsimd(pool, l):
            m = ff[l]
            pool.wait_ge(x_ready, 2 if l == 0 else 5)

            def halve(hl, x, signal):
                nc.gpsimd.tensor_tensor(hl[0], x, ones[:, 0:1].broadcast_to([128, FF]), ALU.mult)\
                    .then_inc(pool_step, 1)
                pool_count[0] = pool_count[0] + 1
                pool.wait_ge(pool_step, pool_count[0])
                nc.gpsimd.tensor_tensor(hl[1], x, hl[0].bitcast(fp32), ALU.subtract).then_inc(signal, 1)

            def weights(e, par):
                pool.wait_ge(ld_w[l][par], (e // 2 + 1) * 32 if isinstance(e, int) else (e - par) * 16 + 32)
                wait_past(pool, m["h"], NF * e, NF + 1)
                halve(w1_hl[par], w1[par], m["w1sp"])
                wait_past(pool, m["y"], NF * e, NF + 1)
                halve(w2_hl[par], w2[par].rearrange("p g d -> p (g d)"), m["w2sp"])

            weights(0, 0)
            weights(1, 1)
            start = pool_count[0]
            with pool.Fori(2, E - 1, 2) as i:
                pool_count[0] = (i - 2) * 2 + start
                weights(i, 0)
                weights(i + 1, 1)
            pool_count[0] = start + 2 * (E - 2)

        def experts_sync(sp, l):
            m = ff[l]

            def load(e, par):
                wait_past(sp, m["w2sp"], e, 2)
                w1s = t["L0_ffn_w1" if l == 0 else "L1_ffn_W1"]
                w2s = t["L0_ffn_w2" if l == 0 else "L1_ffn_W2"]
                sp.dma_start(w1[par], w1s[bass.ds(e, 1), :, :].rearrange("a c f -> (a c) f"))\
                    .then_inc(ld_w[l][par], 16)
                sp.dma_start(w2[par], w2s[bass.ds(e, 1), :, :].rearrange("a (g p) d -> (a p) g d", p=128))\
                    .then_inc(ld_w[l][par], 16)

            if l == 0:
                sp.wait_ge(xa[0]["kspl"], B)
                sp.wait_ge(xa[0]["vspl"], 3 * B)
            else:
                sp.wait_ge(xa[1]["vmm"], 3 * B)
                sp.wait_ge(x_ready, 5)
            load(0, 0)
            load(1, 1)
            with sp.Fori(2, E - 1, 2) as i:
                load(i, 0)
                load(i + 1, 1)

        def experts_scalar(act, l):
            m = ff[l]
            func = ACT.Gelu if l == 0 else ACT.Gelu_apprx_tanh
            act.wait_ge(m["gsub"], 1)
            ins = nc.scalar.activation(gate[:, :, 0:E], gate[:, :, 0:E], ACT.Exp)
            if l == 1:
                ins = nc.scalar.activation(gate[:, :, E:WCOLS], gate[:, :, E:WCOLS], ACT.Exp, scale=-1.0)
            ins.then_inc(m["gexp"], 1)

            def gelu(e, f):
                act.wait_ge(m["h"], NF * e + f + 1)
                wait_past(act, m["hlo"], NF * e + f, NF)
                bias = b1[:, l, bass.ds(e * NF + f, 1)]
                nc.scalar.activation(halves(hidden[:, f, :]), two(2 * (f % 2)), func, bias=bias)\
                    .then_inc(m["hact"], 1)

            def high(e, f):
                act.wait_ge(m["hact"], NF * e + f + 1)
                wait_past(act, m["y"], NF * e + f, NF)
                nc.scalar.activation(hid_hl[0][:, f * NTOK:(f + 1) * NTOK], hidden[:, f, :], ACT.Copy)\
                    .then_inc(m["hhi"], 1)

            def copy_gates(e, par):
                act.wait_ge(m["wmm"], e + 1)
                wait_past(act, m["ymul"], e + l, 2 + l)
                nc.scalar.activation(halves(w_cols[:, par, :]), two(6), ACT.Copy).then_inc(m["wcols"], 1)

            def step(e, par, final=False):
                if not final:
                    gelu(e + 1, 0)
                high(e, NF - 1)
                copy_gates(e, par)
                if not final:
                    for f in range(1, NF):
                        gelu(e + 1, f)
                        high(e + 1, f - 1)

            gelu(0, 0)
            for f in range(1, NF):
                gelu(0, f)
                high(0, f - 1)
            step(0, 0)
            step(1, 1)
            with act.Fori(2, E - 3, 2) as i:
                step(i, 0)
                step(i + 1, 1)
            step(E - 2, 0)
            step(E - 1, 1, final=True)

        def experts_vector(dve, l, chain):
            m = ff[l]
            ng = E if l == 0 else WCOLS
            G = gate[:, :, 0:E]

            def per_batch(x):
                return x.rearrange("p (b a) -> p b a", a=1).broadcast_to([S, B, E])

            dve.wait_ge(xn_ready, 6 if l == 0 else 12)
            chain.link(dve, nc.vector.tensor_copy(xn_hl[0], XN[:, :]))
            nc.vector.tensor_tensor(xn_hl[1], XN[:, :], xn_hl[0].bitcast(fp32), ALU.subtract).then_inc(m["xsp"], 1)
            st = [gate_stat[:, k, :] for k in range(4)]
            dve.wait_ge(m["logit"], 1)
            logits = PS[0:S, 6, 0:B * ng].rearrange("p (b e) -> p b e", b=B)
            if l == 0:
                chain.link(dve, nc.vector.tensor_copy(G, logits))
            else:
                chain.link(dve, nc.vector.tensor_tensor(
                    gate[:, :, :], logits,
                    gate_b[:, :].rearrange("p (a e) -> p a e", a=1).broadcast_to([S, B, WCOLS]), ALU.add))
            chain.link(dve, nc.vector.tensor_reduce(st[0], G, AX, ALU.max))
            nc.vector.tensor_tensor(G, G, per_batch(st[0]), ALU.subtract).then_inc(m["gsub"], 1)
            dve.wait_ge(m["gexp"], 1)
            chain.link(dve, nc.vector.tensor_reduce(st[1], G, AX, ALU.add))
            chain.link(dve, nc.vector.reciprocal(st[2], st[1]))
            if l == 0:
                nc.vector.tensor_tensor(routed[:, :, :], G, per_batch(st[2]), ALU.mult).then_inc(m["gates"], 1)
            else:
                chain.link(dve, nc.vector.tensor_tensor(gate2[:, :, :], G, per_batch(st[2]), ALU.mult))
                z = gate[:, :, E]
                chain.link(dve, nc.vector.tensor_scalar(st[0], z, 1.0, None, ALU.add))
                chain.link(dve, nc.vector.reciprocal(st[1], st[0]))
                chain.link(dve, nc.vector.tensor_scalar(st[0], st[1], THRESHOLD, None, ALU.mult))
                chain.link(dve, nc.vector.tensor_tensor(gate2[:, :, :], gate2[:, :, :], per_batch(st[0]),
                                                        ALU.subtract))
                chain.link(dve, nc.vector.tensor_scalar(gate2[:, :, :], gate2[:, :, :], 0.0, None, ALU.max))
                chain.link(dve, nc.vector.tensor_reduce(st[1], gate2[:, :, :], AX, ALU.add))
                chain.link(dve, nc.vector.tensor_scalar(st[2], st[1], 0.0, None, ALU.is_equal))
                chain.link(dve, nc.vector.tensor_tensor(st[3], st[1], st[2], ALU.add))
                chain.link(dve, nc.vector.reciprocal(st[0], st[3]))
                nc.vector.tensor_tensor(routed[:, :, :], gate2[:, :, :], per_batch(st[0]), ALU.mult)\
                    .then_inc(m["gates"], 1)
            dve.wait_ge(m["gtr"], 1)
            if l == 0:
                rest = CAP - 8
                chain.link(dve, nc.vector.memset(work[:, :], 2.0))
                chain.link(dve, nc.vector.tensor_copy(gT[:, :], PS[:, 7, 0:S]))
                chain.link(dve, nc.vector.tensor_copy(work[:, 0:S], gT[:, :]))
                chain.link(dve, nc.vector.max(top8[:, 0, :], work[:, 0:S]))
                chain.link(dve, nc.vector.match_replace(work2[:, 0:S], top8[:, 0, :], work[:, 0:S], -1.0))
                chain.link(dve, nc.vector.tensor_copy(work2[:, S:64], work[:, S:64]))
                chain.link(dve, nc.vector.max(top8[:, 1, :], work2[:, 0:S]))
                chain.link(dve, nc.vector.memset(top8[:, 1, rest:8], 2.0))
                chain.link(dve, nc.vector.match_replace(work[:, :], top8[:, 1, :], work2[:, :], -1.0))
                chain.link(dve, nc.vector.tensor_scalar(work[:, 0:S], work[:, 0:S], -1.0, None, ALU.is_equal))
                chain.link(dve, nc.vector.tensor_tensor(w_be[:, :], gT[:, :], work[:, 0:S], ALU.mult))
            else:
                chain.link(dve, nc.vector.tensor_copy(w_be[:, :], PS[:, 7, 0:S]))
            ins = nc.vector.tensor_tensor(
                w_blk[:, :, :], w_be[:, :].rearrange("p (a s) -> p a s", a=1).broadcast_to([128, B, S]),
                batch_mask[:, :].rearrange("p (b a) -> p b a", a=1).broadcast_to([128, B, S]), ALU.mult)
            ins.then_inc(m["blk"], 1)
            dve.wait_ge(m["blk"], 1)

            flat = w_blk[:, :, :].rearrange("p b s -> p (b s)")
            chain.link(dve, nc.vector.tensor_copy(w_blk_hl[0], flat))
            nc.vector.tensor_tensor(w_blk_hl[1], flat, w_blk_hl[0].bitcast(fp32), ALU.subtract)\
                .then_inc(m["bsp"], 1)

            def select(e, par):
                wait_past(dve, m["wmm"], e, 2)
                nc.vector.tensor_copy(mask_cols[par], expert_mask[:, bass.ds(e, 1)].broadcast_to([128, 128]))\
                    .then_inc(m["wsel"], 1)

            def low(e, f):
                dve.wait_ge(m["hhi"], NF * e + f + 1)
                at = slice(f * NTOK, (f + 1) * NTOK)
                nc.vector.tensor_tensor(hid_hl[1][:, at], hidden[:, f, :], hid_hl[0][:, at].bitcast(fp32),
                                        ALU.subtract).then_inc(m["hlo"], 1)

            if l == 1:
                dve.wait_ge(m["b2mm"], 1)
                nc.vector.tensor_tensor(halves(X[:, :]), halves(X[:, :]), two(4), ALU.add).then_inc(m["ymul"], 1)
            select(0, 0)
            start = chain.count

            def step(e, par, final=False):
                low(e, NF - 1)
                if not final:
                    select(e + 1, 1 - par)
                    for f in range(NF - 2):
                        low(e + 1, f)
                dve.wait_ge(m["y"], NF * e + NF)
                dve.wait_ge(m["wcols"], e + 1)
                ins = nc.vector.tensor_tensor(halves(XC[:, :]), two(4), halves(w_cols[:, par, :]), ALU.mult)
                ins.then_inc(m["ymul"], 1)
                if not final:
                    low(e + 1, NF - 2)
                dve.wait_ge(m["ymul"], e + 1 + l)
                ins = nc.vector.tensor_tensor(X[:, :], X[:, :], XC[:, :], ALU.add)
                if final:
                    ins.then_inc(x_ready, 1)
                else:
                    chain.link(dve, ins)

            for f in range(NF - 1):
                low(0, f)
            step(0, 0)
            with dve.Fori(1, E - 2, 2) as i:
                chain.count = i + start
                step(i, 1)
                step(i + 1, 0)
            chain.count = start + E - 1
            step(E - 1, 1, final=True)

        block = ctx.enter_context(nc.Block())

        @block.sync
        def _(sp):
            sp.dma_start(X[:, :], t["x_T"]).then_inc(ld_x, 16)
            for w, name in enumerate(("sa0_q", "sa0_k", "sa0_v", "sa0_o")):
                sp.dma_start(sa_w[0][:, w, :], t[name]).then_inc(ld_sa, 16)
            for w, name in enumerate(("sa1_q", "sa1_k", "sa1_v", "sa1_o")):
                sp.dma_start(sa_w[1][:, w, :], t[name]).then_inc(ld_sa, 16)
            for w, name in enumerate(("L1_attn_wq_b", "L1_attn_wk_b")):
                sp.dma_start(sa_bias[:, w:w + 1], t[name]).then_inc(ld_sa, 16)
            sp.dma_start(sa_bias[:, 3:4], t["L1_attn_wo_b"]).then_inc(ld_sa, 16)
            sp.dma_start(sa_bv[:, :], t["sa_bv"].broadcast_to([128, D])).then_inc(ld_sa, 16)
            for w, name in enumerate(("xa0_qT", "xa0_kT", "xa0_vT", "L0_xattn_W_out")):
                sp.dma_start(fold_in[w], t[name].rearrange("(g p) c -> p g c", p=128))\
                    .then_inc(ld_fold, 16)
            sp.wait_ge(consts_set, 2)
            sp.dma_start(prob0[0:S, 0:S2], t["fside_SxS2_0"]).then_inc(ld_bias, 16)
            sp.dma_start(prob0[64:64 + S, 0:S2], t["fside_SxS2_0"]).then_inc(ld_bias, 16)
            sp.dma_start(prob0[:, S2:S2 + HQ], t["bias_sel"]).then_inc(ld_bias, 16)
            sp.dma_start(gate_w[0][:, 0:E], t["L0_ffn_gate_w"]).then_inc(ld_ffn, 16)
            sp.dma_start(gate_w[1][:, 0:E], t["L1_ffn_Wg"]).then_inc(ld_ffn, 16)
            sp.dma_start(gate_w[1][:, E:WCOLS], t["L1_ffn_Wt"]).then_inc(ld_ffn, 16)
            sp.dma_start(gate_b[:, 0:E], t["L1_ffn_bg"].broadcast_to([S, E])).then_inc(ld_ffn, 16)
            sp.dma_start(gate_b[:, E:WCOLS], t["L1_ffn_bt"].broadcast_to([S, 1])).then_inc(ld_ffn, 16)
            sp.dma_start(b1[:, 1, :], t["b1_cols"]).then_inc(ld_ffn, 16)
            for b in range(B):
                sp.dma_start(b2[b * E:(b + 1) * E, :], t["L1_ffn_b2"]).then_inc(ld_ffn, 16)
            for w, name in enumerate(("xa1_q", "xa1_k", "xa1_v", "xa1_o")):
                sp.dma_start(xa_w[:, w, :], t[name]).then_inc(ld_xa, 16)
            sp.dma_start(xa_bq[:, :], t["xa_bq"]).then_inc(ld_xa, 16)
            for w, name in ((1, "L1_xattn_b_k"), (3, "L1_xattn_b_o"),
                            (4, "L0_xattn_b_out")):
                sp.dma_start(xa_bias[:, w:w + 1], t[name]).then_inc(ld_xa, 16)
            sp.dma_start(xa_bv[:, :], t["xa_bv"].broadcast_to([128, D])).then_inc(ld_xa, 16)
            cross_sync(sp, 0)
            experts_sync(sp, 0)
            cross_sync(sp, 1)
            experts_sync(sp, 1)
            sp.wait_ge(x_ready, 6)
            sp.dma_start(out, X[:, :]).then_inc(out_done, 16)
            sp.wait_ge(out_done, 16)

        @block.gpsimd
        def _(pool):
            pool.wait_ge(ld_const, 16 * CONST_LOADS)
            self_gpsimd(pool, 0)
            cross_gpsimd(pool, 0)
            experts_gpsimd(pool, 0)
            self_gpsimd(pool, 1)
            cross_gpsimd(pool, 1)
            experts_gpsimd(pool, 1)

        @block.scalar
        def _(act):
            act.dma_start(ident[:, :], t["ident"]).then_inc(ld_const, 16)
            act.dma_start(head_mask[:, :], t["head_mask"]).then_inc(ld_const, 16)
            act.dma_start(rope[:, :, :], t["rope"]).then_inc(ld_const, 16)
            act.dma_start(quad_mask[:, :], t["quad_mask"]).then_inc(ld_const, 16)
            act.dma_start(batch_mask[:, :], t["batch_mask"]).then_inc(ld_const, 16)
            act.dma_start(expert_mask[:, :], t["expert_mask"]).then_inc(ld_const, 16)
            act.wait_ge(consts_set, 1)
            norm_scalar(act, 0)
            self_scalar(act, 0)
            norm_scalar(act, 1)
            fold_scalar(act)
            cross_scalar(act, 0)
            norm_scalar(act, 2)
            act.wait_ge(ld_ffn, 16 * FFN_LOADS)
            experts_scalar(act, 0)
            norm_scalar(act, 3)
            self_scalar(act, 1)
            norm_scalar(act, 4)
            act.wait_ge(ld_xa, 16 * XA_LOADS)
            cross_scalar(act, 1)
            norm_scalar(act, 5)
            experts_scalar(act, 1)

        @block.tensor
        def _(pe):
            pe.wait_ge(ld_const, 16 * CONST_LOADS)
            norm_tensor(pe, 0)
            self_tensor(pe, 0, 0)
            norm_tensor(pe, 1)
            fold_tensor(pe)
            cross_tensor(pe, 0, 1)
            norm_tensor(pe, 2)
            experts_tensor(pe, 0, 2)
            norm_tensor(pe, 3)
            self_tensor(pe, 1, 3)
            norm_tensor(pe, 4)
            cross_tensor(pe, 1, 4)
            norm_tensor(pe, 5)
            experts_tensor(pe, 1, 5)

        @block.vector
        def _(dve):
            chain = Chain()
            nc.vector.memset(b1[:, 0, :], 0.0)
            nc.vector.memset(ones[:, :], 1.0)
            nc.vector.memset(mean_w[:, :], 1.0 / D)
            nc.vector.memset(eps[:, :], EPS).then_inc(consts_set, 1)
            nc.vector.memset(prob[0][:, 0, :], 0.0).then_inc(consts_set, 1)
            dve.wait_ge(ld_x, 16)
            norm_vector(dve, 0, chain)
            dve.wait_ge(ld_sa, 16 * SA_LOADS)
            self_vector(dve, 0, chain)
            bias_vector(dve, chain)
            norm_vector(dve, 1, chain)
            dve.wait_ge(ld_xa, 16 * XA_LOADS)
            cross_vector(dve, 0, chain)
            norm_vector(dve, 2, chain)
            dve.wait_ge(ld_ffn, 16 * FFN_LOADS)
            experts_vector(dve, 0, chain)
            norm_vector(dve, 3, chain)
            self_vector(dve, 1, chain)
            norm_vector(dve, 4, chain)
            cross_vector(dve, 1, chain)
            norm_vector(dve, 5, chain)
            experts_vector(dve, 1, chain)


def kernel(**inputs):
    import concourse.bacc as bacc
    from concourse.bass_utils import run_bass_kernel_spmd

    x = {k: np.asarray(v) for k, v in inputs.items()}
    ch = np.arange(D)
    circ = (ch[None, :] - ch[:, None]) % D
    even = ch - ch % 2
    arrays = {
        "x_T": x["x"].transpose(2, 0, 1).reshape(D, NTOK),
        "ctx_1024": x["ctx_1024"],
        "ctx_T": x["ctx_1024"].transpose(0, 2, 1),
        "fside_SxS2_0": x["fside_SxS2_0"],
        "sa0_q": x["L0_attn_Wq"].T[:, even], "sa0_k": x["L0_attn_Wk"].T[:, even],
        "sa0_v": x["L0_attn_Wv"].T, "sa0_o": x["L0_attn_Wo"].T,
        "sa1_q": x["L1_attn_wq_c"][circ], "sa1_k": x["L1_attn_wk_c"][circ],
        "sa1_v": x["L1_attn_wv_c"][circ], "sa1_o": x["L1_attn_wo_c"][circ],
        "xa0_qT": x["L0_xattn_W_q"].T, "xa0_kT": x["L0_xattn_W_k"].T, "xa0_vT": x["L0_xattn_W_v"].T,
        "xa1_q": x["L1_xattn_W_q"].T, "xa1_k": x["L1_xattn_W_k"].T,
        "xa1_v": x["L1_xattn_W_v"].T, "xa1_o": x["L1_xattn_W_o"].T,
        "sa_bv": x["L1_attn_wv_b"][None, :], "xa_bv": x["L1_xattn_b_v"][None, :],
        "L1_ffn_bg": x["L1_ffn_bg"][None, :], "L1_ffn_bt": x["L1_ffn_bt"][None, :],
        "b1_cols": x["L1_ffn_b1"].reshape(E * NF, 128).T,
    }
    for name in ("L0_xattn_W_out", "L0_ffn_gate_w", "L0_ffn_w1", "L0_ffn_w2", "L1_ffn_Wg", "L1_ffn_Wt",
                 "L1_ffn_W1", "L1_ffn_W2", "L1_ffn_b2"):
        arrays[name] = x[name]
    for name in ("L1_attn_wq_b", "L1_attn_wk_b", "L1_attn_wo_b", "L1_xattn_b_k",
                 "L1_xattn_b_o", "L0_xattn_b_out"):
        arrays[name] = x[name][:, None]

    quad_ch = np.arange(3 * QUAD)[:, None] % QUAD + QUAD * np.arange(4)[None, :]
    arrays["xa_bq"] = x["L1_xattn_b_q"][quad_ch]

    pos = np.arange(S, dtype=np.float32)
    freqs = np.exp(np.arange(0, HD, 2, dtype=np.float32) * np.float32(-math.log(10000.0) / HD))
    angle = (pos[None, :] * freqs[(ch % HD) // 2][:, None]).astype(np.float32)
    table = np.where((ch % 2 == 0)[:, None], np.cos(angle), -np.sin(angle)).astype(np.float32)
    arrays["rope"] = np.stack([table * np.float32(HD ** -0.5), table], 1)
    arrays["ident"] = np.eye(128, dtype=np.float32)
    arrays["head_mask"] = (ch[:, None] // HD == np.arange(NH)[None, :]).astype(np.float32)
    arrays["batch_mask"] = (ch[:, None] // E == np.arange(B)[None, :]).astype(np.float32)
    arrays["expert_mask"] = (ch[:, None] % E == np.arange(E)[None, :]).astype(np.float32)
    row, col = np.arange(128)[:, None] % 64, np.arange(HQ)[None, :]
    arrays["bias_sel"] = np.where(row == col % S, 2.0 ** -(col // S + 1.0), 0.0).astype(np.float32)
    arrays["quad_mask"] = (ch[:, None] // HD % 4 == np.arange(4)[None, :]).astype(np.float32)
    arrays = {f"in_{k}": np.ascontiguousarray(v) for k, v in arrays.items()}

    nc = bacc.Bacc("TRN2", target_bir_lowering=False, num_devices=1)
    t = {k[3:]: nc.dram_tensor(k, a.shape, mybir.dt.from_np(a.dtype), kind="ExternalInput").ap()
         for k, a in arrays.items()}
    out = nc.dram_tensor("out_0", (D, NTOK), mybir.dt.float32, kind="ExternalOutput").ap()
    decoder_kernel(nc, t, out)
    r = run_bass_kernel_spmd(nc, [arrays], core_ids=[0])
    y = r.results[0]["out_0"]
    return y.reshape(D, B, S).transpose(1, 2, 0)
```
